# Optimizing a Trainium2 kernel written in Bass

```python
import numpy as np
import jax
import jax.numpy as jnp

def _softmax(x, axis=-1):
    return jax.nn.softmax(x, axis=axis)

def _gelu(x):
    return jax.nn.gelu(x, approximate=True)

def _silu(x):
    return jax.nn.silu(x)

def _sigmoid(x):
    return jax.nn.sigmoid(x)

def _layernorm(x, axis=-1, eps=1e-05):
    m = jnp.mean(x, axis=axis, keepdims=True)
    v = jnp.var(x, axis=axis, keepdims=True)
    return (x - m) / jnp.sqrt(v + eps)

def _scatter_add(tgt, idx, src, axis=0):
    return tgt.at[idx].add(src)

def _segment_sum(src, seg, n):
    return jax.ops.segment_sum(src, seg, n)
kernel_name = 'mk_adaln_d2_jaxref_r4_d32104'

def setup_inputs(seed: int=0):
    np.random.seed(seed)
    _w = jnp.asarray

    def _L0_attn_setup():
        import math
        import jax, jax.numpy as jnp
        import numpy as np
        E = 256
        H = 16
        D = E // H

        def _l2norm(t, eps=1e-12):
            n = jnp.sqrt(jnp.sum(t * t, axis=-1, keepdims=True))
            return t / jnp.maximum(n, eps)
        key = jax.random.key(seed)
        ks = jax.random.split(key, 10)
        s = 0.02
        x = jax.random.normal(ks[0], (2, 1024, E), dtype=jnp.float32)
        Wq = jax.random.normal(ks[1], (E, E), dtype=jnp.float32) * s
        Wk = jax.random.normal(ks[2], (E, E), dtype=jnp.float32) * s
        Wv = jax.random.normal(ks[3], (E, E), dtype=jnp.float32) * s
        Walpha = jax.random.normal(ks[4], (E, H), dtype=jnp.float32) * s
        Wbeta = jax.random.normal(ks[5], (E, H), dtype=jnp.float32) * s
        A_log = jnp.linspace(0.0, math.log(16.0), H).astype(jnp.float32)
        dt_bias = jnp.zeros((H,), dtype=jnp.float32)
        Wgate = jax.random.normal(ks[6], (E, E), dtype=jnp.float32) * s
        Wout = jax.random.normal(ks[7], (E, E), dtype=jnp.float32) * s
        rms_w = jnp.ones((D,), dtype=jnp.float32)
        return {'x': x, 'Wq': Wq, 'Wk': Wk, 'Wv': Wv, 'Walpha': Walpha, 'Wbeta': Wbeta, 'A_log': A_log, 'dt_bias': dt_bias, 'Wgate': Wgate, 'Wout': Wout, 'rms_w': rms_w}
    _L0_attn_in = _L0_attn_setup()

    def _L0_ffn_setup():
        import jax, jax.numpy as jnp
        import numpy as np
        B, S, D, E, H, K = (64, 512, 256, 32, 1024, 8)
        key = jax.random.key(seed)
        k0, k1, k2, k3 = jax.random.split(key, 4)
        x = jax.random.normal(k0, (B, S, D), jnp.float32)
        gate_w = jax.random.normal(k1, (E, D), jnp.float32) * (1.0 / np.sqrt(D))
        gate_b = jnp.zeros((E,), jnp.float32)
        w1 = jax.random.normal(k2, (E, D + 1, H), jnp.float32) * (1.0 / np.sqrt(D + 1))
        w2 = jax.random.normal(k3, (E, H + 1, D), jnp.float32) * (1.0 / np.sqrt(H + 1))
        return {'x': x, 'gate_w': gate_w, 'gate_b': gate_b, 'w1': w1, 'w2': w2}
    _L0_ffn_in = _L0_ffn_setup()
    _L0_c = _w((lambda *s: np.random.randn(*s).astype(np.float32) * 0.05)(2, 256))
    _L0_wmod = _w((lambda *s: np.random.randn(*s).astype(np.float32) * 0.05)(256, 6 * 256) * 256 ** (-0.5))

    def _L1_attn_setup():
        import jax, jax.numpy as jnp
        import numpy as np
        B, S, D = (2, 1024, 256)
        LOOKBACK = 64
        TOPK = 16
        CHUNK = 32
        NEG = -1e+30

        def _phrase_states(h):
            b, seq, d = h.shape
            hc = h.reshape(b, seq // CHUNK, CHUNK, d)
            pref = jnp.cumsum(hc, axis=2)
            denom = jnp.arange(1, CHUNK + 1, dtype=h.dtype).reshape(1, 1, CHUNK, 1)
            return (pref / denom).reshape(b, seq, d)

        def _shift1(x):
            return jnp.pad(x, ((0, 0), (1, 0), (0, 0)))[:, :-1]
        key = jax.random.key(seed)
        ks = jax.random.split(key, 11)
        s = 0.02
        inp = {'h': jax.random.normal(ks[0], (B, S, D), jnp.float32)}
        names = ['q_w', 'k_w', 'v_w', 'pk_w', 'pv_w']
        for i, n in enumerate(names):
            inp[n] = jax.random.normal(ks[1 + i], (D, D), jnp.float32) * s
            inp[n.replace('_w', '_b')] = jax.random.normal(ks[6 + i], (D,), jnp.float32) * s
        return inp
    _L1_attn_in = _L1_attn_setup()

    def _L1_ffn_setup():
        import jax, jax.numpy as jnp
        import numpy as np
        B, S, D = (2, 512, 256)
        DFF = 512
        E_FFN = 8
        E_ZERO = 4
        E_TOT = E_FFN + E_ZERO
        TOP_K = 2
        key = jax.random.key(seed)
        k1, k2, k3, k4 = jax.random.split(key, 4)
        x = jax.random.normal(k1, (B, S, D), dtype=jnp.float32)
        gate_w = jax.random.normal(k2, (E_TOT, D), dtype=jnp.float32) * (1.0 / np.sqrt(D))
        expert_bias = jnp.zeros((E_TOT,), dtype=jnp.float32)
        w1 = jax.random.normal(k3, (E_FFN, DFF, D), dtype=jnp.float32) * (1.0 / np.sqrt(D))
        w2 = jax.random.normal(k4, (E_FFN, D, DFF), dtype=jnp.float32) * (1.0 / np.sqrt(DFF))
        return {'x': x, 'gate_w': gate_w, 'expert_bias': expert_bias, 'w1': w1, 'w2': w2}
    _L1_ffn_in = _L1_ffn_setup()
    _L1_c = _w((lambda *s: np.random.randn(*s).astype(np.float32) * 0.05)(2, 256))
    _L1_wmod = _w((lambda *s: np.random.randn(*s).astype(np.float32) * 0.05)(256, 6 * 256) * 256 ** (-0.5))
    _d = {'L0_attn_x': _L0_attn_in['x'], 'L0_attn_Wq': _L0_attn_in['Wq'], 'L0_attn_Wk': _L0_attn_in['Wk'], 'L0_attn_Wv': _L0_attn_in['Wv'], 'L0_attn_Walpha': _L0_attn_in['Walpha'], 'L0_attn_Wbeta': _L0_attn_in['Wbeta'], 'L0_attn_A_log': _L0_attn_in['A_log'], 'L0_attn_dt_bias': _L0_attn_in['dt_bias'], 'L0_attn_Wgate': _L0_attn_in['Wgate'], 'L0_attn_Wout': _L0_attn_in['Wout'], 'L0_attn_rms_w': _L0_attn_in['rms_w'], 'L0_ffn_gate_w': _L0_ffn_in['gate_w'], 'L0_ffn_gate_b': _L0_ffn_in['gate_b'], 'L0_ffn_w1': _L0_ffn_in['w1'], 'L0_ffn_w2': _L0_ffn_in['w2'], 'L0_c': _L0_c, 'L0_wmod': _L0_wmod, 'L1_attn_q_w': _L1_attn_in['q_w'], 'L1_attn_q_b': _L1_attn_in['q_b'], 'L1_attn_k_w': _L1_attn_in['k_w'], 'L1_attn_k_b': _L1_attn_in['k_b'], 'L1_attn_v_w': _L1_attn_in['v_w'], 'L1_attn_v_b': _L1_attn_in['v_b'], 'L1_attn_pk_w': _L1_attn_in['pk_w'], 'L1_attn_pk_b': _L1_attn_in['pk_b'], 'L1_attn_pv_w': _L1_attn_in['pv_w'], 'L1_attn_pv_b': _L1_attn_in['pv_b'], 'L1_ffn_gate_w': _L1_ffn_in['gate_w'], 'L1_ffn_expert_bias': _L1_ffn_in['expert_bias'], 'L1_ffn_w1': _L1_ffn_in['w1'], 'L1_ffn_w2': _L1_ffn_in['w2'], 'L1_c': _L1_c, 'L1_wmod': _L1_wmod}
    _x0 = _d['L0_attn_x']
    _d['L0_attn_x'] = jax.random.normal(jax.random.fold_in(jax.random.key(seed), 1), (2, 4096, 256), dtype=_x0.dtype)
    del _x0
    return _d

def reference(L0_attn_x, L0_attn_Wq, L0_attn_Wk, L0_attn_Wv, L0_attn_Walpha, L0_attn_Wbeta, L0_attn_A_log, L0_attn_dt_bias, L0_attn_Wgate, L0_attn_Wout, L0_attn_rms_w, L0_ffn_gate_w, L0_ffn_gate_b, L0_ffn_w1, L0_ffn_w2, L0_c, L0_wmod, L1_attn_q_w, L1_attn_q_b, L1_attn_k_w, L1_attn_k_b, L1_attn_v_w, L1_attn_v_b, L1_attn_pk_w, L1_attn_pk_b, L1_attn_pv_w, L1_attn_pv_b, L1_ffn_gate_w, L1_ffn_expert_bias, L1_ffn_w1, L1_ffn_w2, L1_c, L1_wmod):

    def _L0_attn_ref(x, Wq, Wk, Wv, Walpha, Wbeta, A_log, dt_bias, Wgate, Wout, rms_w):
        import math
        import jax, jax.numpy as jnp
        import numpy as np
        E = 256
        H = 16
        D = E // H

        def _l2norm(t, eps=1e-12):
            n = jnp.sqrt(jnp.sum(t * t, axis=-1, keepdims=True))
            return t / jnp.maximum(n, eps)
        b, s, _ = x.shape
        q = (x @ Wq).reshape(b, s, H, D)
        k = (x @ Wk).reshape(b, s, H, D)
        v = (x @ Wv).reshape(b, s, H, D)
        q = _l2norm(q) / math.sqrt(D)
        k = _l2norm(k)
        dt = jax.nn.softplus(x @ Walpha + dt_bias)
        alpha = jnp.exp(-jnp.exp(A_log) * dt)
        beta = jax.nn.sigmoid(x @ Wbeta)
        qT = jnp.moveaxis(q, 1, 0)
        kT = jnp.moveaxis(k, 1, 0)
        vT = jnp.moveaxis(v, 1, 0)
        aT = jnp.moveaxis(alpha, 1, 0)
        bT = jnp.moveaxis(beta, 1, 0)
        state0 = jnp.zeros((b, H, D, D), dtype=x.dtype)

        def step(state, inp):
            q_t, k_t, v_t, a_t, b_t = inp
            state = a_t[..., None, None] * state
            stored = jnp.einsum('bhij,bhj->bhi', state, k_t)
            delta = b_t[..., None] * (v_t - stored)
            state = state + jnp.einsum('bhi,bhj->bhij', delta, k_t)
            o_t = jnp.einsum('bhij,bhj->bhi', state, q_t)
            return (state, o_t)
        qs = jnp.swapaxes(qT, 1, 2).swapaxes(1, 1)
        _, outs = jax.lax.scan(step, state0, (qT, kT, vT, aT, bT))
        out = jnp.moveaxis(outs, 0, 1)
        var = jnp.mean(out * out, axis=-1, keepdims=True)
        out = out * jax.lax.rsqrt(var + 1e-06) * rms_w
        out = out.reshape(b, s, E)
        gate = jax.nn.silu(x @ Wgate)
        return out * gate @ Wout

    def _L0_ffn_ref(x, gate_w, gate_b, w1, w2):
        import jax, jax.numpy as jnp
        import numpy as np
        B, S, D, E, H, K = (64, 512, 256, 32, 1024, 8)
        b, s, d = x.shape
        logits = jnp.einsum('bsd,ed->bse', x, gate_w) + gate_b
        probs = jax.nn.softmax(logits, axis=-2)
        vals_t, idx_t = jax.lax.top_k(probs.transpose(0, 2, 1), K)
        vals = vals_t.transpose(0, 2, 1)
        idx = idx_t.transpose(0, 2, 1)
        flat_idx = idx.reshape(b, K * E)
        tok = jnp.take_along_axis(x, flat_idx[:, :, None], axis=1)
        tok = tok.reshape(b, K, E, d)
        merged = jnp.einsum('bked,bke->bed', tok, vals)
        ones = jnp.ones(merged.shape[:-1] + (1,), merged.dtype)
        h = jnp.einsum('bei,eih->beh', jnp.concatenate([merged, ones], -1), w1)
        h = jax.nn.gelu(h, approximate=False)
        o = jnp.einsum('bej,ejo->beo', jnp.concatenate([h, ones], -1), w2)
        out_tok = jnp.einsum('beo,bke->bkeo', o, vals).reshape(b, K * E, d)
        out = jnp.zeros_like(x).at[jnp.arange(b)[:, None], flat_idx].add(out_tok)
        return out

    def _L1_attn_ref(h, q_w, q_b, k_w, k_b, v_w, v_b, pk_w, pk_b, pv_w, pv_b):
        import jax, jax.numpy as jnp
        import numpy as np
        B, S, D = (2, 1024, 256)
        LOOKBACK = 64
        TOPK = 16
        CHUNK = 32
        NEG = -1e+30

        def _phrase_states(h):
            b, seq, d = h.shape
            hc = h.reshape(b, seq // CHUNK, CHUNK, d)
            pref = jnp.cumsum(hc, axis=2)
            denom = jnp.arange(1, CHUNK + 1, dtype=h.dtype).reshape(1, 1, CHUNK, 1)
            return (pref / denom).reshape(b, seq, d)

        def _shift1(x):
            return jnp.pad(x, ((0, 0), (1, 0), (0, 0)))[:, :-1]
        b, seq, d = h.shape
        scale = 1.0 / np.sqrt(d)
        q = h @ q_w.T + q_b
        k = h @ k_w.T + k_b
        v = h @ v_w.T + v_b
        ph = _phrase_states(h)
        pk = ph @ pk_w.T + pk_b
        pv = ph @ pv_w.T + pv_b
        k_prev, v_prev = (_shift1(k), _shift1(v))
        pk_prev, pv_prev = (_shift1(pk), _shift1(pv))
        seq_score = jnp.einsum('bsd,bsd->bs', q, k_prev) * scale
        phr_score = jnp.einsum('bsd,bsd->bs', q, pk_prev) * scale
        k_pad = jnp.pad(k, ((0, 0), (LOOKBACK, 0), (0, 0)))
        t_idx = jnp.arange(seq)

        def step(_, l):
            kl = jax.lax.dynamic_slice_in_dim(k_pad, l, seq, axis=1)
            sc = jnp.einsum('bsd,bsd->bs', q, kl) * scale
            valid = t_idx + l >= LOOKBACK
            return (None, jnp.where(valid[None, :], sc, NEG))
        _, scores = jax.lax.scan(step, None, jnp.arange(LOOKBACK))
        scores = jnp.moveaxis(scores, 0, -1)
        top_sc, top_l = jax.lax.top_k(scores, TOPK)
        gidx = jnp.clip(t_idx[None, :, None] - LOOKBACK + top_l, 0, seq - 1)
        sem_v = jax.vmap(lambda vb, ib: vb[ib])(v, gidx)
        all_sc = jnp.concatenate([seq_score[..., None], top_sc, phr_score[..., None]], axis=-1)
        all_v = jnp.concatenate([v_prev[:, :, None, :], sem_v, pv_prev[:, :, None, :]], axis=2)
        w = jax.nn.softmax(all_sc, axis=-1)
        out = jnp.einsum('bsn,bsnd->bsd', w, all_v)
        return jnp.where(t_idx[None, :, None] > 0, out, jnp.zeros((), out.dtype))

    def _L1_ffn_ref(x, gate_w, expert_bias, w1, w2):
        import jax, jax.numpy as jnp
        import numpy as np
        B, S, D = (2, 512, 256)
        DFF = 512
        E_FFN = 8
        E_ZERO = 4
        E_TOT = E_FFN + E_ZERO
        TOP_K = 2
        logits = jnp.einsum('btd,ed->bte', x, gate_w) + expert_bias
        topk_logits, topk_idx = jax.lax.top_k(logits, TOP_K)
        topk_w = jax.nn.softmax(topk_logits, axis=-1)
        onehot = jax.nn.one_hot(topk_idx, E_TOT, dtype=x.dtype)
        w = jnp.einsum('btk,btke->bte', topk_w, onehot)
        w_ffn = w[..., :E_FFN]
        w_zero = jnp.sum(w[..., E_FFN:], axis=-1)
        h = jax.nn.silu(jnp.einsum('btd,efd->btef', x, w1))
        y = jnp.einsum('btef,edf->bted', h, w2)
        out = jnp.einsum('bte,bted->btd', w_ffn, y) + w_zero[..., None] * x
        return out
    x = L0_attn_x
    mod = (_silu(L0_c) @ L0_wmod).reshape(L0_c.shape[0], 6, 1, -1)
    sa, ca, ga, sb, cb, gb = (mod[:, 0], mod[:, 1], mod[:, 2], mod[:, 3], mod[:, 4], mod[:, 5])
    ga = (2 * (ga >= 0) - 1) * jnp.maximum(jnp.abs(ga), 0.25)
    gb = (2 * (gb >= 0) - 1) * jnp.maximum(jnp.abs(gb), 0.25)
    h = _layernorm(x, axis=-1) * (1 + ca) + sa
    x = x + ga * _L0_attn_ref(h, L0_attn_Wq, L0_attn_Wk, L0_attn_Wv, L0_attn_Walpha, L0_attn_Wbeta, L0_attn_A_log, L0_attn_dt_bias, L0_attn_Wgate, L0_attn_Wout, L0_attn_rms_w)
    h = _layernorm(x, axis=-1) * (1 + cb) + sb
    x = x + gb * _L0_ffn_ref(h, L0_ffn_gate_w, L0_ffn_gate_b, L0_ffn_w1, L0_ffn_w2)
    mod = (_silu(L1_c) @ L1_wmod).reshape(L1_c.shape[0], 6, 1, -1)
    sa, ca, ga, sb, cb, gb = (mod[:, 0], mod[:, 1], mod[:, 2], mod[:, 3], mod[:, 4], mod[:, 5])
    ga = (2 * (ga >= 0) - 1) * jnp.maximum(jnp.abs(ga), 0.25)
    gb = (2 * (gb >= 0) - 1) * jnp.maximum(jnp.abs(gb), 0.25)
    h = _layernorm(x, axis=-1) * (1 + ca) + sa
    x = x + ga * _L1_attn_ref(h, L1_attn_q_w, L1_attn_q_b, L1_attn_k_w, L1_attn_k_b, L1_attn_v_w, L1_attn_v_b, L1_attn_pk_w, L1_attn_pk_b, L1_attn_pv_w, L1_attn_pv_b)
    h = _layernorm(x, axis=-1) * (1 + cb) + sb
    x = x + gb * _L1_ffn_ref(h, L1_ffn_gate_w, L1_ffn_expert_bias, L1_ffn_w1, L1_ffn_w2)
    return x

_drawn_inputs = setup_inputs


def setup_inputs(seed=0):
    import zlib

    import numpy as np

    out = dict(_drawn_inputs(seed))
    spreads = {'L0_attn_dt_bias': (0.0, 2.0),
     'L0_attn_rms_w': (1.0, 0.6),
     'L0_ffn_gate_b': (0.0, 2.0),
     'L1_ffn_expert_bias': (0.0, 0.1)}
    factors = {'L0_attn_Wq': 3.264,
     'L0_attn_Wk': 3.261,
     'L0_attn_Wv': 3.229,
     'L0_attn_Walpha': 8.0,
     'L0_attn_Wbeta': 8.0,
     'L0_attn_A_log': 7.64,
     'L0_attn_Wgate': 3.28,
     'L0_attn_Wout': 3.217,
     'L0_ffn_gate_w': 7.767,
     'L0_ffn_w1': 6.168,
     'L0_ffn_w2': 5.5,
     'L0_c': 2.708,
     'L0_wmod': 2.803,
     'L1_attn_q_w': 2.742,
     'L1_attn_q_b': 47.215,
     'L1_attn_k_w': 2.76,
     'L1_attn_k_b': 64.0,
     'L1_attn_v_b': 6.784,
     'L1_attn_pk_w': 8.0,
     'L1_attn_pk_b': 64.0,
     'L1_attn_pv_w': 8.0,
     'L1_attn_pv_b': 64.0}
    for name, (base, spread) in spreads.items():
        noise = np.random.default_rng([zlib.crc32(name.encode()), seed]).standard_normal(out[name].shape)
        drawn = base * np.exp(spread * noise) if base else spread * noise
        out[name] = jnp.asarray(drawn.astype(out[name].dtype))
    for name, factor in factors.items():
        out[name] = (out[name] * factor).astype(out[name].dtype)
    return out
```

```python
import concourse.bass as bass
from concourse import mybir
from concourse.alu_op_type import AluOpType as ALU
from contextlib import ExitStack

F32 = mybir.dt.float32
ACT = mybir.ActivationFunctionType
AX = mybir.AxisListType
AP = bass.AP

BATCH, SEQ, DIM = 2, 4096, 256
TOKENS = BATCH * SEQ
P = 128
HALVES = DIM // P
HEADS, HEAD = 16, 16
CHUNK = 16
GROUPS = TOKENS // (P * CHUNK)
GROUPS_PER_BATCH = GROUPS // BATCH
CHUNKS = TOKENS // CHUNK
MODS = 6 * DIM
MOD_SA, MOD_CA, MOD_GA, MOD_SB, MOD_CB, MOD_GB = range(6)


START = 1


def at(signals):
    return signals + START


class Semaphores:

    def __init__(self, nc, ctx, prefix):
        self.nc, self.ctx, self.prefix, self.all = nc, ctx, prefix, []

    def __call__(self, name):
        self.all.append(self.ctx.enter_context(self.nc.semaphore(self.prefix + name)))
        return self.all[-1]

    def start(self):
        with self.nc.Block() as block:
            @block.sync
            def _(sync):
                for s in self.all:
                    sync.sem_inc(s, START)


class Chain:

    def __init__(self, engine, sem, start=0):
        self.engine, self.sem, self.start, self.steps = engine, sem, start, 0
        self.last = (sem, start)

    def wait(self):
        self.engine.wait_ge(self.last[0], at(self.last[1]))

    def done(self, instruction):
        self.steps += 1
        self.last = (self.sem, self.start + self.steps)
        return instruction.then_inc(self.sem, 1)

    def tell(self, instruction, sem, value):
        self.last = (sem, value)
        return instruction.then_inc(sem, 1)


def spread(ap, size):
    return ap.unsqueeze(len(ap.shape)).broadcast_to(list(ap.shape) + [size])


def view(ap, *dims, offset=0):
    return AP(ap.tensor, ap.offset + offset, [list(ap.ap[0])] + [list(d) for d in dims])


def build_modulation(nc, d):
    with ExitStack() as ctx:
        sb = lambda name, shape: ctx.enter_context(nc.sbuf_tensor(name, shape, F32))
        sem = Semaphores(nc, ctx, "")
        c_raw = sb("mod_c", [P, 2, HALVES * BATCH])
        c_silu = sb("mod_c_silu", [P, 2, HALVES * BATCH])
        weights = sb("mod_weights", [P, 2, HALVES, MODS])
        rows = sb("mod_rows", [BATCH, 2, MODS])
        tmp = sb("mod_tmp", [BATCH, 2, 2, DIM])
        out_ps = ctx.enter_context(nc.psum_tensor("mod_ps", [BATCH, 2, 4 * 512], F32))
        loaded, silued, multiplied, copied = (sem(f"mod_{n}") for n in ("loaded", "silued", "multiplied", "copied"))
        order, gated, stored = (sem(f"mod_{n}") for n in ("order", "gated", "stored"))

        sem.start()
        with nc.Block() as block:
            @block.sync
            def _(sync):
                for l in range(2):
                    sync.dma_start(c_raw[:, l, :], d["cT"][l]).then_inc(loaded, 16)
                    sync.dma_start(weights[:, l, :, :], d["wmod"][l].rearrange("(k p) n -> p k n", p=P)).then_inc(loaded, 16)
                sync.wait_ge(gated, at(1))
                for l in range(2):
                    for b in range(BATCH):
                        for g in range(GROUPS_PER_BATCH):
                            sync.dma_start(d["mod"][l, b * GROUPS_PER_BATCH + g:b * GROUPS_PER_BATCH + g + 1, :],
                                           rows[b:b + 1, l, :]).then_inc(stored, 16)
                sync.wait_ge(stored, at(16 * 2 * GROUPS))

            @block.scalar
            def _(act):
                act.wait_ge(loaded, at(64))
                act.activation(c_silu[:, :, :], c_raw[:, :, :], ACT.Silu).then_inc(silued, 1)
                act.wait_ge(multiplied, at(1))
                for l in range(2):
                    ins = act.copy(rows[:, l, :], out_ps[:, l, 0:MODS])
                    ins.then_inc(copied, 1)

            @block.tensor
            def _(pe):
                pe.wait_ge(silued, at(1))
                for l in range(2):
                    for n in range(MODS // 512):
                        for k in range(HALVES):
                            mm = pe.matmul(out_ps[:, l, n * 512:(n + 1) * 512], c_silu[:, l, k * BATCH:(k + 1) * BATCH],
                                           weights[:, l, k, n * 512:(n + 1) * 512], start=(k == 0), stop=(k == HALVES - 1))
                mm.then_inc(multiplied, 1)

            @block.vector
            def _(vec):
                seq = Chain(vec, order)
                vec.wait_ge(copied, at(2))
                part = rows[:, :, :].rearrange("b l (m f) -> b l m f", m=6)
                for m in (MOD_CA, MOD_CB):
                    seq.wait()
                    seq.done(vec.tensor_scalar(part[:, :, m, :], part[:, :, m, :], 1.0, None, ALU.add))
                for m in (MOD_GA, MOD_GB):
                    seq.wait()
                    seq.done(vec.scalar_tensor_tensor(tmp[:, 0], part[:, :, m, :], -1.0, part[:, :, m, :], ALU.mult, ALU.max))
                    seq.wait()
                    seq.done(vec.tensor_scalar(tmp[:, 0], tmp[:, 0], 0.25, 2.0, ALU.max, ALU.mult))
                    seq.wait()
                    seq.done(vec.tensor_scalar(tmp[:, 1], part[:, :, m, :], 0.0, 0.5, ALU.is_ge, ALU.subtract))
                    seq.wait()
                    ins = vec.tensor_tensor(part[:, :, m, :], tmp[:, 0], tmp[:, 1], ALU.mult)
                    if m == MOD_GB:
                        seq.tell(ins, gated, 1)
                    else:
                        seq.done(ins)


def layernorm_steps(vec, seq, x, stats, moments, scale_shift, tiles, rooted, rooted_value, variances_ready, variances_value, out=None):
    out = x if out is None else out
    for j in range(tiles):
        ins = seq.done(vec.bn_stats(stats[:, j, :], x[:, j, :]))
    mean_even, mean_odd, spread_even, spread_odd = (stats[:, :, n] for n in (1, 4, 2, 5))
    mean, gap, total, var = moments[:, 0, :], moments[:, 1, :], moments[:, 2, :], scale_shift[:, 0, :]
    seq.wait()
    seq.done(vec.tensor_tensor(gap, mean_even, mean_odd, ALU.subtract))
    seq.done(vec.tensor_tensor(mean, mean_even, mean_odd, ALU.add))
    seq.done(vec.tensor_tensor(total, spread_even, spread_odd, ALU.add))
    seq.wait()
    seq.done(vec.tensor_tensor(gap, gap, gap, ALU.mult))
    seq.done(vec.tensor_scalar(mean, mean, 0.5, None, ALU.mult))
    seq.wait()
    seq.done(vec.tensor_scalar(gap, gap, 0.25, 1e-5, ALU.mult, ALU.add))
    seq.wait()
    seq.tell(vec.scalar_tensor_tensor(var, total, 1.0 / DIM, gap, ALU.mult, ALU.add), variances_ready, variances_value)
    vec.wait_ge(rooted, at(rooted_value))
    seq.done(vec.reciprocal(scale_shift[:, 0, :], scale_shift[:, 1, :]))
    seq.wait()
    for j in range(tiles):
        seq.done(vec.tensor_scalar(out[:, j, :], x[:, j, :], moments[:, 0, j:j + 1], scale_shift[:, 0, j:j + 1],
                                   ALU.subtract, ALU.mult))


PROJ = 4 * DIM + 2 * HEADS
AB = 2 * HEADS
PAIRS = CHUNK * CHUNK * HEADS


def build_delta_chunks(nc, d, gamma_last):
    T = CHUNK
    VEC_STEPS = 207
    with ExitStack() as ctx:
        sb = lambda name, shape: ctx.enter_context(nc.sbuf_tensor(name, shape, F32))
        ps = lambda name, shape: ctx.enter_context(nc.psum_tensor(name, shape, F32))
        sem = Semaphores(nc, ctx, "dc_")
        weights = sb("dc_weights", [P, HALVES, PROJ])
        ident = sb("dc_ident", [P, P])
        dt_bias = sb("dc_dt_bias", [P, HEADS])
        rate = sb("dc_rate", [P, 2, HEADS])
        mod = sb("dc_mod", [P, 2, DIM])
        h = sb("dc_h", [P, T, DIM])
        stats = sb("dc_stats", [P, T, 6])
        moments = sb("dc_moments", [P, 3, T])
        ss = sb("dc_scale_shift", [P, 2, T])
        hT = [sb(f"dc_hT{i}", [P, HALVES, P]) for i in range(2)]
        qk = sb("dc_qk", [P, T, 2 * DIM])
        vw = sb("dc_vw", [P, T, 2 * DIM])
        gate = [sb(f"dc_gate{i}", [P, DIM]) for i in range(2)]
        ab = sb("dc_ab", [P, T, AB])
        scratch = sb("dc_scratch", [P, T * DIM])
        norms = sb("dc_norms", [P, 2, 2, T * HEADS])
        decay = sb("dc_decay", [P, PAIRS])
        kk = sb("dc_kk", [P, PAIRS])
        qkd = sb("dc_qkd", [P, PAIRS])
        small = sb("dc_small", [P, 10, T * HEADS])
        Z, AZ, EZ, SQ, W2, ACC, DT, ALPHA, BETA, GAMMA = range(10)
        suffix = sb("dc_suffix", [P, T, HEADS])
        last = sb("dc_last", [P, HEADS, HEAD])
        tr_ps = [ps(f"dc_tr_ps{i}", [P, 512]) for i in range(2)]
        qk_ps = [ps(f"dc_qk_ps{i}", [P, 512]) for i in range(2)]
        vg_ps = [ps(f"dc_vg_ps{i}", [P, 512]) for i in range(2)]
        ab_ps = [ps(f"dc_ab_ps{i}", [P, 512]) for i in range(2)]
        consts, cleared, x_in, x_free, var_ready, rooted = map(sem, ("consts", "cleared", "x_in", "x_free", "var_ready", "rooted"))
        h_ready, turned, hT_ready, projected, copied, gate_ready, gate_out = map(sem, (
            "h_ready", "turned", "hT_ready", "projected", "copied", "gate_ready", "gate_out0"))
        gate_out = [gate_out, sem("gate_out1")]
        order, norms_ready, norms_rooted, z_ready, z_abs, z_exp, dt_ready, rate_ready = map(sem, (
            "order", "norms_ready", "norms_rooted", "z_ready", "z_abs", "z_exp", "dt_ready", "rate_ready"))
        qk_out_ready, vw_out_ready, g_out_ready, out_done, last_ready, last_turned, last_copied = map(sem, (
            "qk_out_ready", "vw_out_ready", "g_out_ready", "out_done", "last_ready", "last_turned", "last_copied"))

        x_v = d["x"].rearrange("(g p t) f -> g p (t f)", g=GROUPS, p=P)
        qk_v = d["qk"].rearrange("(g p t) f -> g p (t f)", g=GROUPS, p=P)
        vw_v = d["vw"].rearrange("(g p t) f -> g p (t f)", g=GROUPS, p=P)
        gate_v = d["gate"].rearrange("(g p t) f -> g p t f", g=GROUPS, p=P)
        TURNS = T

        sem.start()
        with nc.Block() as block:
            @block.sync
            def _(sync):
                sync.dma_start(weights[:, :, :], d["w_proj"].rearrange("(k p) n -> p k n", p=P)).then_inc(consts, 16)
                sync.dma_start(ident[:, :], d["ident"]).then_inc(consts, 16)
                sync.dma_start(dt_bias[:, :], d["dt_bias"].partition_broadcast(P)).then_inc(consts, 16)
                sync.dma_start(rate[:, 0, :], d["A_log"].partition_broadcast(P)).then_inc(consts, 16)
                with sync.Fori(0, GROUPS) as g:
                    sync.wait_ge(h_ready, at(g))
                    sync.wait_ge(turned, at(g * TURNS))
                    sync.dma_start(h[:, :, :].rearrange("p t f -> p (t f)"), x_v[bass.ds(g, 1)].rearrange("a p f -> (a p) f")).then_inc(x_in, 16)
                    for n, m in enumerate((MOD_SA, MOD_CA)):
                        sync.dma_start(mod[:, n, :], d["mod"][0, bass.ds(g, 1), m * DIM:(m + 1) * DIM].rearrange("a f -> (a f)").partition_broadcast(P)).then_inc(x_in, 16)
                    for j in range(T):
                        sync.wait_ge(gate_ready, at(g * T + j + 1))
                        sync.dma_start(gate_v[bass.ds(g, 1), :, j, :].rearrange("a p f -> (a p) f"), gate[j % 2][:, :]).then_inc(gate_out[j % 2], 16)
                    sync.wait_ge(g_out_ready, at(g + 1))
                    sync.dma_start(d["qkd"][bass.ds(g, 1)].rearrange("a p f -> (a p) f"), qkd[:, :]).then_inc(out_done, 16)
                    sync.wait_ge(qk_out_ready, at(g + 1))
                    sync.dma_start(qk_v[bass.ds(g, 1)].rearrange("a p f -> (a p) f"), qk[:, :, :].rearrange("p t f -> p (t f)")).then_inc(out_done, 16)
                    sync.wait_ge(vw_out_ready, at(g + 1))
                    sync.dma_start(vw_v[bass.ds(g, 1)].rearrange("a p f -> (a p) f"), vw[:, :, :].rearrange("p t f -> p (t f)")).then_inc(out_done, 16)
                for stored in gate_out:
                    sync.wait_ge(stored, at(16 * GROUPS * T // 2))
                sync.wait_ge(out_done, at(48 * GROUPS))

            @block.tensor
            def _(pe):
                pe.wait_ge(consts, at(64))

                def turn(g, j):
                    if j == 0:
                        pe.wait_ge(h_ready, at(g + 1))
                    if j >= 2:
                        pe.wait_ge(hT_ready, at(g * T + j - 1))
                    else:
                        pe.wait_ge(hT_ready, at(g * T))
                        pe.wait_ge(last_copied, at(g))
                    for k in range(HALVES):
                        mm = pe.transpose(tr_ps[j % 2][:, k * P:(k + 1) * P], h[:, j, k * P:(k + 1) * P], ident[:, :])
                    mm.then_inc(turned, 1)

                def project(g, j):
                    pe.wait_ge(hT_ready, at(g * T + j + 1))
                    if j >= 2:
                        pe.wait_ge(copied, at((g * T + j - 1) * 3))
                    else:
                        pe.wait_ge(copied, at(g * T * 3))
                    for out, a, b in ((qk_ps, 0, 512), (vg_ps, 512, 1024), (ab_ps, 1024, PROJ)):
                        for k in range(HALVES):
                            mm = pe.matmul(out[j % 2][:, 0:b - a], hT[j % 2][:, k, :], weights[:, k, a:b], start=(k == 0), stop=(k == HALVES - 1))
                    mm.then_inc(projected, 1)

                with pe.Fori(0, GROUPS) as g:
                    turn(g, 0)
                    for j in range(T):
                        if j + 1 < T:
                            turn(g, j + 1)
                        project(g, j)
                    pe.wait_ge(last_ready, at(g + 1))
                    pe.wait_ge(hT_ready, at((g + 1) * T))
                    for k in range(HALVES):
                        mm = pe.transpose(tr_ps[0][:, k * P:(k + 1) * P], last[:, k * 8:(k + 1) * 8, :].rearrange("p h j -> p (h j)"), ident[:, :])
                    mm.then_inc(last_turned, 1)

            @block.scalar
            def _(act):
                act.wait_ge(consts, at(64))
                act.activation(rate[:, 1, :], rate[:, 0, :], ACT.Exp).then_inc(rate_ready, 1)
                with act.Fori(0, GROUPS) as g:
                    act.wait_ge(var_ready, at(g + 1))
                    act.activation(ss[:, 1, :], ss[:, 0, :], ACT.Sqrt).then_inc(rooted, 1)
                    act.wait_ge(out_done, at(g * 48))
                    for j in range(T + 1):
                        if j < T:
                            act.wait_ge(turned, at(g * T + j + 1))
                            act.wait_ge(projected, at(g * T + j - 1 if j >= 2 else g * T))
                            act.copy(hT[j % 2][:, :, :].rearrange("p k t -> p (k t)"), tr_ps[j % 2][:, 0:2 * P]).then_inc(hT_ready, 1)
                        if j > 0:
                            i = j - 1
                            act.wait_ge(projected, at(g * T + i + 1))
                            act.copy(qk[:, i, :], qk_ps[i % 2][:, :]).then_inc(copied, 1)
                            act.copy(vw[:, i, 0:DIM], vg_ps[i % 2][:, 0:DIM]).then_inc(copied, 1)
                            act.wait_ge(gate_out[i % 2], at((g * (T // 2) + i // 2) * 16))
                            act.copy(gate[i % 2][:, :], vg_ps[i % 2][:, DIM:2 * DIM]).then_inc(gate_ready, 1)
                            act.copy(ab[:, i, :], ab_ps[i % 2][:, 0:AB]).then_inc(copied, 1)
                    act.wait_ge(norms_ready, at(g + 1))
                    act.activation(norms[:, 1, :, :], norms[:, 0, :, :], ACT.Sqrt).then_inc(norms_rooted, 1)
                    act.wait_ge(z_ready, at(g + 1))
                    act.activation(small[:, AZ, :], small[:, Z, :], ACT.Abs).then_inc(z_abs, 1)
                    act.wait_ge(z_abs, at(g + 1))
                    act.activation(small[:, EZ, :], small[:, AZ, :], ACT.Exp, scale=-1.0).then_inc(z_exp, 1)
                    act.wait_ge(dt_ready, at(g + 1))
                    act.activation(small[:, ALPHA, :], small[:, DT, :], ACT.Exp, scale=-1.0).then_inc(z_exp, 1)
                    act.activation(small[:, BETA, :].rearrange("p (t h) -> p t h", t=T), ab[:, :, HEADS:AB], ACT.Sigmoid).then_inc(z_exp, 1)
                    act.wait_ge(last_turned, at(g + 1))
                    act.copy(gamma_last[:, :, bass.ds(g * P, P)], tr_ps[0][:, 0:2 * P].rearrange("p (k c) -> p k c", k=HALVES)).then_inc(last_copied, 1)
                act.wait_ge(last_copied, at(GROUPS))

            @block.vector
            def _(vec):
                for z in (kk, qkd, decay):
                    vec.memset(z[:, :], 0.0).then_inc(cleared, 1)
                vec.wait_ge(cleared, at(3))
                vec.memset(decay[:, 0:T * HEADS], 1.0).then_inc(cleared, 1)
                vec.wait_ge(cleared, at(4))
                vec.memset(suffix[:, T - 1, :], 1.0).then_inc(cleared, 1)
                vec.wait_ge(cleared, at(5))
                vec.wait_ge(rate_ready, at(1))
                vec.wait_ge(consts, at(64))
                with vec.Fori(0, GROUPS) as g:
                    seq = Chain(vec, order, g * VEC_STEPS)
                    ready_at = g + 1
                    seq.wait()
                    vec.wait_ge(x_in, at((g + 1) * 48))
                    layernorm_steps(vec, seq, h[:, :, :], stats, moments, ss, T, rooted, g + 1, var_ready, g + 1)
                    seq.wait()
                    seq.done(vec.tensor_tensor(h[:, :, :], h[:, :, :], mod[:, 1:2, :].broadcast_to([P, T, DIM]), ALU.mult))
                    seq.wait()
                    seq.tell(vec.tensor_tensor(h[:, :, :], h[:, :, :], mod[:, 0:1, :].broadcast_to([P, T, DIM]), ALU.add), h_ready, g + 1)

                    vec.wait_ge(copied, at((g + 1) * T * 3))
                    qk_heads = qk[:, :, :].rearrange("p t (a h e) -> p t a h e", a=2, h=HEADS)
                    sc = scratch[:, :].rearrange("p (t f) -> p t f", t=T)
                    for a in range(2):
                        part = qk[:, :, a * DIM:(a + 1) * DIM]
                        seq.wait()
                        seq.done(vec.tensor_tensor(sc, part, part, ALU.mult))
                        seq.wait()
                        ins = vec.tensor_reduce(norms[:, 0, a, :], scratch[:, :].rearrange("p (n e) -> p n e", e=HEAD), AX.X, ALU.add)
                        if a == 0:
                            seq.done(ins)
                        else:
                            seq.tell(ins, norms_ready, g + 1)

                    def sm(n):
                        return small[:, n, :].rearrange("p (t h) -> p t h", t=T)
                    seq.wait()
                    seq.tell(vec.tensor_tensor(sm(Z), ab[:, :, 0:HEADS], dt_bias[:, :].unsqueeze(1).broadcast_to([P, T, HEADS]), ALU.add), z_ready, g + 1)
                    vec.wait_ge(norms_rooted, at(g + 1))
                    seq.done(vec.tensor_scalar(norms[:, 1, :, :], norms[:, 1, :, :], 1e-12, None, ALU.max))
                    seq.wait()
                    seq.done(vec.reciprocal(norms[:, 1, :, :], norms[:, 1, :, :]))
                    seq.wait()
                    seq.done(vec.tensor_scalar(norms[:, 1, 0, :], norms[:, 1, 0, :], HEAD ** -0.5, None, ALU.mult))
                    for a in range(2):
                        part = qk[:, :, a * DIM:(a + 1) * DIM].rearrange("p t (h e) -> p t h e", h=HEADS)
                        seq.wait()
                        seq.done(vec.tensor_tensor(part, part, spread(norms[:, 1, a, :].rearrange("p (t h) -> p t h", t=T), HEAD), ALU.mult))
                    vec.wait_ge(z_exp, at(g * 3 + 1))
                    seq.done(vec.tensor_scalar(sm(SQ), sm(EZ), 2.0, None, ALU.add))
                    seq.wait()
                    seq.done(vec.reciprocal(sm(SQ), sm(SQ)))
                    seq.wait()
                    seq.done(vec.tensor_tensor(sm(SQ), sm(EZ), sm(SQ), ALU.mult))
                    seq.wait()
                    seq.done(vec.tensor_tensor(sm(W2), sm(SQ), sm(SQ), ALU.mult))
                    seq.wait()
                    seq.done(vec.tensor_scalar(sm(ACC), sm(W2), 1.0 / 15.0, None, ALU.mult))
                    for n in (13, 11, 9, 7, 5, 3):
                        seq.wait()
                        seq.done(vec.scalar_tensor_tensor(sm(ACC), sm(ACC), 1.0 / n, sm(W2), ALU.add, ALU.mult))
                    seq.wait()
                    seq.done(vec.scalar_tensor_tensor(sm(ACC), sm(ACC), 1.0, sm(SQ), ALU.add, ALU.mult))
                    seq.wait()
                    seq.done(vec.tensor_scalar(sm(Z), sm(Z), 0.0, None, ALU.max))
                    seq.wait()
                    seq.done(vec.scalar_tensor_tensor(sm(DT), sm(ACC), 2.0, sm(Z), ALU.mult, ALU.add))
                    seq.wait()
                    seq.tell(vec.tensor_tensor(sm(DT), sm(DT), rate[:, 1:2, :].broadcast_to([P, T, HEADS]), ALU.mult), dt_ready, g + 1)

                    lag_v = lambda m, lag: m[:, lag * T * HEADS + lag * HEADS:(lag + 1) * T * HEADS]
                    for lag in range(T):
                        n = T - lag
                        for a, m in ((0, qkd), (1, kk)):
                            if a == 1 and lag == 0:
                                continue
                            if lag == 0:
                                vec.wait_ge(out_done, at(g * 48))
                            seq.wait()
                            seq.done(vec.tensor_tensor(sc[:, 0:n, :], qk[:, lag:T, a * DIM:(a + 1) * DIM], qk[:, 0:n, DIM:2 * DIM], ALU.mult))
                            seq.wait()
                            seq.done(vec.tensor_reduce(lag_v(m, lag), scratch[:, 0:n * DIM].rearrange("p (n e) -> p n e", e=HEAD), AX.X, ALU.add))

                    vec.wait_ge(z_exp, at(g * 3 + 3))
                    for lag in range(1, T):
                        seq.wait()
                        seq.done(vec.tensor_tensor(lag_v(decay, lag), decay[:, (lag - 1) * T * HEADS + lag * HEADS:lag * T * HEADS],
                                                   small[:, ALPHA, HEADS:(T - lag + 1) * HEADS], ALU.mult))
                    seq.wait()
                    seq.done(vec.tensor_tensor(sm(GAMMA), view(decay[:, :], [(T + 1) * HEADS, T], [1, HEADS]),
                                               sm(ALPHA)[:, 0:1, :].broadcast_to([P, T, HEADS]), ALU.mult))
                    seq.wait()
                    seq.done(vec.tensor_copy(suffix[:, :, :], view(decay[:, :], [-T * HEADS, T], [1, HEADS], offset=(T - 1) * (T + 1) * HEADS)))
                    seq.wait()
                    seq.tell(vec.tensor_copy(last[:, :, :], spread(sm(GAMMA)[:, T - 1, :], HEAD)), last_ready, g + 1)
                    seq.wait()
                    seq.tell(vec.tensor_tensor(qkd[:, :], qkd[:, :], decay[:, :], ALU.mult), g_out_ready, g + 1)
                    seq.wait()
                    seq.done(vec.tensor_tensor(kk[:, :], kk[:, :], decay[:, :], ALU.mult))
                    seq.wait()
                    seq.done(vec.tensor_tensor(kk[:, :].rearrange("p (l n) -> p l n", l=T), kk[:, :].rearrange("p (l n) -> p l n", l=T),
                                               small[:, BETA:BETA + 1, :].broadcast_to([P, T, T * HEADS]), ALU.mult))

                    def heads_of(buf, a):
                        return buf[:, :, a * DIM:(a + 1) * DIM].rearrange("p t (h e) -> p t h e", h=HEADS)
                    seq.wait()
                    seq.done(vec.tensor_tensor(heads_of(vw, 0), heads_of(vw, 0), spread(sm(BETA), HEAD), ALU.mult))
                    seq.wait()
                    seq.done(vec.tensor_tensor(sm(BETA), sm(BETA), sm(GAMMA), ALU.mult))
                    seq.wait()
                    seq.done(vec.tensor_tensor(heads_of(vw, 1), heads_of(qk, 1), spread(sm(BETA), HEAD), ALU.mult))
                    seq.wait()
                    seq.done(vec.tensor_scalar(sm(GAMMA), sm(GAMMA), -1.0, None, ALU.mult))
                    seq.wait()
                    seq.done(vec.tensor_tensor(heads_of(qk, 0), heads_of(qk, 0), spread(sm(GAMMA), HEAD), ALU.mult))
                    seq.wait()
                    seq.tell(vec.tensor_tensor(heads_of(qk, 1), heads_of(qk, 1), spread(suffix[:, :, :], HEAD), ALU.mult), qk_out_ready, g + 1)

                    for s in range(T - 1):
                        n = T - 1 - s
                        for a in range(2):
                            seq.wait()
                            seq.done(vec.tensor_tensor(
                                scratch[:, 0:n * DIM].rearrange("p (t h e) -> p t h e", t=n, h=HEADS),
                                view(vw[:, :, :], [0, n], [HEAD, HEADS], [1, HEAD], offset=s * 2 * DIM + a * DIM),
                                view(kk[:, :], [(T + 1) * HEADS, n], [1, HEADS], [0, HEAD], offset=T * HEADS + (s + 1) * HEADS), ALU.mult))
                            seq.wait()
                            rest = vw[:, s + 1:T, a * DIM:(a + 1) * DIM]
                            ins = vec.tensor_tensor(rest, rest, sc[:, 0:n, :], ALU.subtract)
                            if s == T - 2 and a == 1:
                                seq.tell(ins, vw_out_ready, g + 1)
                            else:
                                seq.done(ins)
                    assert seq.steps == VEC_STEPS, seq.steps


TILE_CHUNKS = P // CHUNK
BATCH_TILES = SEQ // P


def build_state_scan(nc, d, gamma_last):
    N = TILE_CHUNKS
    with ExitStack() as ctx:
        sb = lambda name, shape: ctx.enter_context(nc.sbuf_tensor("ss_" + name, shape, F32))
        ps = lambda name, shape: ctx.enter_context(nc.psum_tensor("ss_" + name, shape, F32))
        sem = Semaphores(nc, ctx, "ss_")
        both = range(2)
        ident = sb("ident", [P, P])
        block_mask = sb("block_mask", [P, P])
        wq_rows = [sb(f"wq_rows{i}", [P, BATCH, 2, DIM]) for i in both]
        k_rows = [sb(f"k_rows{i}", [CHUNK, BATCH, N, DIM]) for i in both]
        u_rows = [sb(f"u_rows{i}", [2 * CHUNK, BATCH, N, DIM]) for i in both]
        solved = [sb(f"solved{i}", [2 * CHUNK, BATCH, N, DIM]) for i in both]
        wq = [sb(f"wq{i}", [P, BATCH, HALVES, N, 2 * CHUNK]) for i in both]
        gammas = [sb(f"gammas{i}", [P, BATCH, HALVES, N]) for i in both]
        state = [sb(f"state{b}", [P, HALVES, P]) for b in range(BATCH)]
        decayed = [sb(f"decayed{b}", [P, HALVES, P]) for b in range(BATCH)]
        update = [sb(f"update{b}", [P, HALVES, P]) for b in range(BATCH)]
        turn_ps = [ps(f"turn_ps{b}", [P, 2, HALVES, P]) for b in range(BATCH)]
        read_ps = [ps(f"read_ps{b}", [2 * CHUNK, 512]) for b in range(BATCH)]
        write_ps = [ps(f"write_ps{b}", [P, 512]) for b in range(BATCH)]
        consts, order, cleared = map(sem, ("consts", "order", "cleared"))
        rows_in = [sem(f"rows_in{i}") for i in both]
        out_done = [sem(f"out_done{i}") for i in both]
        turned, wq_ready, gammas_ready = map(sem, ("turned", "wq_ready", "gammas_ready"))
        state_read = [sem(f"state_read{b}") for b in range(BATCH)]
        u_ready = [sem(f"u_ready{b}") for b in range(BATCH)]
        state_written = [sem(f"state_written{b}") for b in range(BATCH)]
        state_ready = [sem(f"state_ready{b}") for b in range(BATCH)]
        masked = [sem(f"masked{b}") for b in range(BATCH)]
        decay_ready = [sem(f"decay_ready{b}") for b in range(BATCH)]

        vw_v = d["vw"].rearrange("(b i p) f -> b i p f", b=BATCH, p=P)
        qk_v = d["qk"].rearrange("(b i p) f -> b i p f", b=BATCH, p=P)
        vw_c = d["vw"].rearrange("(b i c t) f -> b i t c f", b=BATCH, c=N, t=CHUNK)
        qk_c = d["qk"].rearrange("(b i c t) f -> b i t c f", b=BATCH, c=N, t=CHUNK)
        u_c = d["u"].rearrange("(b i c t) f -> b i t c f", b=BATCH, c=N, t=CHUNK)
        qs_c = d["qs"].rearrange("(b i c t) f -> b i t c f", b=BATCH, c=N, t=CHUNK)
        PAIR = BATCH_TILES // 2
        LOADS = 4 * BATCH * 16

        sem.start()
        with nc.Block() as block:
            @block.sync
            def _(sync):
                sync.dma_start(ident[:, :], d["ident"]).then_inc(consts, 16)
                sync.dma_start(block_mask[:, :], d["block_mask"]).then_inc(consts, 16)
                sync.wait_ge(cleared, at(2))
                with sync.Fori(0, PAIR) as ii:
                    for i in both:
                        tile = ii * 2 + i
                        for b in range(BATCH):
                            sync.wait_ge(state_written[b], at(tile * N))
                        for b in range(BATCH):
                            sync.dma_start(wq_rows[i][:, b, 0, :], vw_v[b, bass.ds(tile, 1), :, DIM:2 * DIM].rearrange("a p f -> (a p) f")).then_inc(rows_in[i], 16)
                            sync.dma_start(wq_rows[i][:, b, 1, :], qk_v[b, bass.ds(tile, 1), :, 0:DIM].rearrange("a p f -> (a p) f")).then_inc(rows_in[i], 16)
                            sync.dma_start(k_rows[i][:, b, :, :], qk_c[b, bass.ds(tile, 1), :, :, DIM:2 * DIM].rearrange("a t c f -> (a t) c f")).then_inc(rows_in[i], 16)
                            sync.dma_start(u_rows[i][0:CHUNK, b, :, :], vw_c[b, bass.ds(tile, 1), :, :, 0:DIM].rearrange("a t c f -> (a t) c f")).then_inc(rows_in[i], 16)
                    for i in both:
                        tile = ii * 2 + i
                        for b in range(BATCH):
                            sync.wait_ge(u_ready[b], at((tile + 1) * N))
                            sync.dma_start(u_c[b, bass.ds(tile, 1)].rearrange("a t c f -> (a t) c f"), solved[i][0:CHUNK, b, :, :]).then_inc(out_done[i], 16)
                            sync.dma_start(qs_c[b, bass.ds(tile, 1)].rearrange("a t c f -> (a t) c f"), solved[i][CHUNK:2 * CHUNK, b, :, :]).then_inc(out_done[i], 16)
                for i in both:
                    sync.wait_ge(out_done[i], at(PAIR * BATCH * 32))

            @block.tensor
            def _(pe):
                pe.wait_ge(consts, at(32))
                with pe.Fori(0, PAIR) as ii:
                    for i in both:
                        tile = ii * 2 + i
                        pe.wait_ge(rows_in[i], at((ii + 1) * LOADS))
                        pe.wait_ge(wq_ready, at(tile * BATCH))
                        for b in range(BATCH):
                            for a in range(2):
                                for k in range(HALVES):
                                    mm = pe.transpose(turn_ps[b][:, a, k, :], wq_rows[i][:, b, a, k * P:(k + 1) * P], ident[:, :])
                            mm.then_inc(turned, 1)
                        pe.wait_ge(wq_ready, at((tile + 1) * BATCH))
                        for c in range(N):
                            for b in range(BATCH):
                                pe.wait_ge(state_ready[b], at(tile * N + c + 1))
                                for k in range(HALVES):
                                    mm = pe.matmul(read_ps[b][:, k * P:(k + 1) * P], wq[i][:, b, k, c, :], state[b][:, k, :], start=(k == 0), stop=(k == HALVES - 1), skip_group_check=True)
                                mm.then_inc(state_read[b], 1)
                            for b in range(BATCH):
                                pe.wait_ge(u_ready[b], at(tile * N + c + 1))
                                for k in range(HALVES):
                                    mm = pe.matmul(write_ps[b][:, k * P:(k + 1) * P], k_rows[i][:, b, c, k * P:(k + 1) * P], solved[i][0:CHUNK, b, c, k * P:(k + 1) * P], start=(k == 0), stop=(k == HALVES - 1), skip_group_check=True)
                                mm.then_inc(state_written[b], 1)

            @block.scalar
            def _(act):
                with act.Fori(0, PAIR) as ii:
                    for i in both:
                        tile = ii * 2 + i
                        for b in range(BATCH):
                            act.wait_ge(state_written[b], at(tile * N))
                            act.wait_ge(turned, at(tile * BATCH + b + 1))
                            act.copy(wq[i][:, b, :, :, 0:CHUNK], turn_ps[b][:, 0, :, :].rearrange("p k (c t) -> p k c t", c=N))
                            act.copy(wq[i][:, b, :, :, CHUNK:2 * CHUNK], turn_ps[b][:, 1, :, :].rearrange("p k (c t) -> p k c t", c=N)).then_inc(wq_ready, 1)
                        act.wait_ge(gammas_ready, at((tile + 1) * BATCH))
                        for c in range(N):
                            for b in range(BATCH):
                                act.wait_ge(state_ready[b], at(tile * N + c + 1))
                                for k in range(HALVES):
                                    ins = act.activation(decayed[b][:, k, :], state[b][:, k, :], ACT.Copy, scale=gammas[i][:, b, k, c:c + 1])
                                ins.then_inc(decay_ready[b], 1)

            @block.vector
            def _(vec):
                for i in both:
                    vec.memset(u_rows[i][:, :, :, :], 0.0).then_inc(cleared, 1)
                for b in range(BATCH):
                    vec.memset(state[b][:, :, :], 0.0).then_inc(state_ready[b], 1)
                vec.wait_ge(consts, at(32))
                with vec.Fori(0, PAIR) as ii:
                    for i in both:
                        tile = ii * 2 + i
                        for b in range(BATCH):
                            vec.wait_ge(decay_ready[b], at(tile * N))
                            vec.tensor_copy(gammas[i][:, b, :, :], gamma_last[:, :, bass.ds(tile * N + b * (CHUNKS // BATCH), N)]).then_inc(gammas_ready, 1)
                        vec.wait_ge(rows_in[i], at((ii + 1) * LOADS))
                        vec.wait_ge(out_done[i], at(ii * (BATCH * 32)))
                        for c in range(N):
                            for b in range(BATCH):
                                vec.wait_ge(state_read[b], at(tile * N + c + 1))
                                vec.tensor_tensor(solved[i][:, b, c, :], u_rows[i][:, b, c, :], read_ps[b][:, 0:DIM], ALU.subtract).then_inc(u_ready[b], 1)
                            for b in range(BATCH):
                                vec.wait_ge(state_written[b], at(tile * N + c + 1))
                                vec.tensor_tensor(update[b][:, :, :], write_ps[b][:, 0:DIM].rearrange("p (k f) -> p k f", k=HALVES),
                                                  block_mask[:, :].unsqueeze(1).broadcast_to([P, HALVES, P]), ALU.mult).then_inc(masked[b], 1)
                                vec.wait_ge(decay_ready[b], at(tile * N + c + 1))
                                vec.wait_ge(masked[b], at(tile * N + c + 1))
                                vec.tensor_tensor(state[b][:, :, :], update[b][:, :, :], decayed[b][:, :, :], ALU.add).then_inc(state_ready[b], 1)


def chunk_rows(dram, g):
    return dram.rearrange("(g p t) f -> g p (t f)", g=GROUPS, p=P)[bass.ds(g, 1)].rearrange("a p f -> (a p) f")


def flat(tile):
    return tile.rearrange("p t f -> p (t f)")


def mod_row(d, layer, g, m):
    return d["mod"][layer, bass.ds(g, 1), m * DIM:(m + 1) * DIM].rearrange("a f -> (a f)").partition_broadcast(P)


def build_delta_outputs(nc, d):
    T = CHUNK
    VEC_STEPS = 36
    with ExitStack() as ctx:
        sb = lambda name, shape: ctx.enter_context(nc.sbuf_tensor("do_" + name, shape, F32))
        ps = lambda name, shape: ctx.enter_context(nc.psum_tensor("do_" + name, shape, F32))
        sem = Semaphores(nc, ctx, "do_")
        ident = sb("ident", [P, P])
        w_out = sb("w_out", [P, HALVES, DIM])
        rms_w = sb("rms_w", [P, HEAD])
        u = sb("u", [P, T, DIM])
        o = sb("o", [P, T, DIM])
        qkd = sb("qkd", [P, PAIRS])
        gate = sb("gate", [P, T, DIM])
        x = sb("x", [P, T, DIM])
        ga = sb("ga", [P, DIM])
        scratch = sb("scratch", [P, T * DIM])
        rms = sb("rms", [P, 2, T * HEADS])
        oT = [sb(f"oT{i}", [P, HALVES, P]) for i in range(2)]
        gated = [sb(f"gated{i}", [P, DIM]) for i in range(2)]
        tr_ps = [ps(f"tr_ps{i}", [P, 512]) for i in range(2)]
        y_ps = [ps(f"y_ps{i}", [P, 512]) for i in range(2)]
        consts, rows_in, order, gate_silu, gate_scaled, rms_ready, rms_rooted, o_ready = map(sem, (
            "consts", "rows_in", "order", "gate_silu", "gate_scaled", "rms_ready", "rms_rooted", "o_ready"))
        turned, oT_ready, projected, y_used, x_ready, x_out = map(sem, ("turned", "oT_ready", "projected", "y_used", "x_ready", "x_out"))

        sem.start()
        with nc.Block() as block:
            @block.sync
            def _(sync):
                sync.dma_start(ident[:, :], d["ident"]).then_inc(consts, 16)
                sync.dma_start(w_out[:, :, :], d["w_out"].rearrange("(k p) n -> p k n", p=P)).then_inc(consts, 16)
                sync.dma_start(rms_w[:, :], d["rms_w"].partition_broadcast(P)).then_inc(consts, 16)
                with sync.Fori(0, GROUPS) as g:
                    sync.wait_ge(x_out, at(g * 16))
                    sync.dma_start(flat(u[:, :, :]), chunk_rows(d["u"], g)).then_inc(rows_in, 16)
                    sync.dma_start(flat(o[:, :, :]), chunk_rows(d["qs"], g)).then_inc(rows_in, 16)
                    sync.dma_start(qkd[:, :], d["qkd"][bass.ds(g, 1)].rearrange("a p f -> (a p) f")).then_inc(rows_in, 16)
                    sync.dma_start(flat(gate[:, :, :]), chunk_rows(d["gate"], g)).then_inc(rows_in, 16)
                    sync.dma_start(flat(x[:, :, :]), chunk_rows(d["x"], g)).then_inc(rows_in, 16)
                    sync.dma_start(ga[:, :], mod_row(d, 0, g, MOD_GA)).then_inc(rows_in, 16)
                    sync.wait_ge(x_ready, at((g + 1) * T))
                    sync.dma_start(chunk_rows(d["x1"], g), flat(x[:, :, :])).then_inc(x_out, 16)
                sync.wait_ge(x_out, at(GROUPS * 16))

            @block.scalar
            def _(act):
                with act.Fori(0, GROUPS) as g:
                    act.wait_ge(rows_in, at((g + 1) * 96))
                    act.activation(gate[:, :, :], gate[:, :, :], ACT.Silu).then_inc(gate_silu, 1)
                    act.wait_ge(rms_ready, at(g + 1))
                    act.activation(rms[:, 1, :], rms[:, 0, :], ACT.Sqrt).then_inc(rms_rooted, 1)
                    for j in range(T):
                        act.wait_ge(turned, at(g * T + j + 1))
                        act.wait_ge(projected, at(g * T + j - 1 if j >= 2 else g * T))
                        act.copy(flat(oT[j % 2][:, :, :]), tr_ps[j % 2][:, 0:2 * P]).then_inc(oT_ready, 1)

            @block.gpsimd
            def _(pool):
                pool.wait_ge(consts, at(48))
                with pool.Fori(0, GROUPS) as g:
                    pool.wait_ge(gate_silu, at(g + 1))
                    rows = gate[:, :, :].rearrange("p t (h e) -> p (t h) e", e=HEAD)
                    pool.tensor_tensor(rows, rows, rms_w[:, :].unsqueeze(1).broadcast_to([P, T * HEADS, HEAD]), ALU.mult).then_inc(gate_scaled, 1)

            @block.tensor
            def _(pe):
                pe.wait_ge(consts, at(48))
                with pe.Fori(0, GROUPS) as g:
                    pe.wait_ge(o_ready, at(g + 1))
                    for j in range(T + 1):
                        if j < T:
                            pe.wait_ge(oT_ready, at(g * T + j - 1 if j >= 2 else g * T))
                            for k in range(HALVES):
                                mm = pe.transpose(tr_ps[j % 2][:, k * P:(k + 1) * P], o[:, j, k * P:(k + 1) * P], ident[:, :])
                            mm.then_inc(turned, 1)
                        if j > 0:
                            i = j - 1
                            pe.wait_ge(oT_ready, at(g * T + i + 1))
                            pe.wait_ge(y_used, at(g * T + i - 1 if i >= 2 else g * T))
                            for k in range(HALVES):
                                mm = pe.matmul(y_ps[i % 2][:, 0:DIM], oT[i % 2][:, k, :], w_out[:, k, :], start=(k == 0), stop=(k == HALVES - 1))
                            mm.then_inc(projected, 1)

            @block.vector
            def _(vec):
                vec.wait_ge(consts, at(48))
                with vec.Fori(0, GROUPS) as g:
                    seq = Chain(vec, order, g * VEC_STEPS)
                    seq.wait()
                    vec.wait_ge(rows_in, at((g + 1) * 96))
                    heads4 = lambda ap, n: ap.rearrange("p t (h e) -> p t h e", h=HEADS)
                    sc = scratch[:, :].rearrange("p (t f) -> p t f", t=T)
                    for lag in range(T):
                        n = T - lag
                        m = qkd[:, lag * T * HEADS + lag * HEADS:(lag + 1) * T * HEADS].rearrange("p (t h) -> p t h", t=n)
                        seq.wait()
                        seq.done(vec.tensor_tensor(heads4(sc[:, 0:n, :], n), heads4(u[:, 0:n, :], n), spread(m, HEAD), ALU.mult))
                        seq.wait()
                        seq.done(vec.tensor_tensor(o[:, lag:T, :], o[:, lag:T, :], sc[:, 0:n, :], ALU.add))
                    seq.wait()
                    seq.done(vec.tensor_tensor(sc, o[:, :, :], o[:, :, :], ALU.mult))
                    seq.wait()
                    seq.done(vec.tensor_reduce(rms[:, 0, :], scratch[:, :].rearrange("p (n e) -> p n e", e=HEAD), AX.X, ALU.add))
                    seq.wait()
                    seq.tell(vec.tensor_scalar(rms[:, 0, :], rms[:, 0, :], 1.0 / HEAD, 1e-6, ALU.mult, ALU.add), rms_ready, g + 1)
                    vec.wait_ge(rms_rooted, at(g + 1))
                    seq.done(vec.reciprocal(rms[:, 1, :], rms[:, 1, :]))
                    seq.wait()
                    seq.done(vec.tensor_tensor(heads4(o[:, :, :], T), heads4(o[:, :, :], T), spread(rms[:, 1, :].rearrange("p (t h) -> p t h", t=T), HEAD), ALU.mult))
                    seq.wait()
                    vec.wait_ge(gate_scaled, at(g + 1))
                    seq.tell(vec.tensor_tensor(o[:, :, :], o[:, :, :], gate[:, :, :], ALU.mult), o_ready, g + 1)
                    for j in range(T):
                        vec.wait_ge(projected, at(g * T + j + 1))
                        seq.tell(vec.tensor_tensor(gated[j % 2][:, :], y_ps[j % 2][:, 0:DIM], ga[:, :], ALU.mult), y_used, g * T + j + 1)
                        seq.wait()
                        vec.tensor_tensor(x[:, j, :], x[:, j, :], gated[j % 2][:, :], ALU.add).then_inc(x_ready, 1)
                    vec.wait_ge(x_ready, at((g + 1) * T))
                    assert seq.steps == VEC_STEPS, seq.steps


EXPERTS, TOP, HIDDEN = 32, 8, 1024
HC = HIDDEN // P


def build_token_choice(nc, d, merged, chosen):
    T = CHUNK
    VEC_STEPS = 41
    with ExitStack() as ctx:
        sb = lambda name, shape: ctx.enter_context(nc.sbuf_tensor("tc_" + name, shape, F32))
        ps = lambda name, shape: ctx.enter_context(nc.psum_tensor("tc_" + name, shape, F32))
        sem = Semaphores(nc, ctx, "tc_")
        ident = sb("ident", [P, P])
        gate_w = sb("gate_w", [P, HALVES, EXPERTS])
        gate_b = sb("gate_b", [EXPERTS, 1])
        h = sb("h", [P, GROUPS, T, DIM])
        mod = sb("mod", [P, 2, DIM])
        hm = sb("hm", [P, T, DIM])
        stats = sb("stats", [P, T, 6])
        moments = sb("moments", [P, 3, T])
        ss = sb("scale_shift", [P, 2, T])
        hT = [sb(f"hT{i}", [P, HALVES, P]) for i in range(2)]
        probs = sb("probs", [EXPERTS, BATCH, SEQ])
        stat = sb("stat", [EXPERTS, BATCH, 4])
        top = sb("top", [EXPERTS, BATCH, TOP])
        chosen_T = sb("chosen_T", [P, GROUPS * T, EXPERTS])
        tr_ps = [ps(f"tr_ps{i}", [P, 512]) for i in range(2)]
        lg_ps = [ps(f"lg_ps{i}", [EXPERTS, 512]) for i in range(2)]
        ch_ps = [ps(f"ch_ps{i}", [P, 512]) for i in range(2)]
        mg_ps = ps("mg_ps", [P, BATCH, HALVES, EXPERTS])
        consts, rows_in, order, var_ready, rooted, h_ready, turned, hT_ready = map(sem, (
            "consts", "rows_in", "order", "var_ready", "rooted", "h_ready", "turned", "hT_ready"))
        routed, logits_out, peak_ready, exp_done, chosen_ready, chosen_turned, chosen_copied, summed, merged_out = map(sem, (
            "routed", "logits_out", "peak_ready", "exp_done", "chosen_ready", "chosen_turned", "chosen_copied", "summed", "merged_out"))
        Q = 4

        sem.start()
        with nc.Block() as block:
            @block.sync
            def _(sync):
                sync.dma_start(ident[:, :], d["ident"]).then_inc(consts, 16)
                sync.dma_start(gate_w[:, :, :], d["gate0_wT"].rearrange("(k p) n -> p k n", p=P)).then_inc(consts, 16)
                sync.dma_start(gate_b[:, :], d["gate0_b"]).then_inc(consts, 16)
                with sync.Fori(0, GROUPS) as g:
                    sync.wait_ge(h_ready, at(g))
                    sync.wait_ge(turned, at(g * T))
                    sync.dma_start(flat(hm[:, :, :]), chunk_rows(d["x1"], g)).then_inc(rows_in, 16)
                    for n, m in enumerate((MOD_SB, MOD_CB)):
                        sync.dma_start(mod[:, n, :], mod_row(d, 0, g, m)).then_inc(rows_in, 16)

            @block.tensor
            def _(pe):
                pe.wait_ge(consts, at(48))
                with pe.Fori(0, GROUPS) as g:
                    pe.wait_ge(h_ready, at(g + 1))
                    for j in range(T + 1):
                        if j < T:
                            pe.wait_ge(hT_ready, at(g * T + j - 1 if j >= 2 else g * T))
                            for k in range(HALVES):
                                mm = pe.transpose(tr_ps[j % 2][:, k * P:(k + 1) * P], hm[:, j, k * P:(k + 1) * P], ident[:, :])
                            mm.then_inc(turned, 1)
                        if j > 0:
                            i = j - 1
                            bank, place = i // Q, i % Q
                            pe.wait_ge(hT_ready, at(g * T + i + 1))
                            if place == 0:
                                pe.wait_ge(logits_out, at(g * (T // Q) + bank - 1 if bank >= 2 else g * (T // Q)))
                            for k in range(HALVES):
                                mm = pe.matmul(lg_ps[bank % 2][:, place * P:(place + 1) * P], gate_w[:, k, :], hT[i % 2][:, k, :],
                                               start=(k == 0), stop=(k == HALVES - 1))
                            mm.then_inc(routed, 1)
                for b in range(BATCH):
                    pe.wait_ge(chosen_ready, at(b + 1))
                    for gg in range(GROUPS_PER_BATCH):
                        n = b * GROUPS_PER_BATCH + gg
                        if n >= 2:
                            pe.wait_ge(chosen_copied, at(n - 1))
                        for j in range(T):
                            mm = pe.transpose(ch_ps[n % 2][:, j * EXPERTS:(j + 1) * EXPERTS],
                                              chosen[:, b, gg * P * T + j:(gg + 1) * P * T:T], ident[0:EXPERTS, 0:EXPERTS])
                        mm.then_inc(chosen_turned, 1)
                for b in range(BATCH):
                    pe.wait_ge(chosen_copied, at((b + 1) * GROUPS_PER_BATCH))
                    for k in range(HALVES):
                        tiles = GROUPS_PER_BATCH * T
                        for n in range(tiles):
                            gg, j = b * GROUPS_PER_BATCH + n // T, n % T
                            mm = pe.matmul(mg_ps[:, b, k, :], h[:, gg, j, k * P:(k + 1) * P], chosen_T[:, gg * T + j, :],
                                           start=(n == 0), stop=(n == tiles - 1), skip_group_check=True)
                mm.then_inc(summed, 1)

            @block.scalar
            def _(act):
                act.wait_ge(consts, at(48))
                with act.Fori(0, GROUPS) as g:
                    act.wait_ge(var_ready, at(g + 1))
                    act.activation(ss[:, 1, :], ss[:, 0, :], ACT.Sqrt).then_inc(rooted, 1)
                    for j in range(T):
                        act.wait_ge(turned, at(g * T + j + 1))
                        act.wait_ge(routed, at(g * T + j - 1 if j >= 2 else g * T))
                        act.copy(flat(hT[j % 2][:, :, :]), tr_ps[j % 2][:, 0:2 * P]).then_inc(hT_ready, 1)
                        if j % Q == Q - 1:
                            bank = j // Q
                            act.wait_ge(routed, at(g * T + j + 1))
                            out = probs[:, :, :].rearrange("e b s -> e (b s)")[:, bass.ds(g * (P * T) + bank * Q, (P - 1) * T + Q)]
                            out = AP(out.tensor, out.offset, [list(out.ap[0]), [1, Q], [T, P]])
                            act.activation(out, lg_ps[bank % 2][:, :].rearrange("e (q p) -> e q p", q=Q), ACT.Identity, bias=gate_b[:, :]).then_inc(logits_out, 1)
                for b in range(BATCH):
                    act.wait_ge(peak_ready, at(b + 1))
                    act.activation(probs[:, b, :], probs[:, b, :], ACT.Exp, bias=stat[:, b, 0:1], accum_out=stat[:, b, 1:2]).then_inc(exp_done, 1)
                for n in range(GROUPS):
                    act.wait_ge(chosen_turned, at(n + 1))
                    act.copy(chosen_T[:, n * T:(n + 1) * T, :].rearrange("p t e -> p (t e)"), ch_ps[n % 2][:, :]).then_inc(chosen_copied, 1)
                act.wait_ge(summed, at(1))
                for b in range(BATCH):
                    for k in range(HALVES):
                        act.copy(merged[:, k, :, b], mg_ps[:, b, k, :]).then_inc(merged_out, 1)
                act.wait_ge(merged_out, at(BATCH * HALVES))

            @block.vector
            def _(vec):
                with vec.Fori(0, GROUPS) as g:
                    seq = Chain(vec, order, g * VEC_STEPS)
                    seq.wait()
                    vec.wait_ge(rows_in, at((g + 1) * 48))
                    layernorm_steps(vec, seq, hm[:, :, :], stats, moments, ss, T, rooted, g + 1, var_ready, g + 1)
                    seq.wait()
                    seq.done(vec.tensor_tensor(hm[:, :, :], hm[:, :, :], mod[:, 1:2, :].broadcast_to([P, T, DIM]), ALU.mult))
                    seq.wait()
                    seq.done(vec.tensor_tensor(hm[:, :, :], hm[:, :, :], mod[:, 0:1, :].broadcast_to([P, T, DIM]), ALU.add))
                    seq.wait()
                    seq.tell(vec.tensor_copy(h[:, bass.ds(g, 1), :, :].rearrange("p a t f -> p (a t f)"), flat(hm[:, :, :])), h_ready, g + 1)
                    assert seq.steps == VEC_STEPS, seq.steps
                vec.wait_ge(logits_out, at(GROUPS * T // Q))
                for b in range(BATCH):
                    last = vec.tensor_reduce(stat[:, b, 0:1], probs[:, b, :], AX.X, ALU.max, negate=True).then_inc(peak_ready, 1)
                seq = Chain(vec, order, GROUPS * VEC_STEPS)
                for b in range(BATCH):
                    vec.wait_ge(exp_done, at(b + 1))
                    seq.done(vec.reciprocal(stat[:, b, 2:3], stat[:, b, 1:2]))
                    seq.wait()
                    seq.done(vec.tensor_scalar(probs[:, b, :], probs[:, b, :], stat[:, b, 2:3], None, ALU.mult))
                    seq.wait()
                    seq.done(vec.max(top[:, b, :], probs[:, b, :]))
                    seq.wait()
                    seq.done(vec.match_replace(chosen[:, b, :], top[:, b, :], probs[:, b, :], 0.0))
                    seq.wait()
                    seq.tell(vec.tensor_tensor(chosen[:, b, :], probs[:, b, :], chosen[:, b, :], ALU.subtract), chosen_ready, b + 1)


def build_experts(nc, d, merged, expert_out):
    DEPTH = 4
    with ExitStack() as ctx:
        sb = lambda name, shape: ctx.enter_context(nc.sbuf_tensor("ex_" + name, shape, F32))
        ps = lambda name, shape: ctx.enter_context(nc.psum_tensor("ex_" + name, shape, F32))
        sem = Semaphores(nc, ctx, "ex_")
        ident = sb("ident", [P, P])
        w1 = [sb(f"w1_{i}", [P, HALVES, HIDDEN]) for i in range(DEPTH)]
        w2 = [sb(f"w2_{i}", [P, HC, DIM]) for i in range(DEPTH)]
        w1_bias = sb("w1_bias", [P, EXPERTS, HC])
        w2_bias = sb("w2_bias", [EXPERTS, DIM])
        hidden = [sb(f"hidden{i}", [P, HC, BATCH]) for i in range(2)]
        gelu = [sb(f"gelu{i}", [P, HC, BATCH]) for i in range(2)]
        outs = sb("outs", [P, HALVES, BATCH, EXPERTS])
        h_ps = [ps(f"h_ps{i}", [P, HC, BATCH]) for i in range(2)]
        o_ps = [ps(f"o_ps{i}", [P, HALVES, BATCH]) for i in range(2)]
        t_ps = [ps(f"t_ps{b}", [EXPERTS, DIM]) for b in range(BATCH)]
        consts, w1_done, h_ready, gelu_ready, w2_done, outs_ready, outs_turned, finished = map(sem, (
            "consts", "w1_done", "h_ready", "gelu_ready", "w2_done", "outs_ready", "outs_turned", "finished"))
        w1_in = [sem(f"w1_in{i}") for i in range(DEPTH)]
        w2_in = [sem(f"w2_in{i}") for i in range(DEPTH)]
        ROUNDS = EXPERTS // DEPTH

        sem.start()
        with nc.Block() as block:
            @block.sync
            def _(sync):
                sync.dma_start(ident[:, :], d["ident"]).then_inc(consts, 16)
                sync.dma_start(w1_bias[:, :, :], d["w1_bias"]).then_inc(consts, 16)
                sync.dma_start(w2_bias[:, :], d["w2_all"][:, HIDDEN, :]).then_inc(consts, 16)
                with sync.Fori(0, ROUNDS) as r:
                    for i in range(DEPTH):
                        e = r * DEPTH + i
                        sync.wait_ge(w1_done, at(r * DEPTH))
                        sync.dma_start(w1[i][:, :, :], d["w1_all"][bass.ds(e, 1), 0:DIM, :].rearrange("a (k p) n -> (a p) k n", p=P)).then_inc(w1_in[i], 16)
                        sync.wait_ge(w2_done, at(r * DEPTH))
                        sync.dma_start(w2[i][:, :, :], d["w2_all"][bass.ds(e, 1), 0:HIDDEN, :].rearrange("a (p c) n -> (a p) c n", p=P)).then_inc(w2_in[i], 16)

            @block.tensor
            def _(pe):
                pe.wait_ge(consts, at(48))
                with pe.Fori(0, ROUNDS) as r:
                    for i in range(DEPTH + 1):
                        if i < DEPTH:
                            e = r * DEPTH + i
                            pe.wait_ge(w1_in[i], at((r + 1) * 16))
                            pe.wait_ge(h_ready, at(r * DEPTH + i - 1 if i >= 2 else r * DEPTH))
                            for c in range(HC):
                                for k in range(HALVES):
                                    mm = pe.matmul(h_ps[i % 2][:, c, :], w1[i][:, k, c:HIDDEN:HC], merged[:, k, bass.ds(e, 1), :].rearrange("p a b -> p (a b)"),
                                                   start=(k == 0), stop=(k == HALVES - 1), skip_group_check=True)
                            mm.then_inc(w1_done, 1)
                        if i > 0:
                            n = i - 1
                            pe.wait_ge(w2_in[n], at((r + 1) * 16))
                            pe.wait_ge(gelu_ready, at(r * DEPTH + n + 1))
                            pe.wait_ge(outs_ready, at(r * DEPTH + n - 1 if n >= 2 else r * DEPTH))
                            for k in range(HALVES):
                                for c in range(HC):
                                    mm = pe.matmul(o_ps[n % 2][:, k, :], w2[n][:, c, k * P:(k + 1) * P], gelu[n % 2][:, c, :],
                                                   start=(c == 0), stop=(c == HC - 1), skip_group_check=True)
                            mm.then_inc(w2_done, 1)
                pe.wait_ge(outs_ready, at(EXPERTS))
                for b in range(BATCH):
                    for k in range(HALVES):
                        mm = pe.transpose(t_ps[b][:, k * P:(k + 1) * P], outs[:, k, b, :], ident[:, :])
                mm.then_inc(outs_turned, 1)

            @block.scalar
            def _(act):
                with act.Fori(0, ROUNDS) as r:
                    for i in range(DEPTH):
                        act.wait_ge(h_ready, at(r * DEPTH + i + 1))
                        act.wait_ge(w2_done, at(r * DEPTH + i - 1 if i >= 2 else r * DEPTH))
                        act.activation(gelu[i % 2][:, :, :], hidden[i % 2][:, :, :], ACT.Gelu).then_inc(gelu_ready, 1)

            @block.vector
            def _(vec):
                vec.wait_ge(consts, at(48))
                with vec.Fori(0, ROUNDS) as r:
                    for i in range(DEPTH + 1):
                        if i < DEPTH:
                            e = r * DEPTH + i
                            vec.wait_ge(w1_done, at(r * DEPTH + i + 1))
                            vec.wait_ge(gelu_ready, at(r * DEPTH + i - 1 if i >= 2 else r * DEPTH))
                            vec.tensor_tensor(hidden[i % 2][:, :, :], h_ps[i % 2][:, :, :],
                                              spread(w1_bias[:, bass.ds(e, 1), :].rearrange("p a c -> p (a c)"), BATCH), ALU.add).then_inc(h_ready, 1)
                        if i > 0:
                            n = i - 1
                            vec.wait_ge(w2_done, at(r * DEPTH + n + 1))
                            vec.tensor_copy(outs[:, :, :, bass.ds(r * DEPTH + n, 1)].rearrange("p k b a -> p k (b a)"), o_ps[n % 2][:, :, :]).then_inc(outs_ready, 1)
                vec.wait_ge(outs_turned, at(1))
                for b in range(BATCH):
                    vec.tensor_tensor(expert_out[:, b, :], t_ps[b][:, :], w2_bias[:, :], ALU.add).then_inc(finished, 1)
                vec.wait_ge(finished, at(BATCH))


def build_scatter(nc, d, chosen, expert_out):
    T = CHUNK
    with ExitStack() as ctx:
        sb = lambda name, shape: ctx.enter_context(nc.sbuf_tensor("sc_" + name, shape, F32))
        ps = lambda name, shape: ctx.enter_context(nc.psum_tensor("sc_" + name, shape, F32))
        sem = Semaphores(nc, ctx, "sc_")
        x = [sb(f"x{i}", [P, T, DIM]) for i in range(2)]
        gb = [sb(f"gb{i}", [P, DIM]) for i in range(2)]
        weights = [sb(f"weights{i}", [EXPERTS, P * T]) for i in range(2)]
        outs = [sb(f"outs{i}", [EXPERTS, DIM]) for i in range(2)]
        gated = [sb(f"gated{i}", [P, 2, DIM]) for i in range(2)]
        y_ps = [ps(f"y_ps{i}", [P, 2, DIM]) for i in range(2)]
        copied, summed, y_used, x_ready = map(sem, ("copied", "summed", "y_used", "x_ready"))
        rows_in = [sem(f"rows_in{i}") for i in range(2)]
        x_out = [sem(f"x_out{i}") for i in range(2)]
        PAIRS_OF_TILES = T // 2
        ROUNDS = GROUPS // 2

        sem.start()
        with nc.Block() as block:
            @block.sync
            def _(sync):
                with sync.Fori(0, ROUNDS) as r:
                    for i in range(2):
                        g = r * 2 + i
                        sync.wait_ge(x_out[i], at(r * 16))
                        sync.dma_start(flat(x[i][:, :, :]), chunk_rows(d["x1"], g)).then_inc(rows_in[i], 16)
                        sync.dma_start(gb[i][:, :], mod_row(d, 0, g, MOD_GB)).then_inc(rows_in[i], 16)
                    for i in range(2):
                        g = r * 2 + i
                        sync.wait_ge(x_ready, at((g + 1) * PAIRS_OF_TILES))
                        sync.dma_start(chunk_rows(d["x2"], g), flat(x[i][:, :, :])).then_inc(x_out[i], 16)
                for i in range(2):
                    sync.wait_ge(x_out[i], at(ROUNDS * 16))

            @block.scalar
            def _(act):
                with act.Fori(0, ROUNDS) as r:
                    for i in range(2):
                        g = r * 2 + i
                        act.wait_ge(summed, at(r * 2 * PAIRS_OF_TILES))
                        act.copy(weights[i][:, :], chosen[:, :, :].rearrange("e b s -> e (b s)")[:, bass.ds(g * (P * T), P * T)]).then_inc(copied, 1)
                        act.copy(outs[i][:, :], expert_out[:, bass.ds(r, 1), :].rearrange("e b f -> e (b f)")).then_inc(copied, 1)

            @block.tensor
            def _(pe):
                with pe.Fori(0, ROUNDS) as r:
                    for i in range(2):
                        g = r * 2 + i
                        pe.wait_ge(copied, at((g + 1) * 2))
                        for jj in range(PAIRS_OF_TILES):
                            n = g * PAIRS_OF_TILES + jj
                            pe.wait_ge(y_used, at(n - 1 if jj >= 2 else g * PAIRS_OF_TILES))
                            for s in range(2):
                                j = jj * 2 + s
                                mm = pe.matmul(y_ps[jj % 2][:, s, :], weights[i][:, j:P * T:T], outs[i][:, :], start=True, stop=True)
                            mm.then_inc(summed, 1)

            @block.vector
            def _(vec):
                with vec.Fori(0, ROUNDS) as r:
                    for i in range(2):
                        g = r * 2 + i
                        vec.wait_ge(rows_in[i], at((r + 1) * 32))
                        for jj in range(PAIRS_OF_TILES):
                            n = g * PAIRS_OF_TILES + jj
                            vec.wait_ge(summed, at(n + 1))
                            vec.tensor_tensor(gated[jj % 2][:, :, :], y_ps[jj % 2][:, :, :], gb[i][:, :].unsqueeze(1).broadcast_to([P, 2, DIM]), ALU.mult).then_inc(y_used, 1)
                            vec.wait_ge(y_used, at(n + 1))
                            vec.tensor_tensor(x[i][:, jj * 2:jj * 2 + 2, :], x[i][:, jj * 2:jj * 2 + 2, :], gated[jj % 2][:, :, :], ALU.add).then_inc(x_ready, 1)


WINDOW, TOPK, PHRASE = 64, 16, 32
SPAN = WINDOW + P
NT = 4
STEP = NT * P
STEPS = SEQ // STEP
NEG = -1e30
TAKEN = -3e38


def step_rows(dram, step):
    return dram.rearrange("(s n p) f -> s p n f", n=NT, p=P)[bass.ds(step, 1)].rearrange("a p n f -> (a p) n f")


def batch_mods(mods, b, n):
    return mods[:, bass.ds(b, 1), n, :]


def build_window_attention(nc, d):
    VEC_STEPS = 54
    WIDE = 8
    with ExitStack() as ctx:
        sb = lambda name, shape: ctx.enter_context(nc.sbuf_tensor("wa_" + name, shape, F32))
        ps = lambda name, shape: ctx.enter_context(nc.psum_tensor("wa_" + name, shape, F32))
        sem = Semaphores(nc, ctx, "wa_")
        ident = sb("ident", [P, P])
        ones = sb("ones", [P, 1])
        means = sb("means", [P, P])
        nears = sb("nears", [P, SPAN])
        w_cols = sb("w_cols", [P, 3, HALVES, DIM])
        w_rows = sb("w_rows", [P, 2, HALVES, DIM])
        col_bias = sb("col_bias", [P, 3, HALVES])
        row_bias = sb("row_bias", [P, 2 * DIM])
        band = sb("band", [P, STEPS, SPAN])
        keep = sb("keep", [P, STEPS])
        mods = sb("mods", [P, BATCH, 3, DIM])
        x = sb("x", [P, NT, DIM])
        h = sb("h", [P, NT, DIM])
        stats = sb("stats", [P, NT, 6])
        moments = sb("moments", [P, 3, NT])
        ss = sb("scale_shift", [P, 2, NT])
        hT = sb("hT", [P, HALVES, STEP])
        phT = sb("phT", [P, HALVES, 1 + STEP])
        qT = sb("qT", [P, HALVES, STEP])
        pT = sb("pT", [P, HALVES, STEP])
        kT = sb("kT", [P, HALVES, WINDOW + STEP])
        v = sb("v", [P, 1 + NT, 2 * DIM])
        scores = [sb(f"scores{i}", [P, SPAN]) for i in range(2)]
        rest = [sb(f"rest{i}", [P, 2, SPAN]) for i in range(2)]
        exps = [sb(f"exps{i}", [P, 2, SPAN]) for i in range(2)]
        probs = [sb(f"probs{i}", [P, 2 * P]) for i in range(2)]
        probs_T = [sb(f"probs_T{i}", [P, 2, P]) for i in range(2)]
        top = [sb(f"top{i}", [P, 2, 8]) for i in range(2)]
        one = [sb(f"one{i}", [P, 8]) for i in range(2)]
        out = [sb(f"out{i}", [P, DIM]) for i in range(2)]
        PH, MAX, WPH, SUM, INV = range(5)
        tr_ps = ps("tr_ps", [P, 512])
        wide_ps = [ps(f"wide_ps{i}", [P, 512]) for i in range(2)]
        vo_ps = [ps(f"vo_ps{i}", [P, 512]) for i in range(2)]
        sc_ps = [ps(f"sc_ps{i}", [P, 512]) for i in range(2)]
        pt_ps = ps("pt_ps", [P, 512])
        consts, cleared, x_in, x_out, order, var_ready, rooted, h_ready = map(sem, (
            "consts", "cleared", "x_in", "x_out", "order", "var_ready", "rooted", "h_ready"))
        turned, hT_ready, wide_done, wide_out, carried, vo_done, vo_used = map(sem, (
            "turned", "hT_ready", "wide_done", "wide_out", "carried", "vo_done", "vo_used"))
        products_ready, scored, sc_used, rest_ready, exp_done, near_done, probs_ready, probs_turned, probs_T_ready, x_ready = map(sem, (
            "products_ready", "scored", "sc_used", "rest_ready", "exp_done", "near_done", "probs_ready", "probs_turned", "probs_T_ready", "x_ready"))
        passed = sem("passed")
        CONSTS = 16 * (13 + 3 * BATCH)

        sem.start()
        with nc.Block() as block:
            @block.sync
            def _(sync):
                for tile, name in ((ident, "ident"), (ones, "ones"), (means, "means"), (nears, "nears"), (col_bias, "col_bias"),
                                   (band, "band"), (keep, "keep")):
                    sync.dma_start(tile[tuple([slice(None)] * len(tile.shape))], d[name]).then_inc(consts, 16)
                for n in range(3):
                    sync.dma_start(w_cols[:, n, :, :], d["w_cols"][n].rearrange("(k p) f -> p k f", p=P)).then_inc(consts, 16)
                for n in range(2):
                    sync.dma_start(w_rows[:, n, :, :], d["w_rows"][n].rearrange("(k p) f -> p k f", p=P)).then_inc(consts, 16)
                sync.dma_start(row_bias[:, :], d["row_bias"].partition_broadcast(P)).then_inc(consts, 16)
                for b in range(BATCH):
                    for n, m in enumerate((MOD_SA, MOD_CA, MOD_GA)):
                        sync.dma_start(mods[:, b, n, :], d["mod"][1, b * GROUPS_PER_BATCH, m * DIM:(m + 1) * DIM].partition_broadcast(P)).then_inc(consts, 16)
                with sync.Fori(0, BATCH * STEPS) as it:
                    sync.wait_ge(x_out, at(it * 16))
                    sync.dma_start(x[:, :, :], step_rows(d["x2"], it)).then_inc(x_in, 16)
                    sync.wait_ge(x_ready, at((it + 1) * NT))
                    sync.dma_start(step_rows(d["x3"], it), x[:, :, :]).then_inc(x_out, 16)
                sync.wait_ge(x_out, at(BATCH * STEPS * 16))

            @block.tensor
            def _(pe):
                pe.wait_ge(consts, at(CONSTS))
                pe.wait_ge(cleared, at(5))
                with pe.Fori(0, BATCH * STEPS) as it:
                    pe.wait_ge(h_ready, at(it + 1))
                    for n in range(NT // 2):
                        pe.wait_ge(hT_ready, at(it * (NT // 2) + n))
                        for k in range(HALVES):
                            for s in range(2):
                                mm = pe.transpose(tr_ps[:, (k * 2 + s) * P:(k * 2 + s + 1) * P], h[:, n * 2 + s, k * P:(k + 1) * P], ident[:, :])
                        mm.then_inc(turned, 1)

                    def wide(n):
                        pe.wait_ge(wide_out, at(it * WIDE + n - 1 if n >= 2 else it * WIDE))
                        bank = wide_ps[n % 2]
                        if n < 2:
                            for j in range(NT):
                                mm = pe.matmul(bank[:, j * P:(j + 1) * P], h[:, j, n * P:(n + 1) * P], means[:, :], start=True, stop=True)
                        else:
                            which, m = (n - 2) // 2, n % 2
                            if n == 2:
                                pe.wait_ge(hT_ready, at((it + 1) * (NT // 2)))
                            if n == 6:
                                pe.wait_ge(wide_out, at(it * WIDE + 2))
                            moving = phT if which == 2 else hT
                            for k in range(HALVES):
                                mm = pe.matmul(bank[:, :], w_cols[:, which, k, m * P:(m + 1) * P], moving[:, k, 0:STEP], start=(k == 0), stop=(k == HALVES - 1))
                        mm.then_inc(wide_done, 1)

                    for n in range(WIDE):
                        wide(n)
                    for j in range(NT):
                        pe.wait_ge(vo_used, at(it * 2 * NT + j - 1 if j >= 2 else it * 2 * NT))
                        for which, src in ((0, hT), (1, phT)):
                            for k in range(HALVES):
                                mm = pe.matmul(vo_ps[j % 2][:, which * DIM:(which + 1) * DIM], src[:, k, j * P:(j + 1) * P], w_rows[:, which, k, :],
                                               start=(k == 0), stop=(k == HALVES - 1))
                        mm.then_inc(vo_done, 1)
                    pe.wait_ge(wide_out, at((it + 1) * WIDE))

                    def score(j):
                        pe.wait_ge(sc_used, at(it * NT + j - 1 if j >= 2 else it * NT))
                        for k in range(HALVES):
                            pe.matmul(sc_ps[j % 2][:, 0:SPAN], qT[:, k, j * P:(j + 1) * P], kT[:, k, j * P:j * P + SPAN], start=(k == 0), stop=(k == HALVES - 1))
                        if j == 0:
                            pe.wait_ge(products_ready, at(it + 1))
                        for k in range(HALVES):
                            mm = pe.matmul(sc_ps[j % 2][:, SPAN:SPAN + 1], pT[:, k, j * P:(j + 1) * P], ones[:, :], start=(k == 0), stop=(k == HALVES - 1))
                        mm.then_inc(scored, 1)

                    score(0)
                    score(1)
                    for j in range(NT):
                        pe.wait_ge(probs_ready, at(it * NT + j + 1))
                        pe.wait_ge(probs_T_ready, at(it * NT + j))
                        for c in range(2):
                            mm = pe.transpose(pt_ps[:, c * P:(c + 1) * P], probs[j % 2][:, c * P:(c + 1) * P], ident[:, :])
                        mm.then_inc(probs_turned, 1)
                        if j + 2 < NT:
                            score(j + 2)
                        pe.wait_ge(vo_used, at(it * 2 * NT + NT + j - 1))
                        if j == 0:
                            pe.wait_ge(vo_used, at(it * 2 * NT + NT))
                        pe.wait_ge(probs_T_ready, at(it * NT + j + 1))
                        for c in range(2):
                            mm = pe.matmul(vo_ps[j % 2][:, 0:DIM], probs_T[j % 2][:, c, :], v[:, j + c, 0:DIM], start=(c == 0), stop=(c == 1))
                        mm.then_inc(vo_done, 1)

            @block.scalar
            def _(act):
                act.wait_ge(consts, at(CONSTS))
                act.wait_ge(cleared, at(5))
                with act.Fori(0, BATCH * STEPS) as it:
                    act.wait_ge(var_ready, at(it + 1))
                    act.activation(ss[:, 1, :], ss[:, 0, :], ACT.Sqrt).then_inc(rooted, 1)
                    for n in range(NT // 2):
                        act.wait_ge(turned, at(it * (NT // 2) + n + 1))
                        act.copy(hT[:, :, n * 2 * P:(n + 1) * 2 * P], tr_ps[:, :].rearrange("p (k t) -> p k t", k=HALVES)).then_inc(hT_ready, 1)
                    act.copy(phT[:, :, 0:1], phT[:, :, STEP:STEP + 1]).then_inc(carried, 1)
                    act.copy(kT[:, :, 0:WINDOW], kT[:, :, STEP:STEP + WINDOW]).then_inc(carried, 1)
                    act.wait_ge(carried, at((it + 1) * 2))
                    for n in range(WIDE):
                        act.wait_ge(wide_done, at(it * WIDE + n + 1))
                        m = n % 2
                        if n < 2:
                            ins = act.copy(phT[:, m, 1:1 + STEP], wide_ps[m][:, :])
                        else:
                            which = (n - 2) // 2
                            to = (qT[:, m, :], kT[:, m, WINDOW:WINDOW + STEP], pT[:, m, :])[which]
                            ins = act.activation(to, wide_ps[m][:, :], ACT.Identity, bias=col_bias[:, which, m:m + 1])
                        ins.then_inc(wide_out, 1)
                    for j in range(NT):
                        act.wait_ge(rest_ready, at(it * NT + j + 1))
                        act.activation(exps[j % 2][:, 0, :], scores[j % 2][:, :], ACT.Exp, bias=one[j % 2][:, MAX:MAX + 1])
                        act.activation(exps[j % 2][:, 1, :], rest[j % 2][:, 1, :], ACT.Exp, bias=one[j % 2][:, MAX:MAX + 1])
                        act.activation(one[j % 2][:, WPH:WPH + 1], one[j % 2][:, PH:PH + 1], ACT.Exp, bias=one[j % 2][:, MAX:MAX + 1]).then_inc(exp_done, 1)
                        act.wait_ge(probs_turned, at(it * NT + j + 1))
                        act.copy(probs_T[j % 2][:, :, :].rearrange("p c q -> p (c q)"), pt_ps[:, 0:2 * P]).then_inc(probs_T_ready, 1)

            @block.gpsimd
            def _(pool):
                pool.wait_ge(consts, at(CONSTS))
                with pool.Fori(0, BATCH * STEPS) as it:
                    pool.wait_ge(wide_out, at((it + 1) * WIDE))
                    pool.tensor_tensor(pT[:, :, :], qT[:, :, :], pT[:, :, :], ALU.mult).then_inc(products_ready, 1)
                    for j in range(NT):
                        pool.wait_ge(exp_done, at(it * NT + j + 1))
                        pool.tensor_tensor(exps[j % 2][:, 0, :], exps[j % 2][:, 0, :], nears[:, :], ALU.mult).then_inc(near_done, 1)

            @block.vector
            def _(vec):
                for z in (probs[0][:, :], probs[1][:, :], v[:, :, :], phT[:, :, :], kT[:, :, :]):
                    vec.memset(z, 0.0).then_inc(cleared, 1)
                vec.wait_ge(cleared, at(5))
                vec.wait_ge(consts, at(CONSTS))
                with vec.Fori(0, BATCH) as b:
                    with vec.Fori(0, STEPS) as s:
                        it = b * STEPS + s
                        seq = Chain(vec, order, it * VEC_STEPS)
                        seq.wait()
                        vec.wait_ge(x_in, at((it + 1) * 16))
                        layernorm_steps(vec, seq, x[:, :, :], stats, moments, ss, NT, rooted, it + 1, var_ready, it + 1, out=h[:, :, :])
                        seq.wait()
                        seq.done(vec.tensor_tensor(h[:, :, :], h[:, :, :], batch_mods(mods, b, 1).broadcast_to([P, NT, DIM]), ALU.mult))
                        seq.wait()
                        seq.tell(vec.tensor_tensor(h[:, :, :], h[:, :, :], batch_mods(mods, b, 0).broadcast_to([P, NT, DIM]), ALU.add), h_ready, it + 1)
                        seq.wait()
                        seq.done(vec.tensor_copy(v[:, 0, 0:DIM], v[:, NT, 0:DIM]))
                        seq.wait()
                        for j in range(NT):
                            vec.wait_ge(vo_done, at(it * 2 * NT + j + 1))
                            seq.tell(vec.tensor_tensor(v[:, 1 + j, :], vo_ps[j % 2][:, :], row_bias[:, :], ALU.add), vo_used, it * 2 * NT + j + 1)

                        def choose(j):
                            i = j % 2
                            mask = band[:, bass.ds(s, 1), :].rearrange("p a c -> p (a c)") if j == 0 else band[:, 1, :]
                            vec.wait_ge(scored, at(it * NT + j + 1))
                            seq.done(vec.scalar_tensor_tensor(scores[i][:, :], sc_ps[i][:, 0:SPAN], DIM ** -0.5, mask, ALU.mult, ALU.add))
                            seq.tell(vec.tensor_scalar(one[i][:, PH:PH + 1], sc_ps[i][:, SPAN:SPAN + 1], DIM ** -0.5, None, ALU.mult), sc_used, it * NT + j + 1)
                            seq.wait()
                            vec.sem_inc(passed, 1)
                            seq.done(vec.max(top[i][:, 0, :], scores[i][:, :]))
                            seq.wait()
                            vec.sem_inc(passed, 1)
                            seq.done(vec.match_replace(rest[i][:, 0, :], top[i][:, 0, :], scores[i][:, :], TAKEN))
                            seq.wait()
                            vec.sem_inc(passed, 1)
                            seq.done(vec.max(top[i][:, 1, :], rest[i][:, 0, :]))
                            seq.done(vec.tensor_tensor(one[i][:, MAX:MAX + 1], one[i][:, PH:PH + 1], top[i][:, 0, 0:1], ALU.max))
                            seq.wait()
                            seq.done(vec.tensor_scalar(one[i][:, MAX:MAX + 1], one[i][:, MAX:MAX + 1], -1.0, None, ALU.mult))
                            seq.wait()
                            vec.sem_inc(passed, 1)
                            seq.tell(vec.match_replace(rest[i][:, 1, :], top[i][:, 1, :], rest[i][:, 0, :], TAKEN), rest_ready, it * NT + j + 1)

                        def weigh(j):
                            i = j % 2
                            vec.wait_ge(near_done, at(it * NT + j + 1))
                            vec.wait_ge(probs_turned, at(it * NT + j - 1 if j >= 2 else it * NT))
                            seq.tell(vec.scalar_tensor_tensor(probs[i][:, 2 * P - SPAN:], exps[i][:, 0, :], 1.0, exps[i][:, 1, :], ALU.mult, ALU.subtract,
                                                                accum_out=one[i][:, SUM:SUM + 1]), probs_ready, it * NT + j + 1)
                            seq.wait()
                            seq.done(vec.tensor_tensor(one[i][:, INV:INV + 1], one[i][:, SUM:SUM + 1], one[i][:, WPH:WPH + 1], ALU.add))
                            seq.wait()
                            seq.done(vec.reciprocal(one[i][:, INV:INV + 1], one[i][:, INV:INV + 1]))
                            if j == 0:
                                seq.wait()
                                seq.done(vec.tensor_tensor(one[i][:, INV:INV + 1], one[i][:, INV:INV + 1], keep[:, bass.ds(s, 1)], ALU.mult))

                        def finish(j):
                            i = j % 2
                            vec.wait_ge(vo_done, at(it * 2 * NT + NT + j + 1))
                            seq.tell(vec.scalar_tensor_tensor(out[i][:, :], v[:, 1 + j, DIM:2 * DIM], one[i][:, WPH:WPH + 1], vo_ps[i][:, 0:DIM],
                                                                ALU.mult, ALU.add), vo_used, it * 2 * NT + NT + j + 1)
                            seq.wait()
                            seq.done(vec.scalar_tensor_tensor(out[i][:, :], out[i][:, :], one[i][:, INV:INV + 1], batch_mods(mods, b, 2).rearrange("p a f -> p (a f)"),
                                                              ALU.mult, ALU.mult))
                            seq.wait()
                            seq.tell(vec.tensor_tensor(x[:, j, :], x[:, j, :], out[i][:, :], ALU.add), x_ready, it * NT + j + 1)

                        choose(0)
                        for j in range(NT):
                            if j + 1 < NT:
                                choose(j + 1)
                            weigh(j)
                            finish(j)
                        assert seq.steps == VEC_STEPS, seq.steps


FFN_EXPERTS, ALL_EXPERTS, DFF = 8, 12, 512
FC = DFF // P


def build_mixture(nc, d):
    VEC_STEPS = 44
    with ExitStack() as ctx:
        sb = lambda name, shape, dt=F32: ctx.enter_context(nc.sbuf_tensor("mx_" + name, shape, dt))
        ps = lambda name, shape: ctx.enter_context(nc.psum_tensor("mx_" + name, shape, F32))
        sem = Semaphores(nc, ctx, "mx_")
        ident = sb("ident", [P, P])
        gate_w = sb("gate_w", [P, HALVES, ALL_EXPERTS])
        gate_b = sb("gate_b", [P, ALL_EXPERTS])
        numbers = sb("numbers", [P, ALL_EXPERTS])
        w1 = sb("w1", [P, FFN_EXPERTS, HALVES, DFF])
        w2 = sb("w2", [P, FFN_EXPERTS, FC, DIM])
        mods = sb("mods", [P, BATCH, 3, DIM])
        x = sb("x", [P, NT, DIM])
        h = sb("h", [P, NT, DIM])
        y = sb("y", [P, NT, DIM])
        stats = sb("stats", [P, NT, 6])
        moments = sb("moments", [P, 3, NT])
        ss = sb("scale_shift", [P, 2, NT])
        hT = sb("hT", [P, HALVES, STEP])
        logits = sb("logits", [P, NT, ALL_EXPERTS])
        best = sb("best", [P, NT, 8])
        best_at = sb("best_at", [P, NT, 8], mybir.dt.uint32)
        best_n = sb("best_n", [P, NT, 8])
        pair = sb("pair", [P, 2, NT])
        gap = sb("gap", [P, 2, NT])
        share = sb("share", [P, 2, NT, ALL_EXPERTS])
        pass_w = sb("pass_w", [P, NT])
        act1 = [sb(f"act1_{i}", [P, FC, STEP]) for i in range(2)]
        tr_ps = ps("tr_ps", [P, 512])
        lg_ps = ps("lg_ps", [P, NT, ALL_EXPERTS])
        h_ps = [ps(f"h_ps{i}", [P, STEP]) for i in range(2)]
        y_ps = [ps(f"y_ps{i}", [P, 2, DIM]) for i in range(4)]
        consts, x_in, x_out, order, var_ready, rooted, h_ready, passed = map(sem, (
            "consts", "x_in", "x_out", "order", "var_ready", "rooted", "h_ready", "passed"))
        turned, hT_ready, routed, gap_ready, gap_exp, up_done, up_used, down_done, down_used, x_ready = map(sem, (
            "turned", "hT_ready", "routed", "gap_ready", "gap_exp", "up_done", "up_used", "down_done", "down_used", "x_ready"))
        CONSTS = 16 * (4 + 2 * FFN_EXPERTS + 3 * BATCH)
        N_E = FFN_EXPERTS

        sem.start()
        with nc.Block() as block:
            @block.sync
            def _(sync):
                sync.dma_start(ident[:, :], d["ident"]).then_inc(consts, 16)
                sync.dma_start(gate_w[:, :, :], d["gate1_wT"].rearrange("(k p) f -> p k f", p=P)).then_inc(consts, 16)
                sync.dma_start(gate_b[:, :], d["gate1_b"].partition_broadcast(P)).then_inc(consts, 16)
                sync.dma_start(numbers[:, :], d["numbers"]).then_inc(consts, 16)
                for b in range(BATCH):
                    for n, m in enumerate((MOD_SB, MOD_CB, MOD_GB)):
                        sync.dma_start(mods[:, b, n, :], d["mod"][1, b * GROUPS_PER_BATCH, m * DIM:(m + 1) * DIM].partition_broadcast(P)).then_inc(consts, 16)
                for e in range(FFN_EXPERTS):
                    sync.dma_start(w1[:, e, :, :], d["ffn1_w1T"][e].rearrange("(k p) f -> p k f", p=P)).then_inc(consts, 16)
                    sync.dma_start(w2[:, e, :, :], d["ffn1_w2T"][e].rearrange("(c p) f -> p c f", p=P)).then_inc(consts, 16)
                with sync.Fori(0, BATCH * STEPS) as it:
                    sync.wait_ge(x_out, at(it * 16))
                    sync.dma_start(x[:, :, :], step_rows(d["x3"], it)).then_inc(x_in, 16)
                    sync.wait_ge(x_ready, at(it + 1))
                    sync.dma_start(step_rows(d["out"], it), x[:, :, :]).then_inc(x_out, 16)
                sync.wait_ge(x_out, at(BATCH * STEPS * 16))

            @block.tensor
            def _(pe):
                pe.wait_ge(consts, at(CONSTS))
                with pe.Fori(0, BATCH * STEPS) as it:
                    pe.wait_ge(h_ready, at(it + 1))
                    for n in range(NT // 2):
                        pe.wait_ge(hT_ready, at(it * (NT // 2) + n))
                        for k in range(HALVES):
                            for s in range(2):
                                mm = pe.transpose(tr_ps[:, (k * 2 + s) * P:(k * 2 + s + 1) * P], h[:, n * 2 + s, k * P:(k + 1) * P], ident[:, :])
                        mm.then_inc(turned, 1)
                    pe.wait_ge(hT_ready, at((it + 1) * (NT // 2)))
                    for j in range(NT):
                        for k in range(HALVES):
                            mm = pe.matmul(lg_ps[:, j, :], hT[:, k, j * P:(j + 1) * P], gate_w[:, k, :], start=(k == 0), stop=(k == HALVES - 1), skip_group_check=True)
                    mm.then_inc(routed, 1)

                    def up(e):
                        for c in range(FC):
                            n = e * FC + c
                            pe.wait_ge(up_used, at(it * (N_E * FC) + n - 1 if n >= 2 else it * (N_E * FC)))
                            for k in range(HALVES):
                                mm = pe.matmul(h_ps[c % 2][:, :], w1[:, e, k, c * P:(c + 1) * P], hT[:, k, :], start=(k == 0), stop=(k == HALVES - 1))
                            mm.then_inc(up_done, 1)

                    def down(e):
                        pe.wait_ge(up_used, at(it * (N_E * FC) + (e + 1) * FC))
                        for n in range(2):
                            m = e * 2 + n
                            pe.wait_ge(down_used, at(it * (N_E * 2) + m - 3 if m >= 4 else it * (N_E * 2)))
                            for s in range(2):
                                j = n * 2 + s
                                for c in range(FC):
                                    mm = pe.matmul(y_ps[m % 4][:, s, :], act1[e % 2][:, c, j * P:(j + 1) * P], w2[:, e, c, :], start=(c == 0), stop=(c == FC - 1))
                            mm.then_inc(down_done, 1)

                    up(0)
                    for e in range(N_E):
                        if e + 1 < N_E:
                            up(e + 1)
                        down(e)

            @block.scalar
            def _(act):
                act.wait_ge(consts, at(CONSTS))
                with act.Fori(0, BATCH * STEPS) as it:
                    act.wait_ge(var_ready, at(it + 1))
                    act.activation(ss[:, 1, :], ss[:, 0, :], ACT.Sqrt).then_inc(rooted, 1)
                    for n in range(NT // 2):
                        act.wait_ge(turned, at(it * (NT // 2) + n + 1))
                        act.copy(hT[:, :, n * 2 * P:(n + 1) * 2 * P], tr_ps[:, :].rearrange("p (k t) -> p k t", k=HALVES)).then_inc(hT_ready, 1)
                    act.wait_ge(gap_ready, at(it + 1))
                    act.activation(gap[:, 1, :], gap[:, 0, :], ACT.Exp).then_inc(gap_exp, 1)
                    for e in range(N_E):
                        for c in range(FC):
                            n = e * FC + c
                            act.wait_ge(up_done, at(it * (N_E * FC) + n + 1))
                            if c == 0:
                                act.wait_ge(down_done, at(it * (N_E * 2) + (e - 1) * 2 if e >= 2 else it * (N_E * 2)))
                            act.activation(act1[e % 2][:, c, :], h_ps[c % 2][:, :], ACT.Silu).then_inc(up_used, 1)

            @block.vector
            def _(vec):
                vec.wait_ge(consts, at(CONSTS))
                with vec.Fori(0, BATCH) as b:
                    with vec.Fori(0, STEPS) as s:
                        it = b * STEPS + s
                        seq = Chain(vec, order, it * VEC_STEPS)
                        seq.wait()
                        vec.wait_ge(x_in, at((it + 1) * 16))
                        layernorm_steps(vec, seq, x[:, :, :], stats, moments, ss, NT, rooted, it + 1, var_ready, it + 1, out=h[:, :, :])
                        seq.wait()
                        seq.done(vec.tensor_tensor(h[:, :, :], h[:, :, :], batch_mods(mods, b, 1).broadcast_to([P, NT, DIM]), ALU.mult))
                        seq.wait()
                        seq.tell(vec.tensor_tensor(h[:, :, :], h[:, :, :], batch_mods(mods, b, 0).broadcast_to([P, NT, DIM]), ALU.add), h_ready, it + 1)
                        vec.wait_ge(routed, at(it + 1))
                        seq.done(vec.tensor_tensor(logits[:, :, :], lg_ps[:, :, :], gate_b[:, :].unsqueeze(1).broadcast_to([P, NT, ALL_EXPERTS]), ALU.add))
                        seq.wait()
                        vec.sem_inc(passed, 1)
                        for j in range(NT):
                            seq.done(vec.max(best[:, j, :], logits[:, j, :]))
                        seq.wait()
                        vec.sem_inc(passed, 1)
                        for j in range(NT):
                            seq.done(vec.max_index(best_at[:, j, :], best[:, j, :], logits[:, j, :]))
                        seq.wait()
                        seq.done(vec.tensor_copy(best_n[:, :, :], best_at[:, :, :]))
                        seq.tell(vec.tensor_tensor(gap[:, 0, :], best[:, :, 1], best[:, :, 0], ALU.subtract), gap_ready, it + 1)
                        vec.wait_ge(gap_exp, at(it + 1))
                        seq.done(vec.tensor_scalar(pair[:, 0, :], gap[:, 1, :], 1.0, None, ALU.add))
                        seq.wait()
                        seq.done(vec.reciprocal(pair[:, 0, :], pair[:, 0, :]))
                        seq.wait()
                        seq.done(vec.tensor_tensor(pair[:, 1, :], pair[:, 0, :], gap[:, 1, :], ALU.mult))
                        seq.wait()
                        for n in range(2):
                            for j in range(NT):
                                seq.done(vec.tensor_scalar(share[:, n, j, :], numbers[:, :], best_n[:, j, n:n + 1], pair[:, n, j:j + 1], ALU.is_equal, ALU.mult))
                        seq.wait()
                        seq.done(vec.tensor_tensor(share[:, 0, :, :], share[:, 0, :, :], share[:, 1, :, :], ALU.add))
                        seq.wait()
                        seq.done(vec.tensor_reduce(pass_w[:, :], share[:, 0, :, FFN_EXPERTS:], AX.X, ALU.add))
                        seq.wait()
                        for j in range(NT):
                            seq.done(vec.tensor_scalar(y[:, j, :], h[:, j, :], pass_w[:, j:j + 1], None, ALU.mult))
                        seq.wait()
                        for e in range(N_E):
                            for n in range(2):
                                m = e * 2 + n
                                vec.wait_ge(down_done, at(it * (N_E * 2) + m + 1))
                                if e > 0:
                                    vec.wait_ge(down_used, at(it * (N_E * 2) + m - 1))
                                for t in range(2):
                                    j = n * 2 + t
                                    ins = vec.scalar_tensor_tensor(y[:, j, :], y_ps[m % 4][:, t, :], share[:, 0, j, e:e + 1], y[:, j, :], ALU.mult, ALU.add)
                                    if t == 1:
                                        seq.tell(ins, down_used, it * (N_E * 2) + m + 1)
                        seq.wait()
                        seq.done(vec.tensor_tensor(y[:, :, :], y[:, :, :], batch_mods(mods, b, 2).broadcast_to([P, NT, DIM]), ALU.mult))
                        seq.wait()
                        seq.tell(vec.tensor_tensor(x[:, :, :], x[:, :, :], y[:, :, :], ALU.add), x_ready, it + 1)
                        assert seq.steps == VEC_STEPS, seq.steps


def build_program(nc, d):
    with ExitStack() as ctx:
        sb = lambda name, shape: ctx.enter_context(nc.sbuf_tensor(name, shape, F32))
        build_modulation(nc, d)
        with nc.sbuf_tensor("gamma_last", [P, HALVES, CHUNKS], F32) as gamma_last:
            build_delta_chunks(nc, d, gamma_last)
            build_state_scan(nc, d, gamma_last)
        build_delta_outputs(nc, d)
        with ExitStack() as ffn:
            chosen = ffn.enter_context(nc.sbuf_tensor("chosen", [EXPERTS, BATCH, SEQ], F32))
            merged = ffn.enter_context(nc.sbuf_tensor("merged", [P, HALVES, EXPERTS, BATCH], F32))
            expert_out = ffn.enter_context(nc.sbuf_tensor("expert_out", [EXPERTS, BATCH, DIM], F32))
            build_token_choice(nc, d, merged, chosen)
            build_experts(nc, d, merged, expert_out)
            build_scatter(nc, d, chosen, expert_out)
        build_window_attention(nc, d)
        build_mixture(nc, d)


def constants():
    import numpy as np
    token, key = np.arange(P)[:, None], np.arange(SPAN)[None]
    other = np.arange(P)[None]
    in_window = (key >= token) & (key < token + WINDOW)
    band = np.where(in_window, 0.0, NEG)
    first = np.where(in_window & (key >= WINDOW), 0.0, NEG)
    keep = np.ones((P, STEPS))
    keep[0, 0] = 0.0
    same_phrase = (token // PHRASE == other // PHRASE) & (token <= other)
    tables = {
        "ident": np.eye(P),
        "block_mask": np.kron(np.eye(P // HEAD), np.ones((HEAD, HEAD))),
        "ones": np.ones((P, 1)),
        "means": np.where(same_phrase, 1.0 / (other % PHRASE + 1), 0.0),
        "nears": 1.0 + (key == token + WINDOW - 1),
        "band": np.stack([first] + [band] * (STEPS - 1), axis=1),
        "keep": keep,
        "numbers": np.tile(np.arange(ALL_EXPERTS), (P, 1)),
    }
    return {name: np.ascontiguousarray(table, dtype=np.float32) for name, table in tables.items()}


def kernel(**inputs):
    import numpy as np
    import concourse.bacc as bacc
    from concourse.bass_utils import run_bass_kernel_spmd as run

    a = {name: np.asarray(value) for name, value in inputs.items()}
    L0, L1 = "L0_attn_", "L1_attn_"
    halves = lambda v: v.reshape(HALVES, P)
    layouts = {
        "cT": np.stack([a[f"L{l}_c"].T.reshape(HALVES, P, BATCH).transpose(1, 0, 2).reshape(P, HALVES * BATCH) for l in range(2)]),
        "wmod": np.stack([a["L0_wmod"], a["L1_wmod"]]),
        "x": a["L0_attn_x"].reshape(TOKENS, DIM),
        "w_proj": np.concatenate([a[L0 + n] for n in ("Wq", "Wk", "Wv", "Wgate", "Walpha", "Wbeta")], axis=1),
        "dt_bias": a[L0 + "dt_bias"], "A_log": a[L0 + "A_log"], "rms_w": a[L0 + "rms_w"], "w_out": a[L0 + "Wout"],
        "gate0_wT": a["L0_ffn_gate_w"].T, "gate0_b": a["L0_ffn_gate_b"].reshape(EXPERTS, 1),
        "w1_all": a["L0_ffn_w1"], "w2_all": a["L0_ffn_w2"],
        "w1_bias": a["L0_ffn_w1"][:, DIM, :].reshape(EXPERTS, P, HC).transpose(1, 0, 2),
        "w_cols": np.stack([a[L1 + n + "_w"].T for n in ("q", "k", "pk")]),
        "w_rows": np.stack([a[L1 + n + "_w"].T for n in ("v", "pv")]),
        "col_bias": np.stack([halves(a[L1 + n + "_b"]) for n in ("q", "k", "pk")]).transpose(2, 0, 1),
        "row_bias": np.concatenate([a[L1 + n + "_b"] for n in ("v", "pv")]),
        "gate1_wT": a["L1_ffn_gate_w"].T, "gate1_b": a["L1_ffn_expert_bias"],
        "ffn1_w1T": a["L1_ffn_w1"].transpose(0, 2, 1), "ffn1_w2T": a["L1_ffn_w2"].transpose(0, 2, 1),
    }
    layouts.update(constants())

    nc = bacc.Bacc("TRN2", target_bir_lowering=False, num_devices=1)
    arrays, d = {}, {}
    for name, value in layouts.items():
        value = np.ascontiguousarray(value)
        arrays[f"in_{name}"] = value
        d[name] = nc.dram_tensor(f"in_{name}", value.shape, F32, kind="ExternalInput").ap()
    scratch = {
        "mod": (2, GROUPS, MODS), "qk": (TOKENS, 2 * DIM), "vw": (TOKENS, 2 * DIM), "gate": (TOKENS, DIM),
        "qkd": (GROUPS, P, PAIRS), "u": (TOKENS, DIM), "qs": (TOKENS, DIM),
        "x1": (TOKENS, DIM), "x2": (TOKENS, DIM), "x3": (TOKENS, DIM),
    }
    for name, shape in scratch.items():
        d[name] = nc.dram_tensor(f"scratch_{name}", shape, F32, kind="Internal").ap()
    d["out"] = nc.dram_tensor("out", (TOKENS, DIM), F32, kind="ExternalOutput").ap()
    build_program(nc, d)
    result = run(nc, [arrays], core_ids=[0])
    return result.results[0]["out"].reshape(BATCH, SEQ, DIM)
```

```python
import concourse.bass as bass
from concourse import mybir
from concourse.alu_op_type import AluOpType as ALU
from contextlib import ExitStack

F32 = mybir.dt.float32
ACT = mybir.ActivationFunctionType
AX = mybir.AxisListType
AP = bass.AP

BATCH, SEQ, DIM = 2, 4096, 256
TOKENS = BATCH * SEQ
P = 128
HALVES = DIM // P
HEADS, HEAD = 16, 16
CHUNK = 16
GROUPS = TOKENS // (P * CHUNK)
GROUPS_PER_BATCH = GROUPS // BATCH
CHUNKS = TOKENS // CHUNK
MODS = 6 * DIM
MOD_SA, MOD_CA, MOD_GA, MOD_SB, MOD_CB, MOD_GB = range(6)


START = 1


def at(signals):
    return signals + START


class Semaphores:

    def __init__(self, nc, ctx, prefix):
        self.nc, self.prefix, self.all, self.unstarted = nc, prefix, [], []
        ctx.callback(self.clear)

    def __call__(self, name):
        self.all.append(self.nc.alloc_semaphore(self.prefix + name))
        return self.all[-1]

    def from_zero(self, name):
        self.unstarted.append(self.nc.alloc_semaphore(self.prefix + name))
        return self.unstarted[-1]

    def clear(self):
        self.nc.clear_and_free_semaphores(self.all + self.unstarted)
        self.nc.all_engine_barrier()

    def start(self):
        with self.nc.Block() as block:
            @block.sync
            def _(sync):
                for s in self.all:
                    sync.sem_inc(s, START)


class Chain:

    def __init__(self, engine, sem, start=0):
        self.engine, self.sem, self.start, self.steps = engine, sem, start, 0
        self.last = (sem, start)

    def wait(self):
        self.engine.wait_ge(self.last[0], at(self.last[1]))

    def done(self, instruction):
        self.steps += 1
        self.last = (self.sem, self.start + self.steps)
        return instruction.then_inc(self.sem, 1)

    def tell(self, instruction, sem, value):
        self.last = (sem, value)
        return instruction.then_inc(sem, 1)


def spread(ap, size):
    return ap.unsqueeze(len(ap.shape)).broadcast_to(list(ap.shape) + [size])


def view(ap, *dims, offset=0):
    return AP(ap.tensor, ap.offset + offset, [list(ap.ap[0])] + [list(d) for d in dims])


def chunk_rows(dram, g):
    return dram.rearrange("(g p t) f -> g p (t f)", g=GROUPS, p=P)[bass.ds(g, 1)].rearrange("a p f -> (a p) f")


def mod_row(d, layer, g, m):
    return d["mod"][layer, bass.ds(g, 1), m * DIM:(m + 1) * DIM].rearrange("a f -> (a f)").partition_broadcast(P)


def build_modulation(nc, d):
    with ExitStack() as ctx:
        sb = lambda name, shape: ctx.enter_context(nc.sbuf_tensor(name, shape, F32))
        sem = Semaphores(nc, ctx, "")
        c_raw = sb("mod_c", [P, 2, HALVES * BATCH])
        c_silu = sb("mod_c_silu", [P, 2, HALVES * BATCH])
        weights = sb("mod_weights", [P, 2, HALVES, MODS])
        rows = sb("mod_rows", [BATCH, 2, MODS])
        tmp = sb("mod_tmp", [BATCH, 2, 2, DIM])
        out_ps = ctx.enter_context(nc.psum_tensor("mod_ps", [BATCH, 2, 4 * 512], F32))
        loaded, silued, multiplied, copied = (sem(f"mod_{n}") for n in ("loaded", "silued", "multiplied", "copied"))
        order, gated, stored = (sem(f"mod_{n}") for n in ("order", "gated", "stored"))

        sem.start()
        with nc.Block() as block:
            @block.sync
            def _(sync):
                for l in range(2):
                    sync.dma_start(c_raw[:, l, :], d["cT"][l]).then_inc(loaded, 16)
                    sync.dma_start(weights[:, l, :, :], d["wmod"][l].rearrange("(k p) n -> p k n", p=P)).then_inc(loaded, 16)
                sync.wait_ge(gated, at(1))
                for l in range(2):
                    for b in range(BATCH):
                        for g in range(GROUPS_PER_BATCH):
                            sync.dma_start(d["mod"][l, b * GROUPS_PER_BATCH + g:b * GROUPS_PER_BATCH + g + 1, :],
                                           rows[b:b + 1, l, :]).then_inc(stored, 16)
                sync.wait_ge(stored, at(16 * 2 * GROUPS))

            @block.scalar
            def _(act):
                act.wait_ge(loaded, at(64))
                act.activation(c_silu[:, :, :], c_raw[:, :, :], ACT.Silu).then_inc(silued, 1)
                act.wait_ge(multiplied, at(1))
                for l in range(2):
                    ins = act.copy(rows[:, l, :], out_ps[:, l, 0:MODS])
                    ins.then_inc(copied, 1)

            @block.tensor
            def _(pe):
                pe.wait_ge(silued, at(1))
                for l in range(2):
                    for n in range(MODS // 512):
                        for k in range(HALVES):
                            mm = pe.matmul(out_ps[:, l, n * 512:(n + 1) * 512], c_silu[:, l, k * BATCH:(k + 1) * BATCH],
                                           weights[:, l, k, n * 512:(n + 1) * 512], start=(k == 0), stop=(k == HALVES - 1))
                mm.then_inc(multiplied, 1)

            @block.vector
            def _(vec):
                seq = Chain(vec, order)
                vec.wait_ge(copied, at(2))
                part = rows[:, :, :].rearrange("b l (m f) -> b l m f", m=6)
                for m in (MOD_CA, MOD_CB):
                    seq.wait()
                    seq.done(vec.tensor_scalar(part[:, :, m, :], part[:, :, m, :], 1.0, None, ALU.add))
                for m in (MOD_GA, MOD_GB):
                    seq.wait()
                    seq.done(vec.scalar_tensor_tensor(tmp[:, 0], part[:, :, m, :], -1.0, part[:, :, m, :], ALU.mult, ALU.max))
                    seq.wait()
                    seq.done(vec.tensor_scalar(tmp[:, 0], tmp[:, 0], 0.25, 2.0, ALU.max, ALU.mult))
                    seq.wait()
                    seq.done(vec.tensor_scalar(tmp[:, 1], part[:, :, m, :], 0.0, 0.5, ALU.is_ge, ALU.subtract))
                    seq.wait()
                    ins = vec.tensor_tensor(part[:, :, m, :], tmp[:, 0], tmp[:, 1], ALU.mult)
                    if m == MOD_GB:
                        seq.tell(ins, gated, 1)
                    else:
                        seq.done(ins)


def layernorm_steps(vec, seq, x, stats, moments, scale_shift, tiles, rooted, rooted_value, variances_ready, variances_value, out=None):
    out = x if out is None else out
    for j in range(tiles):
        ins = seq.done(vec.bn_stats(stats[:, j, :], x[:, j, :]))
    mean_even, mean_odd, spread_even, spread_odd = (stats[:, :, n] for n in (1, 4, 2, 5))
    mean, gap, total, var = moments[:, 0, :], moments[:, 1, :], moments[:, 2, :], scale_shift[:, 0, :]
    seq.wait()
    seq.done(vec.tensor_tensor(gap, mean_even, mean_odd, ALU.subtract))
    seq.done(vec.tensor_tensor(mean, mean_even, mean_odd, ALU.add))
    seq.done(vec.tensor_tensor(total, spread_even, spread_odd, ALU.add))
    seq.wait()
    seq.done(vec.tensor_tensor(gap, gap, gap, ALU.mult))
    seq.done(vec.tensor_scalar(mean, mean, 0.5, None, ALU.mult))
    seq.wait()
    seq.done(vec.tensor_scalar(gap, gap, 0.25, 1e-5, ALU.mult, ALU.add))
    seq.wait()
    seq.tell(vec.scalar_tensor_tensor(var, total, 1.0 / DIM, gap, ALU.mult, ALU.add), variances_ready, variances_value)
    vec.wait_ge(rooted, at(rooted_value))
    seq.done(vec.reciprocal(scale_shift[:, 0, :], scale_shift[:, 1, :]))
    seq.wait()
    for j in range(tiles):
        seq.done(vec.tensor_scalar(out[:, j, :], x[:, j, :], moments[:, 0, j:j + 1], scale_shift[:, 0, j:j + 1],
                                   ALU.subtract, ALU.mult))


PROJ = 4 * DIM + 2 * HEADS
AB = 2 * HEADS
TILE_CHUNKS = P // CHUNK
TILES_OF_GROUP = CHUNK
PAIRS = CHUNK * CHUNK * HEADS


def build_delta_chunks(nc, d, gamma_last):
    T = CHUNK
    VEC_STEPS = 175
    NORM_STEPS = 40
    with ExitStack() as ctx:
        sb = lambda name, shape: ctx.enter_context(nc.sbuf_tensor(name, shape, F32))
        ps = lambda name, shape: ctx.enter_context(nc.psum_tensor(name, shape, F32))
        sem = Semaphores(nc, ctx, "dc_")
        weights = sb("dc_weights", [P, HALVES, PROJ])
        ident = sb("dc_ident", [P, P])
        dt_bias = sb("dc_dt_bias", [P, HEADS])
        rate = sb("dc_rate", [P, 2, HEADS])
        mod = sb("dc_mod", [P, 2, DIM])
        h = sb("dc_h", [P, T, DIM])
        stats = sb("dc_stats", [P, T, 6])
        moments = sb("dc_moments", [P, 3, T])
        ss = sb("dc_scale_shift", [P, 2, T])
        hT = [sb(f"dc_hT{i}", [P, HALVES, P]) for i in range(2)]
        qk = sb("dc_qk", [P, T, 2 * DIM])
        vk = sb("dc_vk", [P, T, 2 * DIM])
        gate = [sb(f"dc_gate{i}", [P, DIM]) for i in range(2)]
        ab = sb("dc_ab", [P, T, AB])
        scratch = sb("dc_scratch", [P, T * DIM])
        norms = sb("dc_norms", [P, 2, 2, T * HEADS])
        decay = sb("dc_decay", [P, PAIRS])
        kk = sb("dc_kk", [P, PAIRS])
        qkd = sb("dc_qkd", [P, PAIRS])
        small = sb("dc_small", [P, 10, T * HEADS])
        Z, AZ, EZ, SQ, W2, ACC, DT, ALPHA, BETA, GAMMA = range(10)
        last = sb("dc_last", [P, HEADS, HEAD])
        chunk_mask = sb("dc_chunk_mask", [P, TILE_CHUNKS])
        inverse = [sb(f"dc_inverse{i}", [P, HEADS, T]) for i in range(2)]
        blocks = [sb(f"dc_blocks{i}", [P, HEADS, TILE_CHUNKS, T]) for i in range(2)]
        sides = [sb(f"dc_sides{i}", [P, 2, DIM]) for i in range(2)]
        vw = [sb(f"dc_vw{i}", [P, 2, DIM]) for i in range(2)]
        tr_ps = [ps(f"dc_tr_ps{i}", [P, 512]) for i in range(2)]
        qk_ps = [ps(f"dc_qk_ps{i}", [P, 512]) for i in range(2)]
        vg_ps = [ps(f"dc_vg_ps{i}", [P, 512]) for i in range(2)]
        ab_ps = [ps(f"dc_ab_ps{i}", [P, 512]) for i in range(2)]
        consts, cleared, x_in, x_free, var_ready, rooted = map(sem, ("consts", "cleared", "x_in", "x_free", "var_ready", "rooted"))
        h_ready, turned, hT_ready, projected, copied, gate_ready, gate_out = map(sem, (
            "h_ready", "turned", "hT_ready", "projected", "copied", "gate_ready", "gate_out0"))
        gate_out = [gate_out, sem("gate_out1")]
        order, norms_ready, norms_rooted, z_ready, z_abs, z_exp, dt_ready, rate_ready = map(sem, (
            "order", "norms_ready", "norms_rooted", "z_ready", "z_abs", "z_exp", "dt_ready", "rate_ready"))
        qk_out_ready, vk_out_ready, g_out_ready, out_done, last_ready, last_turned, last_copied = map(sem, (
            "qk_out_ready", "vk_out_ready", "g_out_ready", "out_done", "last_ready", "last_turned", "last_copied"))
        solved_ready = sem("solved_ready")
        tile_in, blocks_ready, tile_solved, tile_copied, tile_out = ([sem(f"{n}{i}") for i in range(2)] for n in (
            "tile_in", "blocks_ready", "tile_solved", "tile_copied", "tile_out"))
        v_copied, qk_stored = sem("v_copied"), sem("qk_stored")

        qk_v = d["qk"].rearrange("(g p t) f -> g p (t f)", g=GROUPS, p=P)
        vk_v = d["vk"].rearrange("(g p t) f -> g p (t f)", g=GROUPS, p=P)
        gate_v = d["gate"].rearrange("(g p t) f -> g p t f", g=GROUPS, p=P)
        TURNS = 2 * T
        PAIRED = TILES_OF_GROUP // 2
        tile_rows = lambda dram, tile: dram.rearrange("(i p) f -> i p f", p=P)[bass.ds(tile, 1)].rearrange("a p f -> (a p) f")

        sem.start()
        with nc.Block() as block:
            @block.sync
            def _(sync):
                sync.dma_start(weights[:, :, :], d["w_proj"].rearrange("(k p) n -> p k n", p=P)).then_inc(consts, 16)
                sync.dma_start(ident[:, :], d["ident"]).then_inc(consts, 16)
                sync.dma_start(dt_bias[:, :], d["dt_bias"].partition_broadcast(P)).then_inc(consts, 16)
                sync.dma_start(rate[:, 0, :], d["A_log"].partition_broadcast(P)).then_inc(consts, 16)
                sync.dma_start(chunk_mask[:, :], d["chunk_mask"]).then_inc(consts, 16)

                def load_tiles(before):
                    sync.wait_ge(out_done, at((before + 1) * 48))
                    for n in range(TILES_OF_GROUP):
                        i, tile, pair = n % 2, before * TILES_OF_GROUP + n, before * PAIRED + n // 2
                        sync.wait_ge(tile_solved[i], at(pair))
                        sync.dma_start(inverse[i][:, :, :].rearrange("p h t -> p (h t)"), tile_rows(d["inverse"], tile)).then_inc(tile_in[i], 16)
                        sync.dma_start(sides[i][:, :, :].rearrange("p a f -> p (a f)"), tile_rows(d["vk"], tile)).then_inc(tile_in[i], 16)

                def load_rows(g):
                    sync.wait_ge(turned, at(g * TURNS))
                    sync.dma_start(h[:, :, :].rearrange("p t f -> p (t f)"), chunk_rows(d["x"], g)).then_inc(x_in, 16)
                    for n, m in enumerate((MOD_SA, MOD_CA)):
                        sync.dma_start(mod[:, n, :], mod_row(d, 0, g, m)).then_inc(x_in, 16)

                def group(g, before, more):
                    for j in range(T):
                        sync.wait_ge(gate_ready, at(g * T + j + 1))
                        sync.dma_start(gate_v[bass.ds(g, 1), :, j, :].rearrange("a p f -> (a p) f"), gate[j % 2][:, :]).then_inc(gate_out[j % 2], 16)
                    if more:
                        load_rows(g + 1)
                    if before is not None:
                        load_tiles(before)
                    sync.wait_ge(qk_out_ready, at(g + 1))
                    sync.dma_start(qk_v[bass.ds(g, 1)].rearrange("a p f -> (a p) f"), qk[:, :, :].rearrange("p t f -> p (t f)")).then_inc(qk_stored, 16)
                    sync.wait_ge(g_out_ready, at(g + 1))
                    sync.dma_start(chunk_rows(d["qkd"], g), qkd[:, :]).then_inc(out_done, 16)
                    sync.wait_ge(solved_ready, at(g + 1))
                    sync.dma_start(chunk_rows(d["inverse"], g), kk[:, :]).then_inc(out_done, 16)
                    sync.wait_ge(vk_out_ready, at(g + 1))
                    sync.dma_start(vk_v[bass.ds(g, 1)].rearrange("a p f -> (a p) f"), vk[:, :, :].rearrange("p t f -> p (t f)")).then_inc(out_done, 16)

                load_rows(0)
                group(0, None, more=True)
                with sync.Fori(1, GROUPS - 1) as g:
                    group(g, g - 1, more=True)
                group(GROUPS - 1, GROUPS - 2, more=False)
                load_tiles(GROUPS - 1)
                for stored in gate_out:
                    sync.wait_ge(stored, at(16 * GROUPS * T // 2))
                sync.wait_ge(qk_stored, at(16 * GROUPS))
                sync.wait_ge(out_done, at(48 * GROUPS))

            @block.tensor
            def _(pe):
                pe.wait_ge(consts, at(80))

                def turn(g, n):
                    if n == 0:
                        pe.wait_ge(h_ready, at(g + 1))
                    if n >= 2:
                        pe.wait_ge(hT_ready, at(g * TURNS + n - 1))
                    else:
                        pe.wait_ge(hT_ready, at(g * TURNS))
                        pe.wait_ge(last_copied, at(g))
                    for k in range(HALVES):
                        mm = pe.transpose(tr_ps[n % 2][:, k * P:(k + 1) * P], h[:, n % T, k * P:(k + 1) * P], ident[:, :])
                    mm.then_inc(turned, 1)

                def project(g, n, solved):
                    pe.wait_ge(hT_ready, at(g * TURNS + n + 1))
                    i, j = n % 2, n % T
                    if n < T:
                        parts = (qk_ps, 0, 512), (ab_ps, 1024, PROJ)
                        pe.wait_ge(copied, at((g * T + j - 1) * 2 if j >= 2 else g * T * 2))
                        if j < 2 and solved is not None:
                            pe.wait_ge(tile_copied[i], at(solved * PAIRED))
                    else:
                        parts = (vg_ps, 512, 1024),
                        pe.wait_ge(v_copied, at(g * T + j - 1 if j >= 2 else g * T))
                        pe.wait_ge(gate_ready, at(g * T + j - 1 if j >= 2 else g * T))
                    for out, a, b in parts:
                        for k in range(HALVES):
                            mm = pe.matmul(out[i][:, 0:b - a], hT[i][:, k, :], weights[:, k, a:b], start=(k == 0), stop=(k == HALVES - 1))
                    mm.then_inc(projected, 1)

                def solve_tiles(before, projections):
                    pe.wait_ge(copied, at(projections * T * 2))
                    for n in range(TILES_OF_GROUP):
                        i, pair = n % 2, before * PAIRED + n // 2
                        pe.wait_ge(tile_copied[i], at(pair))
                        pe.wait_ge(tile_in[i], at((pair + 1) * 32))
                        pe.wait_ge(blocks_ready[i], at(pair + 1))
                        for h in range(HEADS):
                            mm = pe.matmul(qk_ps[i][:, :].rearrange("p (a f) -> p a f", a=2)[:, :, h * HEAD:(h + 1) * HEAD],
                                           blocks[i][:, h, :, :].rearrange("p c t -> p (c t)"), sides[i][:, :, h * HEAD:(h + 1) * HEAD], start=True, stop=True)
                        mm.then_inc(tile_solved[i], 1)

                def group(g, before):
                    turn(g, 0)
                    for n in range(TURNS):
                        if n + 1 < TURNS:
                            turn(g, n + 1)
                        project(g, n, before)
                    if before is not None:
                        solve_tiles(before, g + 1)
                    pe.wait_ge(last_ready, at(g + 1))
                    pe.wait_ge(hT_ready, at((g + 1) * TURNS))
                    for k in range(HALVES):
                        mm = pe.transpose(tr_ps[0][:, k * P:(k + 1) * P], last[:, k * 8:(k + 1) * 8, :].rearrange("p h j -> p (h j)"), ident[:, :])
                    mm.then_inc(last_turned, 1)

                group(0, None)
                with pe.Fori(1, GROUPS) as g:
                    group(g, g - 1)
                solve_tiles(GROUPS - 1, GROUPS)

            @block.scalar
            def _(act):
                act.wait_ge(consts, at(80))
                act.activation(rate[:, 1, :], rate[:, 0, :], ACT.Exp).then_inc(rate_ready, 1)

                def solve_tiles(before):
                    for n in range(TILES_OF_GROUP + 1):
                        if n < TILES_OF_GROUP:
                            i, pair = n % 2, before * PAIRED + n // 2
                            act.wait_ge(tile_solved[i], at(pair))
                            act.wait_ge(tile_in[i], at((pair + 1) * 32))
                            for c in range(TILE_CHUNKS):
                                ins = act.activation(blocks[i][:, :, c, :], inverse[i][:, :, :], ACT.Copy, scale=chunk_mask[:, c:c + 1])
                            ins.then_inc(blocks_ready[i], 1)
                        if n > 0:
                            m = n - 1
                            i, pair = m % 2, before * PAIRED + m // 2
                            act.wait_ge(tile_out[i], at(pair * 16))
                            act.wait_ge(tile_solved[i], at(pair + 1))
                            act.copy(vw[i][:, :, :].rearrange("p a f -> p (a f)"), qk_ps[i][:, :]).then_inc(tile_copied[i], 1)
                            act.wait_ge(tile_copied[i], at(pair + 1))
                            act.dma_start(tile_rows(d["vw"], before * TILES_OF_GROUP + m), vw[i][:, :, :].rearrange("p a f -> p (a f)")).then_inc(tile_out[i], 16)

                def project(g, half):
                    for j in range(T + 1):
                        n = half * T + j
                        if j < T:
                            act.wait_ge(turned, at(g * TURNS + n + 1))
                            act.wait_ge(projected, at(g * TURNS + n - 1 if n >= 2 else g * TURNS))
                            act.copy(hT[n % 2][:, :, :].rearrange("p k t -> p (k t)"), tr_ps[n % 2][:, 0:2 * P]).then_inc(hT_ready, 1)
                        if j > 0:
                            i = j - 1
                            act.wait_ge(projected, at(g * TURNS + n))
                            if half == 0:
                                act.copy(qk[:, i, :], qk_ps[i % 2][:, :]).then_inc(copied, 1)
                                act.copy(ab[:, i, :], ab_ps[i % 2][:, 0:AB]).then_inc(copied, 1)
                            else:
                                if i == 0:
                                    act.wait_ge(out_done, at(g * 48))
                                act.copy(vk[:, i, 0:DIM], vg_ps[i % 2][:, 0:DIM]).then_inc(v_copied, 1)
                                act.wait_ge(gate_out[i % 2], at((g * (T // 2) + i // 2) * 16))
                                act.copy(gate[i % 2][:, :], vg_ps[i % 2][:, DIM:2 * DIM]).then_inc(gate_ready, 1)

                def root(g):
                    act.wait_ge(var_ready, at(g + 1))
                    act.activation(ss[:, 1, :], ss[:, 0, :], ACT.Sqrt).then_inc(rooted, 1)

                def group(g, before, more):
                    act.wait_ge(qk_stored, at(g * 16))
                    project(g, 0)
                    act.wait_ge(norms_ready, at(g + 1))
                    act.activation(norms[:, 1, :, :], norms[:, 0, :, :], ACT.Sqrt).then_inc(norms_rooted, 1)
                    act.wait_ge(z_ready, at(g + 1))
                    act.activation(small[:, AZ, :], small[:, Z, :], ACT.Abs).then_inc(z_abs, 1)
                    act.wait_ge(z_abs, at(g + 1))
                    act.activation(small[:, EZ, :], small[:, AZ, :], ACT.Exp, scale=-1.0).then_inc(z_exp, 1)
                    project(g, 1)
                    act.wait_ge(dt_ready, at(g + 1))
                    act.activation(small[:, ALPHA, :], small[:, DT, :], ACT.Exp, scale=-1.0).then_inc(z_exp, 1)
                    act.activation(small[:, BETA, :].rearrange("p (t h) -> p t h", t=T), ab[:, :, HEADS:AB], ACT.Sigmoid).then_inc(z_exp, 1)
                    if before is not None:
                        solve_tiles(before)
                    act.wait_ge(last_turned, at(g + 1))
                    act.copy(gamma_last[:, :, bass.ds(g * P, P)], tr_ps[0][:, 0:2 * P].rearrange("p (k c) -> p k c", k=HALVES)).then_inc(last_copied, 1)
                    if more:
                        root(g + 1)

                root(0)
                group(0, None, more=True)
                with act.Fori(1, GROUPS - 1) as g:
                    group(g, g - 1, more=True)
                group(GROUPS - 1, GROUPS - 2, more=False)
                solve_tiles(GROUPS - 1)
                act.wait_ge(last_copied, at(GROUPS))
                for i in range(2):
                    act.wait_ge(tile_out[i], at(GROUPS * PAIRED * 16))

            @block.vector
            def _(vec):
                for z in (kk, qkd, decay):
                    vec.memset(z[:, :], 0.0).then_inc(cleared, 1)
                vec.wait_ge(cleared, at(3))
                vec.memset(view(decay[:, :], [DIM + 1, T], [T, HEADS]), 1.0).then_inc(cleared, 1)
                vec.wait_ge(cleared, at(4))
                vec.wait_ge(rate_ready, at(1))
                vec.wait_ge(consts, at(80))

                def normalize(seq, g):
                    seq.wait()
                    vec.wait_ge(x_in, at((g + 1) * 48))
                    layernorm_steps(vec, seq, h[:, :, :], stats, moments, ss, T, rooted, g + 1, var_ready, g + 1)
                    seq.wait()
                    seq.done(vec.tensor_tensor(h[:, :, :], h[:, :, :], mod[:, 1:2, :].broadcast_to([P, T, DIM]), ALU.mult))
                    seq.wait()
                    seq.tell(vec.tensor_tensor(h[:, :, :], h[:, :, :], mod[:, 0:1, :].broadcast_to([P, T, DIM]), ALU.add), h_ready, g + 1)

                def group(g, more):
                    seq = Chain(vec, order, g * VEC_STEPS + NORM_STEPS)
                    seq.wait()
                    vec.wait_ge(copied, at((g + 1) * T * 2))
                    qk_heads = qk[:, :, :].rearrange("p t (a h e) -> p t a h e", a=2, h=HEADS)
                    sc = scratch[:, :].rearrange("p (t f) -> p t f", t=T)
                    for a in range(2):
                        part = qk[:, :, a * DIM:(a + 1) * DIM]
                        seq.wait()
                        seq.done(vec.tensor_tensor(sc, part, part, ALU.mult))
                        seq.wait()
                        ins = vec.tensor_reduce(norms[:, 0, a, :], scratch[:, :].rearrange("p (n e) -> p n e", e=HEAD), AX.X, ALU.add)
                        if a == 0:
                            seq.done(ins)
                        else:
                            seq.tell(ins, norms_ready, g + 1)

                    def sm(n):
                        return small[:, n, :].rearrange("p (t h) -> p t h", t=T)
                    seq.wait()
                    seq.tell(vec.tensor_tensor(sm(Z), ab[:, :, 0:HEADS], dt_bias[:, :].unsqueeze(1).broadcast_to([P, T, HEADS]), ALU.add), z_ready, g + 1)
                    vec.wait_ge(norms_rooted, at(g + 1))
                    seq.done(vec.tensor_scalar(norms[:, 1, :, :], norms[:, 1, :, :], 1e-12, None, ALU.max))
                    seq.wait()
                    seq.done(vec.reciprocal(norms[:, 1, :, :], norms[:, 1, :, :]))
                    seq.wait()
                    seq.done(vec.tensor_scalar(norms[:, 1, 0, :], norms[:, 1, 0, :], HEAD ** -0.5, None, ALU.mult))
                    for a in range(2):
                        part = qk[:, :, a * DIM:(a + 1) * DIM].rearrange("p t (h e) -> p t h e", h=HEADS)
                        seq.wait()
                        seq.done(vec.tensor_tensor(part, part, spread(norms[:, 1, a, :].rearrange("p (t h) -> p t h", t=T), HEAD), ALU.mult))
                    vec.wait_ge(z_exp, at(g * 3 + 1))
                    seq.done(vec.tensor_scalar(sm(SQ), sm(EZ), 2.0, None, ALU.add))
                    seq.wait()
                    seq.done(vec.reciprocal(sm(SQ), sm(SQ)))
                    seq.wait()
                    seq.done(vec.tensor_tensor(sm(SQ), sm(EZ), sm(SQ), ALU.mult))
                    seq.wait()
                    seq.done(vec.tensor_tensor(sm(W2), sm(SQ), sm(SQ), ALU.mult))
                    seq.wait()
                    seq.done(vec.tensor_scalar(sm(ACC), sm(W2), 1.0 / 15.0, None, ALU.mult))
                    for n in (13, 11, 9, 7, 5, 3):
                        seq.wait()
                        seq.done(vec.scalar_tensor_tensor(sm(ACC), sm(ACC), 1.0 / n, sm(W2), ALU.add, ALU.mult))
                    seq.wait()
                    seq.done(vec.scalar_tensor_tensor(sm(ACC), sm(ACC), 1.0, sm(SQ), ALU.add, ALU.mult))
                    seq.wait()
                    seq.done(vec.tensor_scalar(sm(Z), sm(Z), 0.0, None, ALU.max))
                    seq.wait()
                    seq.done(vec.scalar_tensor_tensor(sm(DT), sm(ACC), 2.0, sm(Z), ALU.mult, ALU.add))
                    seq.wait()
                    seq.tell(vec.tensor_tensor(sm(DT), sm(DT), rate[:, 1:2, :].broadcast_to([P, T, HEADS]), ALU.mult), dt_ready, g + 1)

                    lag_v = lambda m, lag: view(m[:, :], [DIM + 1, T - lag], [T, HEADS], offset=lag)
                    for lag in range(T):
                        n = T - lag
                        for a, m in ((0, qkd), (1, kk)):
                            if a == 1 and lag == 0:
                                continue
                            if lag == 0:
                                vec.wait_ge(out_done, at(g * 48))
                            seq.wait()
                            seq.done(vec.tensor_tensor(sc[:, 0:n, :], qk[:, lag:T, a * DIM:(a + 1) * DIM], qk[:, 0:n, DIM:2 * DIM], ALU.mult))
                            seq.wait()
                            seq.done(vec.tensor_reduce(lag_v(m, lag), scratch[:, 0:n * DIM].rearrange("p (n h e) -> p n h e", n=n, e=HEAD), AX.X, ALU.add))

                    vec.wait_ge(z_exp, at(g * 3 + 3))
                    for lag in range(1, T):
                        seq.wait()
                        seq.done(vec.tensor_tensor(lag_v(decay, lag), view(decay[:, :], [DIM + 1, T - lag], [T, HEADS], offset=lag - 1),
                                                   sm(ALPHA)[:, lag:T, :], ALU.mult))
                    seq.wait()
                    seq.done(vec.tensor_tensor(sm(GAMMA), view(decay[:, :], [1, T], [T, HEADS]),
                                               sm(ALPHA)[:, 0:1, :].broadcast_to([P, T, HEADS]), ALU.mult))
                    seq.wait()
                    seq.tell(vec.tensor_copy(last[:, :, :], spread(sm(GAMMA)[:, T - 1, :], HEAD)), last_ready, g + 1)
                    def heads_of(buf, a):
                        return buf[:, :, a * DIM:(a + 1) * DIM].rearrange("p t (h e) -> p t h e", h=HEADS)
                    seq.wait()
                    seq.done(vec.tensor_tensor(sm(SQ), sm(BETA), sm(GAMMA), ALU.mult))
                    seq.wait()
                    seq.done(vec.tensor_tensor(heads_of(vk, 1), heads_of(qk, 1), spread(sm(SQ), HEAD), ALU.mult))
                    seq.wait()
                    seq.done(vec.tensor_scalar(sm(GAMMA), sm(GAMMA), -1.0, None, ALU.mult))
                    seq.wait()
                    seq.done(vec.tensor_tensor(heads_of(qk, 0), heads_of(qk, 0), spread(sm(GAMMA), HEAD), ALU.mult))
                    seq.wait()
                    seq.tell(vec.tensor_tensor(heads_of(qk, 1), heads_of(qk, 1), view(decay[:, :], [DIM, T], [T, HEADS], [0, HEAD], offset=T - 1), ALU.mult), qk_out_ready, g + 1)
                    if more:
                        normalize(seq, g + 1)
                    seq.wait()
                    seq.tell(vec.tensor_tensor(qkd[:, :], qkd[:, :], decay[:, :], ALU.mult), g_out_ready, g + 1)
                    seq.wait()
                    seq.done(vec.tensor_tensor(kk[:, :], kk[:, :], decay[:, :], ALU.mult))
                    seq.wait()
                    rows = kk[:, :].rearrange("p (s h t) -> p s h t", s=T, h=HEADS)
                    seq.done(vec.tensor_scalar(sm(ACC), sm(BETA), -1.0, None, ALU.mult))
                    seq.wait()
                    seq.done(vec.tensor_tensor(rows, rows, view(small[:, ACC, :], [0, T], [1, HEADS], [HEADS, T]), ALU.mult))
                    seq.wait()
                    seq.done(vec.memset(view(kk[:, :], [DIM + 1, T], [T, HEADS]), 1.0))

                    for r in range(1, T - 1):
                        n = T - 1 - r
                        product = view(scratch[:, :], [HEADS * n, r], [n, HEADS], [1, n])
                        rest = view(kk[:, :], [DIM, r], [T, HEADS], [1, n], offset=r + 1)
                        seq.wait()
                        seq.done(vec.tensor_tensor(product, view(kk[:, :], [0, r], [T, HEADS], [1, n], offset=r * DIM + r + 1),
                                                   view(kk[:, :], [DIM, r], [T, HEADS], [0, n], offset=r), ALU.mult))
                        seq.wait()
                        ins = vec.tensor_tensor(rest, rest, product, ALU.add)
                        if r == T - 2:
                            seq.tell(ins, solved_ready, g + 1)
                        else:
                            seq.done(ins)

                    seq.wait()
                    vec.wait_ge(v_copied, at((g + 1) * T))
                    seq.tell(vec.tensor_tensor(heads_of(vk, 0), heads_of(vk, 0), spread(sm(BETA), HEAD), ALU.mult), vk_out_ready, g + 1)
                    return seq.steps

                first = Chain(vec, order)
                normalize(first, 0)
                assert first.steps == NORM_STEPS, first.steps
                assert group(0, more=True) == VEC_STEPS
                with vec.Fori(1, GROUPS - 1) as g:
                    group(g, more=True)
                group(GROUPS - 1, more=False)


BATCH_TILES = SEQ // P


def build_state_scan(nc, d, gamma_last):
    N = TILE_CHUNKS
    with ExitStack() as ctx:
        sb = lambda name, shape: ctx.enter_context(nc.sbuf_tensor("ss_" + name, shape, F32))
        ps = lambda name, shape: ctx.enter_context(nc.psum_tensor("ss_" + name, shape, F32))
        sem = Semaphores(nc, ctx, "ss_")
        both = range(2)
        ident = sb("ident", [P, P])
        block_mask = sb("block_mask", [P, P])
        wq_rows = [sb(f"wq_rows{i}", [P, BATCH, 2, DIM]) for i in both]
        k_rows = [sb(f"k_rows{i}", [CHUNK, BATCH, N, DIM]) for i in both]
        u_rows = [sb(f"u_rows{i}", [2 * CHUNK, BATCH, N, DIM]) for i in both]
        solved = [sb(f"solved{i}", [2 * CHUNK, BATCH, N, DIM]) for i in both]
        wq = [sb(f"wq{i}", [P, BATCH, HALVES, N, 2 * CHUNK]) for i in both]
        gammas = [sb(f"gammas{i}", [P, BATCH, HALVES, N]) for i in both]
        state = [sb(f"state{b}", [P, HALVES, P]) for b in range(BATCH)]
        decayed = [sb(f"decayed{b}", [P, HALVES, P]) for b in range(BATCH)]
        update = [sb(f"update{b}", [P, HALVES, P]) for b in range(BATCH)]
        turn_ps = [ps(f"turn_ps{b}", [P, 2, HALVES, P]) for b in range(BATCH)]
        read_ps = [ps(f"read_ps{b}", [2 * CHUNK, 512]) for b in range(BATCH)]
        write_ps = [ps(f"write_ps{b}", [P, 512]) for b in range(BATCH)]
        consts, order, cleared = map(sem, ("consts", "order", "cleared"))
        rows_in = [sem(f"rows_in{i}") for i in both]
        out_done = [sem(f"out_done{i}") for i in both]
        turned, wq_ready, gammas_ready = map(sem, ("turned", "wq_ready", "gammas_ready"))
        state_read = [sem(f"state_read{b}") for b in range(BATCH)]
        u_ready = [sem(f"u_ready{b}") for b in range(BATCH)]
        state_written = [sem(f"state_written{b}") for b in range(BATCH)]
        state_ready = [sem(f"state_ready{b}") for b in range(BATCH)]
        masked = [sem(f"masked{b}") for b in range(BATCH)]
        decay_ready = [sem(f"decay_ready{b}") for b in range(BATCH)]

        vw_v = d["vw"].rearrange("(b i p) f -> b i p f", b=BATCH, p=P)
        qk_v = d["qk"].rearrange("(b i p) f -> b i p f", b=BATCH, p=P)
        vw_c = d["vw"].rearrange("(b i c t) f -> b i t c f", b=BATCH, c=N, t=CHUNK)
        qk_c = d["qk"].rearrange("(b i c t) f -> b i t c f", b=BATCH, c=N, t=CHUNK)
        u_c = d["u"].rearrange("(b i c t) f -> b i t c f", b=BATCH, c=N, t=CHUNK)
        qs_c = d["qs"].rearrange("(b i c t) f -> b i t c f", b=BATCH, c=N, t=CHUNK)
        PAIR = BATCH_TILES // 2
        LOADS = 4 * BATCH * 16
        TURN_AT = N // 2

        sem.start()
        with nc.Block() as block:
            @block.sync
            def _(sync):
                sync.dma_start(ident[:, :], d["ident"]).then_inc(consts, 16)
                sync.dma_start(block_mask[:, :], d["block_mask"]).then_inc(consts, 16)
                sync.wait_ge(cleared, at(2))

                def load(tile, i):
                    for b in range(BATCH):
                        sync.dma_start(wq_rows[i][:, b, 0, :], vw_v[b, bass.ds(tile, 1), :, DIM:2 * DIM].rearrange("a p f -> (a p) f")).then_inc(rows_in[i], 16)
                        sync.dma_start(wq_rows[i][:, b, 1, :], qk_v[b, bass.ds(tile, 1), :, 0:DIM].rearrange("a p f -> (a p) f")).then_inc(rows_in[i], 16)
                        sync.dma_start(k_rows[i][:, b, :, :], qk_c[b, bass.ds(tile, 1), :, :, DIM:2 * DIM].rearrange("a t c f -> (a t) c f")).then_inc(rows_in[i], 16)
                        sync.dma_start(u_rows[i][0:CHUNK, b, :, :], vw_c[b, bass.ds(tile, 1), :, :, 0:DIM].rearrange("a t c f -> (a t) c f")).then_inc(rows_in[i], 16)

                def store(tile, i):
                    for b in range(BATCH):
                        sync.dma_start(u_c[b, bass.ds(tile, 1)].rearrange("a t c f -> (a t) c f"), solved[i][0:CHUNK, b, :, :]).then_inc(out_done[i], 16)
                        sync.dma_start(qs_c[b, bass.ds(tile, 1)].rearrange("a t c f -> (a t) c f"), solved[i][CHUNK:2 * CHUNK, b, :, :]).then_inc(out_done[i], 16)

                def tile_pair(ii, more):
                    for i in both:
                        tile = ii * 2 + i
                        for b in range(BATCH):
                            sync.wait_ge(state_written[b], at((tile + 1) * N))
                        if more:
                            load(tile + 2, i)
                        store(tile, i)

                for i in both:
                    load(i, i)
                with sync.Fori(0, PAIR - 1) as ii:
                    tile_pair(ii, more=True)
                tile_pair(PAIR - 1, more=False)
                for i in both:
                    sync.wait_ge(out_done[i], at(PAIR * BATCH * 32))

            @block.tensor
            def _(pe):
                pe.wait_ge(consts, at(32))

                def turn(tile, i, pair):
                    pe.wait_ge(rows_in[i], at((pair + 1) * LOADS))
                    pe.wait_ge(wq_ready, at(tile * BATCH))
                    for b in range(BATCH):
                        for a in range(2):
                            for k in range(HALVES):
                                mm = pe.transpose(turn_ps[b][:, a, k, :], wq_rows[i][:, b, a, k * P:(k + 1) * P], ident[:, :])
                        mm.then_inc(turned, 1)

                def tile_pair(ii, more):
                    for i in both:
                        tile = ii * 2 + i
                        pe.wait_ge(wq_ready, at((tile + 1) * BATCH))
                        for c in range(N):
                            for b in range(BATCH):
                                pe.wait_ge(state_ready[b], at(tile * N + c + 1))
                                for k in range(HALVES):
                                    mm = pe.matmul(read_ps[b][:, k * P:(k + 1) * P], wq[i][:, b, k, c, :], state[b][:, k, :], start=(k == 0), stop=(k == HALVES - 1), skip_group_check=True)
                                mm.then_inc(state_read[b], 1)
                            if c == TURN_AT and (more or i == 0):
                                turn(tile + 1, 1 - i, ii + i)
                            for b in range(BATCH):
                                pe.wait_ge(u_ready[b], at(tile * N + c + 1))
                                for k in range(HALVES):
                                    mm = pe.matmul(write_ps[b][:, k * P:(k + 1) * P], k_rows[i][:, b, c, k * P:(k + 1) * P], solved[i][0:CHUNK, b, c, k * P:(k + 1) * P], start=(k == 0), stop=(k == HALVES - 1), skip_group_check=True)
                                mm.then_inc(state_written[b], 1)

                turn(0, 0, 0)
                with pe.Fori(0, PAIR - 1) as ii:
                    tile_pair(ii, more=True)
                tile_pair(PAIR - 1, more=False)

            @block.scalar
            def _(act):
                def copy_turned(tile, i):
                    for b in range(BATCH):
                        act.wait_ge(turned, at(tile * BATCH + b + 1))
                        act.copy(wq[i][:, b, :, :, 0:CHUNK], turn_ps[b][:, 0, :, :].rearrange("p k (c t) -> p k c t", c=N))
                        act.copy(wq[i][:, b, :, :, CHUNK:2 * CHUNK], turn_ps[b][:, 1, :, :].rearrange("p k (c t) -> p k c t", c=N)).then_inc(wq_ready, 1)

                def tile_pair(ii, more):
                    for i in both:
                        tile = ii * 2 + i
                        act.wait_ge(gammas_ready, at((tile + 1) * BATCH))
                        for c in range(N):
                            for b in range(BATCH):
                                act.wait_ge(state_ready[b], at(tile * N + c + 1))
                                for k in range(HALVES):
                                    ins = act.activation(decayed[b][:, k, :], state[b][:, k, :], ACT.Copy, scale=gammas[i][:, b, k, c:c + 1])
                                ins.then_inc(decay_ready[b], 1)
                            if c == TURN_AT and (more or i == 0):
                                copy_turned(tile + 1, 1 - i)

                copy_turned(0, 0)
                with act.Fori(0, PAIR - 1) as ii:
                    tile_pair(ii, more=True)
                tile_pair(PAIR - 1, more=False)

            @block.vector
            def _(vec):
                for i in both:
                    vec.memset(u_rows[i][:, :, :, :], 0.0).then_inc(cleared, 1)
                for b in range(BATCH):
                    vec.memset(state[b][:, :, :], 0.0).then_inc(state_ready[b], 1)
                vec.wait_ge(consts, at(32))

                def take_gammas(tile, i, used):
                    for b in range(BATCH):
                        vec.wait_ge(decay_ready[b], at(used * N))
                        vec.tensor_copy(gammas[i][:, b, :, :], gamma_last[:, :, bass.ds(tile * N + b * (CHUNKS // BATCH), N)]).then_inc(gammas_ready, 1)

                def tile_pair(ii, more):
                    for i in both:
                        tile = ii * 2 + i
                        vec.wait_ge(rows_in[i], at((ii + 1) * LOADS))
                        vec.wait_ge(out_done[i], at(ii * (BATCH * 32)))
                        for c in range(N):
                            for b in range(BATCH):
                                vec.wait_ge(state_read[b], at(tile * N + c + 1))
                                vec.tensor_tensor(solved[i][:, b, c, :], u_rows[i][:, b, c, :], read_ps[b][:, 0:DIM], ALU.subtract).then_inc(u_ready[b], 1)
                            if c == TURN_AT and (more or i == 0):
                                take_gammas(tile + 1, 1 - i, tile)
                            for b in range(BATCH):
                                vec.wait_ge(state_written[b], at(tile * N + c + 1))
                                vec.tensor_tensor(update[b][:, :, :], write_ps[b][:, 0:DIM].rearrange("p (k f) -> p k f", k=HALVES),
                                                  block_mask[:, :].unsqueeze(1).broadcast_to([P, HALVES, P]), ALU.mult).then_inc(masked[b], 1)
                                vec.wait_ge(decay_ready[b], at(tile * N + c + 1))
                                vec.wait_ge(masked[b], at(tile * N + c + 1))
                                vec.tensor_tensor(state[b][:, :, :], update[b][:, :, :], decayed[b][:, :, :], ALU.add).then_inc(state_ready[b], 1)

                take_gammas(0, 0, 0)
                with vec.Fori(0, PAIR - 1) as ii:
                    tile_pair(ii, more=True)
                tile_pair(PAIR - 1, more=False)


def flat(tile):
    return tile.rearrange("p t f -> p (t f)")


def build_delta_outputs(nc, d):
    T = CHUNK
    VEC_STEPS = 36
    with ExitStack() as ctx:
        sb = lambda name, shape: ctx.enter_context(nc.sbuf_tensor("do_" + name, shape, F32))
        ps = lambda name, shape: ctx.enter_context(nc.psum_tensor("do_" + name, shape, F32))
        sem = Semaphores(nc, ctx, "do_")
        ident = sb("ident", [P, P])
        w_out = sb("w_out", [P, HALVES, DIM])
        rms_w = sb("rms_w", [P, HEAD])
        u = sb("u", [P, T, DIM])
        o = sb("o", [P, T, DIM])
        qkd = sb("qkd", [P, PAIRS])
        gate = sb("gate", [P, T, DIM])
        x = sb("x", [P, T, DIM])
        ga = sb("ga", [P, DIM])
        scratch = sb("scratch", [P, T * DIM])
        rms = sb("rms", [P, 2, T * HEADS])
        oT = [sb(f"oT{i}", [P, HALVES, P]) for i in range(2)]
        gated = [sb(f"gated{i}", [P, DIM]) for i in range(2)]
        tr_ps = [ps(f"tr_ps{i}", [P, 512]) for i in range(2)]
        y_ps = [ps(f"y_ps{i}", [P, 512]) for i in range(2)]
        consts, rows_in, order, gate_silu, gate_scaled, rms_ready, rms_rooted, o_ready = map(sem, (
            "consts", "rows_in", "order", "gate_silu", "gate_scaled", "rms_ready", "rms_rooted", "o_ready"))
        turned, oT_ready, projected, y_used, x_ready, x_out = map(sem, ("turned", "oT_ready", "projected", "y_used", "x_ready", "x_out"))

        sem.start()
        with nc.Block() as block:
            @block.sync
            def _(sync):
                sync.dma_start(ident[:, :], d["ident"]).then_inc(consts, 16)
                sync.dma_start(w_out[:, :, :], d["w_out"].rearrange("(k p) n -> p k n", p=P)).then_inc(consts, 16)
                sync.dma_start(rms_w[:, :], d["rms_w"].partition_broadcast(P)).then_inc(consts, 16)
                with sync.Fori(0, GROUPS) as g:
                    sync.wait_ge(x_out, at(g * 16))
                    sync.dma_start(flat(u[:, :, :]), chunk_rows(d["u"], g)).then_inc(rows_in, 16)
                    sync.dma_start(flat(o[:, :, :]), chunk_rows(d["qs"], g)).then_inc(rows_in, 16)
                    sync.dma_start(qkd[:, :], chunk_rows(d["qkd"], g)).then_inc(rows_in, 16)
                    sync.dma_start(flat(gate[:, :, :]), chunk_rows(d["gate"], g)).then_inc(rows_in, 16)
                    sync.dma_start(flat(x[:, :, :]), chunk_rows(d["x"], g)).then_inc(rows_in, 16)
                    sync.dma_start(ga[:, :], mod_row(d, 0, g, MOD_GA)).then_inc(rows_in, 16)
                    sync.wait_ge(x_ready, at((g + 1) * T))
                    sync.dma_start(chunk_rows(d["x1"], g), flat(x[:, :, :])).then_inc(x_out, 16)
                sync.wait_ge(x_out, at(GROUPS * 16))

            @block.scalar
            def _(act):
                with act.Fori(0, GROUPS) as g:
                    act.wait_ge(rows_in, at((g + 1) * 96))
                    act.activation(gate[:, :, :], gate[:, :, :], ACT.Silu).then_inc(gate_silu, 1)
                    act.wait_ge(rms_ready, at(g + 1))
                    act.activation(rms[:, 1, :], rms[:, 0, :], ACT.Sqrt).then_inc(rms_rooted, 1)
                    for j in range(T):
                        act.wait_ge(turned, at(g * T + j + 1))
                        act.wait_ge(projected, at(g * T + j - 1 if j >= 2 else g * T))
                        act.copy(flat(oT[j % 2][:, :, :]), tr_ps[j % 2][:, 0:2 * P]).then_inc(oT_ready, 1)

            @block.gpsimd
            def _(pool):
                pool.wait_ge(consts, at(48))
                with pool.Fori(0, GROUPS) as g:
                    pool.wait_ge(gate_silu, at(g + 1))
                    rows = gate[:, :, :].rearrange("p t (h e) -> p (t h) e", e=HEAD)
                    pool.tensor_tensor(rows, rows, rms_w[:, :].unsqueeze(1).broadcast_to([P, T * HEADS, HEAD]), ALU.mult).then_inc(gate_scaled, 1)

            @block.tensor
            def _(pe):
                pe.wait_ge(consts, at(48))
                with pe.Fori(0, GROUPS) as g:
                    pe.wait_ge(o_ready, at(g + 1))
                    for j in range(T + 1):
                        if j < T:
                            pe.wait_ge(oT_ready, at(g * T + j - 1 if j >= 2 else g * T))
                            for k in range(HALVES):
                                mm = pe.transpose(tr_ps[j % 2][:, k * P:(k + 1) * P], o[:, j, k * P:(k + 1) * P], ident[:, :])
                            mm.then_inc(turned, 1)
                        if j > 0:
                            i = j - 1
                            pe.wait_ge(oT_ready, at(g * T + i + 1))
                            pe.wait_ge(y_used, at(g * T + i - 1 if i >= 2 else g * T))
                            for k in range(HALVES):
                                mm = pe.matmul(y_ps[i % 2][:, 0:DIM], oT[i % 2][:, k, :], w_out[:, k, :], start=(k == 0), stop=(k == HALVES - 1))
                            mm.then_inc(projected, 1)

            @block.vector
            def _(vec):
                vec.wait_ge(consts, at(48))
                with vec.Fori(0, GROUPS) as g:
                    seq = Chain(vec, order, g * VEC_STEPS)
                    seq.wait()
                    vec.wait_ge(rows_in, at((g + 1) * 96))
                    heads4 = lambda ap, n: ap.rearrange("p t (h e) -> p t h e", h=HEADS)
                    sc = scratch[:, :].rearrange("p (t f) -> p t f", t=T)
                    for lag in range(T):
                        n = T - lag
                        m = view(qkd[:, :], [DIM + 1, n], [T, HEADS], [0, HEAD], offset=lag)
                        seq.wait()
                        seq.done(vec.tensor_tensor(heads4(sc[:, 0:n, :], n), heads4(u[:, 0:n, :], n), m, ALU.mult))
                        seq.wait()
                        seq.done(vec.tensor_tensor(o[:, lag:T, :], o[:, lag:T, :], sc[:, 0:n, :], ALU.add))
                    seq.wait()
                    seq.done(vec.tensor_tensor(sc, o[:, :, :], o[:, :, :], ALU.mult))
                    seq.wait()
                    seq.done(vec.tensor_reduce(rms[:, 0, :], scratch[:, :].rearrange("p (n e) -> p n e", e=HEAD), AX.X, ALU.add))
                    seq.wait()
                    seq.tell(vec.tensor_scalar(rms[:, 0, :], rms[:, 0, :], 1.0 / HEAD, 1e-6, ALU.mult, ALU.add), rms_ready, g + 1)
                    vec.wait_ge(rms_rooted, at(g + 1))
                    seq.done(vec.reciprocal(rms[:, 1, :], rms[:, 1, :]))
                    seq.wait()
                    seq.done(vec.tensor_tensor(heads4(o[:, :, :], T), heads4(o[:, :, :], T), spread(rms[:, 1, :].rearrange("p (t h) -> p t h", t=T), HEAD), ALU.mult))
                    seq.wait()
                    vec.wait_ge(gate_scaled, at(g + 1))
                    seq.tell(vec.tensor_tensor(o[:, :, :], o[:, :, :], gate[:, :, :], ALU.mult), o_ready, g + 1)
                    for j in range(T):
                        vec.wait_ge(projected, at(g * T + j + 1))
                        seq.tell(vec.tensor_tensor(gated[j % 2][:, :], y_ps[j % 2][:, 0:DIM], ga[:, :], ALU.mult), y_used, g * T + j + 1)
                        seq.wait()
                        vec.tensor_tensor(x[:, j, :], x[:, j, :], gated[j % 2][:, :], ALU.add).then_inc(x_ready, 1)
                    vec.wait_ge(x_ready, at((g + 1) * T))
                    assert seq.steps == VEC_STEPS, seq.steps


EXPERTS, TOP, HIDDEN = 32, 8, 1024
HC = HIDDEN // P


def build_token_choice(nc, d, merged, chosen):
    T = CHUNK
    VEC_STEPS = 41
    with ExitStack() as ctx:
        sb = lambda name, shape: ctx.enter_context(nc.sbuf_tensor("tc_" + name, shape, F32))
        ps = lambda name, shape: ctx.enter_context(nc.psum_tensor("tc_" + name, shape, F32))
        sem = Semaphores(nc, ctx, "tc_")
        ident = sb("ident", [P, P])
        gate_w = sb("gate_w", [P, HALVES, EXPERTS])
        gate_b = sb("gate_b", [EXPERTS, 1])
        h = sb("h", [P, GROUPS, T, DIM])
        mod = sb("mod", [P, 2, DIM])
        hm = sb("hm", [P, T, DIM])
        stats = sb("stats", [P, T, 6])
        moments = sb("moments", [P, 3, T])
        ss = sb("scale_shift", [P, 2, T])
        hT = [sb(f"hT{i}", [P, HALVES, P]) for i in range(2)]
        probs = sb("probs", [EXPERTS, BATCH, SEQ])
        stat = sb("stat", [EXPERTS, BATCH, 4])
        top = sb("top", [EXPERTS, BATCH, TOP])
        chosen_T = sb("chosen_T", [P, GROUPS * T, EXPERTS])
        tr_ps = [ps(f"tr_ps{i}", [P, 512]) for i in range(2)]
        lg_ps = [ps(f"lg_ps{i}", [EXPERTS, 512]) for i in range(2)]
        ch_ps = [ps(f"ch_ps{i}", [P, 512]) for i in range(2)]
        mg_ps = ps("mg_ps", [P, BATCH, HALVES, EXPERTS])
        consts, rows_in, order, var_ready, rooted, h_ready, turned, hT_ready = map(sem, (
            "consts", "rows_in", "order", "var_ready", "rooted", "h_ready", "turned", "hT_ready"))
        routed, logits_out, peak_ready, exp_done, chosen_ready, chosen_turned, chosen_copied, summed, merged_out = map(sem, (
            "routed", "logits_out", "peak_ready", "exp_done", "chosen_ready", "chosen_turned", "chosen_copied", "summed", "merged_out"))
        Q = 4

        sem.start()
        with nc.Block() as block:
            @block.sync
            def _(sync):
                sync.dma_start(ident[:, :], d["ident"]).then_inc(consts, 16)
                sync.dma_start(gate_w[:, :, :], d["gate0_wT"].rearrange("(k p) n -> p k n", p=P)).then_inc(consts, 16)
                sync.dma_start(gate_b[:, :], d["gate0_b"]).then_inc(consts, 16)
                with sync.Fori(0, GROUPS) as g:
                    sync.wait_ge(h_ready, at(g))
                    sync.wait_ge(turned, at(g * T))
                    sync.dma_start(flat(hm[:, :, :]), chunk_rows(d["x1"], g)).then_inc(rows_in, 16)
                    for n, m in enumerate((MOD_SB, MOD_CB)):
                        sync.dma_start(mod[:, n, :], mod_row(d, 0, g, m)).then_inc(rows_in, 16)

            @block.tensor
            def _(pe):
                pe.wait_ge(consts, at(48))
                with pe.Fori(0, GROUPS) as g:
                    pe.wait_ge(h_ready, at(g + 1))
                    for j in range(T + 1):
                        if j < T:
                            pe.wait_ge(hT_ready, at(g * T + j - 1 if j >= 2 else g * T))
                            for k in range(HALVES):
                                mm = pe.transpose(tr_ps[j % 2][:, k * P:(k + 1) * P], hm[:, j, k * P:(k + 1) * P], ident[:, :])
                            mm.then_inc(turned, 1)
                        if j > 0:
                            i = j - 1
                            bank, place = i // Q, i % Q
                            pe.wait_ge(hT_ready, at(g * T + i + 1))
                            if place == 0:
                                pe.wait_ge(logits_out, at(g * (T // Q) + bank - 1 if bank >= 2 else g * (T // Q)))
                            for k in range(HALVES):
                                mm = pe.matmul(lg_ps[bank % 2][:, place * P:(place + 1) * P], gate_w[:, k, :], hT[i % 2][:, k, :],
                                               start=(k == 0), stop=(k == HALVES - 1))
                            mm.then_inc(routed, 1)
                for b in range(BATCH):
                    pe.wait_ge(chosen_ready, at(b + 1))
                    for gg in range(GROUPS_PER_BATCH):
                        n = b * GROUPS_PER_BATCH + gg
                        if n >= 2:
                            pe.wait_ge(chosen_copied, at(n - 1))
                        for j in range(T):
                            mm = pe.transpose(ch_ps[n % 2][:, j * EXPERTS:(j + 1) * EXPERTS],
                                              chosen[:, b, gg * P * T + j:(gg + 1) * P * T:T], ident[0:EXPERTS, 0:EXPERTS])
                        mm.then_inc(chosen_turned, 1)
                for b in range(BATCH):
                    pe.wait_ge(chosen_copied, at((b + 1) * GROUPS_PER_BATCH))
                    for k in range(HALVES):
                        tiles = GROUPS_PER_BATCH * T
                        for n in range(tiles):
                            gg, j = b * GROUPS_PER_BATCH + n // T, n % T
                            mm = pe.matmul(mg_ps[:, b, k, :], h[:, gg, j, k * P:(k + 1) * P], chosen_T[:, gg * T + j, :],
                                           start=(n == 0), stop=(n == tiles - 1), skip_group_check=True)
                mm.then_inc(summed, 1)

            @block.scalar
            def _(act):
                act.wait_ge(consts, at(48))
                with act.Fori(0, GROUPS) as g:
                    act.wait_ge(var_ready, at(g + 1))
                    act.activation(ss[:, 1, :], ss[:, 0, :], ACT.Sqrt).then_inc(rooted, 1)
                    for j in range(T):
                        act.wait_ge(turned, at(g * T + j + 1))
                        act.wait_ge(routed, at(g * T + j - 1 if j >= 2 else g * T))
                        act.copy(flat(hT[j % 2][:, :, :]), tr_ps[j % 2][:, 0:2 * P]).then_inc(hT_ready, 1)
                        if j % Q == Q - 1:
                            bank = j // Q
                            act.wait_ge(routed, at(g * T + j + 1))
                            out = probs[:, :, :].rearrange("e b s -> e (b s)")[:, bass.ds(g * (P * T) + bank * Q, (P - 1) * T + Q)]
                            out = AP(out.tensor, out.offset, [list(out.ap[0]), [1, Q], [T, P]])
                            act.activation(out, lg_ps[bank % 2][:, :].rearrange("e (q p) -> e q p", q=Q), ACT.Identity, bias=gate_b[:, :]).then_inc(logits_out, 1)
                for b in range(BATCH):
                    act.wait_ge(peak_ready, at(b + 1))
                    act.activation(probs[:, b, :], probs[:, b, :], ACT.Exp, bias=stat[:, b, 0:1], accum_out=stat[:, b, 1:2]).then_inc(exp_done, 1)
                for n in range(GROUPS):
                    act.wait_ge(chosen_turned, at(n + 1))
                    act.copy(chosen_T[:, n * T:(n + 1) * T, :].rearrange("p t e -> p (t e)"), ch_ps[n % 2][:, :]).then_inc(chosen_copied, 1)
                act.wait_ge(summed, at(1))
                for b in range(BATCH):
                    for k in range(HALVES):
                        act.copy(merged[:, k, :, b], mg_ps[:, b, k, :]).then_inc(merged_out, 1)
                act.wait_ge(merged_out, at(BATCH * HALVES))

            @block.vector
            def _(vec):
                with vec.Fori(0, GROUPS) as g:
                    seq = Chain(vec, order, g * VEC_STEPS)
                    seq.wait()
                    vec.wait_ge(rows_in, at((g + 1) * 48))
                    layernorm_steps(vec, seq, hm[:, :, :], stats, moments, ss, T, rooted, g + 1, var_ready, g + 1)
                    seq.wait()
                    seq.done(vec.tensor_tensor(hm[:, :, :], hm[:, :, :], mod[:, 1:2, :].broadcast_to([P, T, DIM]), ALU.mult))
                    seq.wait()
                    seq.done(vec.tensor_tensor(hm[:, :, :], hm[:, :, :], mod[:, 0:1, :].broadcast_to([P, T, DIM]), ALU.add))
                    seq.wait()
                    seq.tell(vec.tensor_copy(h[:, bass.ds(g, 1), :, :].rearrange("p a t f -> p (a t f)"), flat(hm[:, :, :])), h_ready, g + 1)
                    assert seq.steps == VEC_STEPS, seq.steps
                vec.wait_ge(logits_out, at(GROUPS * T // Q))
                for b in range(BATCH):
                    last = vec.tensor_reduce(stat[:, b, 0:1], probs[:, b, :], AX.X, ALU.max, negate=True).then_inc(peak_ready, 1)
                seq = Chain(vec, order, GROUPS * VEC_STEPS)
                for b in range(BATCH):
                    vec.wait_ge(exp_done, at(b + 1))
                    seq.done(vec.reciprocal(stat[:, b, 2:3], stat[:, b, 1:2]))
                    seq.wait()
                    seq.done(vec.tensor_scalar(probs[:, b, :], probs[:, b, :], stat[:, b, 2:3], None, ALU.mult))
                    seq.wait()
                    seq.done(vec.max(top[:, b, :], probs[:, b, :]))
                    seq.wait()
                    seq.done(vec.match_replace(chosen[:, b, :], top[:, b, :], probs[:, b, :], 0.0))
                    seq.wait()
                    seq.tell(vec.tensor_tensor(chosen[:, b, :], probs[:, b, :], chosen[:, b, :], ALU.subtract), chosen_ready, b + 1)


def build_experts(nc, d, merged, expert_out):
    DEPTH = 4
    with ExitStack() as ctx:
        sb = lambda name, shape: ctx.enter_context(nc.sbuf_tensor("ex_" + name, shape, F32))
        ps = lambda name, shape: ctx.enter_context(nc.psum_tensor("ex_" + name, shape, F32))
        sem = Semaphores(nc, ctx, "ex_")
        ident = sb("ident", [P, P])
        w1 = [sb(f"w1_{i}", [P, HALVES, HIDDEN]) for i in range(DEPTH)]
        w2 = [sb(f"w2_{i}", [P, HC, DIM]) for i in range(DEPTH)]
        w1_bias = sb("w1_bias", [P, EXPERTS, HC])
        w2_bias = sb("w2_bias", [EXPERTS, DIM])
        hidden = [sb(f"hidden{i}", [P, HC, BATCH]) for i in range(2)]
        gelu = [sb(f"gelu{i}", [P, HC, BATCH]) for i in range(2)]
        outs = sb("outs", [P, HALVES, BATCH, EXPERTS])
        h_ps = [ps(f"h_ps{i}", [P, HC, BATCH]) for i in range(2)]
        o_ps = [ps(f"o_ps{i}", [P, HALVES, BATCH]) for i in range(2)]
        t_ps = [ps(f"t_ps{b}", [EXPERTS, DIM]) for b in range(BATCH)]
        consts, w1_done, h_ready, gelu_ready, w2_done, outs_ready, outs_turned, finished = map(sem, (
            "consts", "w1_done", "h_ready", "gelu_ready", "w2_done", "outs_ready", "outs_turned", "finished"))
        w1_in = [sem(f"w1_in{i}") for i in range(DEPTH)]
        w2_in = [sem(f"w2_in{i}") for i in range(DEPTH)]
        ROUNDS = EXPERTS // DEPTH

        sem.start()
        with nc.Block() as block:
            @block.sync
            def _(sync):
                sync.dma_start(ident[:, :], d["ident"]).then_inc(consts, 16)
                sync.dma_start(w1_bias[:, :, :], d["w1_bias"]).then_inc(consts, 16)
                sync.dma_start(w2_bias[:, :], d["w2_all"][:, HIDDEN, :]).then_inc(consts, 16)
                with sync.Fori(0, ROUNDS) as r:
                    for i in range(DEPTH):
                        e = r * DEPTH + i
                        sync.wait_ge(w1_done, at(r * DEPTH))
                        sync.dma_start(w1[i][:, :, :], d["w1_all"][bass.ds(e, 1), 0:DIM, :].rearrange("a (k p) n -> (a p) k n", p=P)).then_inc(w1_in[i], 16)
                        sync.wait_ge(w2_done, at(r * DEPTH))
                        sync.dma_start(w2[i][:, :, :], d["w2_all"][bass.ds(e, 1), 0:HIDDEN, :].rearrange("a (p c) n -> (a p) c n", p=P)).then_inc(w2_in[i], 16)

            @block.tensor
            def _(pe):
                pe.wait_ge(consts, at(48))
                with pe.Fori(0, ROUNDS) as r:
                    for i in range(DEPTH + 1):
                        if i < DEPTH:
                            e = r * DEPTH + i
                            pe.wait_ge(w1_in[i], at((r + 1) * 16))
                            pe.wait_ge(h_ready, at(r * DEPTH + i - 1 if i >= 2 else r * DEPTH))
                            for c in range(HC):
                                for k in range(HALVES):
                                    mm = pe.matmul(h_ps[i % 2][:, c, :], w1[i][:, k, c:HIDDEN:HC], merged[:, k, bass.ds(e, 1), :].rearrange("p a b -> p (a b)"),
                                                   start=(k == 0), stop=(k == HALVES - 1), skip_group_check=True)
                            mm.then_inc(w1_done, 1)
                        if i > 0:
                            n = i - 1
                            pe.wait_ge(w2_in[n], at((r + 1) * 16))
                            pe.wait_ge(gelu_ready, at(r * DEPTH + n + 1))
                            pe.wait_ge(outs_ready, at(r * DEPTH + n - 1 if n >= 2 else r * DEPTH))
                            for k in range(HALVES):
                                for c in range(HC):
                                    mm = pe.matmul(o_ps[n % 2][:, k, :], w2[n][:, c, k * P:(k + 1) * P], gelu[n % 2][:, c, :],
                                                   start=(c == 0), stop=(c == HC - 1), skip_group_check=True)
                            mm.then_inc(w2_done, 1)
                pe.wait_ge(outs_ready, at(EXPERTS))
                for b in range(BATCH):
                    for k in range(HALVES):
                        mm = pe.transpose(t_ps[b][:, k * P:(k + 1) * P], outs[:, k, b, :], ident[:, :])
                mm.then_inc(outs_turned, 1)

            @block.scalar
            def _(act):
                with act.Fori(0, ROUNDS) as r:
                    for i in range(DEPTH):
                        act.wait_ge(h_ready, at(r * DEPTH + i + 1))
                        act.wait_ge(w2_done, at(r * DEPTH + i - 1 if i >= 2 else r * DEPTH))
                        act.activation(gelu[i % 2][:, :, :], hidden[i % 2][:, :, :], ACT.Gelu).then_inc(gelu_ready, 1)

            @block.vector
            def _(vec):
                vec.wait_ge(consts, at(48))
                with vec.Fori(0, ROUNDS) as r:
                    for i in range(DEPTH + 1):
                        if i < DEPTH:
                            e = r * DEPTH + i
                            vec.wait_ge(w1_done, at(r * DEPTH + i + 1))
                            vec.wait_ge(gelu_ready, at(r * DEPTH + i - 1 if i >= 2 else r * DEPTH))
                            vec.tensor_tensor(hidden[i % 2][:, :, :], h_ps[i % 2][:, :, :],
                                              spread(w1_bias[:, bass.ds(e, 1), :].rearrange("p a c -> p (a c)"), BATCH), ALU.add).then_inc(h_ready, 1)
                        if i > 0:
                            n = i - 1
                            vec.wait_ge(w2_done, at(r * DEPTH + n + 1))
                            vec.tensor_copy(outs[:, :, :, bass.ds(r * DEPTH + n, 1)].rearrange("p k b a -> p k (b a)"), o_ps[n % 2][:, :, :]).then_inc(outs_ready, 1)
                vec.wait_ge(outs_turned, at(1))
                for b in range(BATCH):
                    vec.tensor_tensor(expert_out[:, b, :], t_ps[b][:, :], w2_bias[:, :], ALU.add).then_inc(finished, 1)
                vec.wait_ge(finished, at(BATCH))


def build_scatter(nc, d, chosen, expert_out):
    T = CHUNK
    with ExitStack() as ctx:
        sb = lambda name, shape: ctx.enter_context(nc.sbuf_tensor("sc_" + name, shape, F32))
        ps = lambda name, shape: ctx.enter_context(nc.psum_tensor("sc_" + name, shape, F32))
        sem = Semaphores(nc, ctx, "sc_")
        x = [sb(f"x{i}", [P, T, DIM]) for i in range(2)]
        gb = [sb(f"gb{i}", [P, DIM]) for i in range(2)]
        weights = [sb(f"weights{i}", [EXPERTS, P * T]) for i in range(2)]
        outs = [sb(f"outs{i}", [EXPERTS, DIM]) for i in range(2)]
        gated = [sb(f"gated{i}", [P, 2, DIM]) for i in range(2)]
        y_ps = [ps(f"y_ps{i}", [P, 2, DIM]) for i in range(2)]
        copied, summed, y_used, x_ready = map(sem, ("copied", "summed", "y_used", "x_ready"))
        rows_in = [sem(f"rows_in{i}") for i in range(2)]
        x_out = [sem(f"x_out{i}") for i in range(2)]
        PAIRS_OF_TILES = T // 2
        ROUNDS = GROUPS // 2

        sem.start()
        with nc.Block() as block:
            @block.sync
            def _(sync):
                with sync.Fori(0, ROUNDS) as r:
                    for i in range(2):
                        g = r * 2 + i
                        sync.wait_ge(x_out[i], at(r * 16))
                        sync.dma_start(flat(x[i][:, :, :]), chunk_rows(d["x1"], g)).then_inc(rows_in[i], 16)
                        sync.dma_start(gb[i][:, :], mod_row(d, 0, g, MOD_GB)).then_inc(rows_in[i], 16)
                    for i in range(2):
                        g = r * 2 + i
                        sync.wait_ge(x_ready, at((g + 1) * PAIRS_OF_TILES))
                        sync.dma_start(chunk_rows(d["x2"], g), flat(x[i][:, :, :])).then_inc(x_out[i], 16)
                for i in range(2):
                    sync.wait_ge(x_out[i], at(ROUNDS * 16))

            @block.scalar
            def _(act):
                with act.Fori(0, ROUNDS) as r:
                    for i in range(2):
                        g = r * 2 + i
                        act.wait_ge(summed, at(r * 2 * PAIRS_OF_TILES))
                        act.copy(weights[i][:, :], chosen[:, :, :].rearrange("e b s -> e (b s)")[:, bass.ds(g * (P * T), P * T)]).then_inc(copied, 1)
                        act.copy(outs[i][:, :], expert_out[:, bass.ds(r, 1), :].rearrange("e b f -> e (b f)")).then_inc(copied, 1)

            @block.tensor
            def _(pe):
                with pe.Fori(0, ROUNDS) as r:
                    for i in range(2):
                        g = r * 2 + i
                        pe.wait_ge(copied, at((g + 1) * 2))
                        for jj in range(PAIRS_OF_TILES):
                            n = g * PAIRS_OF_TILES + jj
                            pe.wait_ge(y_used, at(n - 1 if jj >= 2 else g * PAIRS_OF_TILES))
                            for s in range(2):
                                j = jj * 2 + s
                                mm = pe.matmul(y_ps[jj % 2][:, s, :], weights[i][:, j:P * T:T], outs[i][:, :], start=True, stop=True)
                            mm.then_inc(summed, 1)

            @block.vector
            def _(vec):
                with vec.Fori(0, ROUNDS) as r:
                    for i in range(2):
                        g = r * 2 + i
                        vec.wait_ge(rows_in[i], at((r + 1) * 32))
                        for jj in range(PAIRS_OF_TILES):
                            n = g * PAIRS_OF_TILES + jj
                            vec.wait_ge(summed, at(n + 1))
                            vec.tensor_tensor(gated[jj % 2][:, :, :], y_ps[jj % 2][:, :, :], gb[i][:, :].unsqueeze(1).broadcast_to([P, 2, DIM]), ALU.mult).then_inc(y_used, 1)
                            vec.wait_ge(y_used, at(n + 1))
                            vec.tensor_tensor(x[i][:, jj * 2:jj * 2 + 2, :], x[i][:, jj * 2:jj * 2 + 2, :], gated[jj % 2][:, :, :], ALU.add).then_inc(x_ready, 1)


WINDOW, TOPK, PHRASE = 64, 16, 32
SPAN = WINDOW + P
NT = 4
STEP = NT * P
STEPS = SEQ // STEP
NEG = -1e30
TAKEN = -3e38


def step_rows(dram, step):
    return dram.rearrange("(s n p) f -> s p n f", n=NT, p=P)[bass.ds(step, 1)].rearrange("a p n f -> (a p) n f")


def batch_mods(mods, b, n):
    return mods[:, bass.ds(b, 1), n, :]


def build_window_attention(nc, d):
    VEC_STEPS = 54
    WIDE = 8
    with ExitStack() as ctx:
        sb = lambda name, shape: ctx.enter_context(nc.sbuf_tensor("wa_" + name, shape, F32))
        ps = lambda name, shape: ctx.enter_context(nc.psum_tensor("wa_" + name, shape, F32))
        sem = Semaphores(nc, ctx, "wa_")
        ident = sb("ident", [P, P])
        ones = sb("ones", [P, 1])
        means = sb("means", [P, P])
        nears = sb("nears", [P, SPAN])
        w_cols = sb("w_cols", [P, 3, HALVES, DIM])
        w_rows = sb("w_rows", [P, 2, HALVES, DIM])
        col_bias = sb("col_bias", [P, 3, HALVES])
        row_bias = sb("row_bias", [P, 2 * DIM])
        band = sb("band", [P, STEPS, SPAN])
        keep = sb("keep", [P, STEPS])
        mods = sb("mods", [P, BATCH, 3, DIM])
        x = sb("x", [P, NT, DIM])
        h = sb("h", [P, NT, DIM])
        stats = sb("stats", [P, NT, 6])
        moments = sb("moments", [P, 3, NT])
        ss = sb("scale_shift", [P, 2, NT])
        hT = sb("hT", [P, HALVES, STEP])
        phT = sb("phT", [P, HALVES, 1 + STEP])
        qT = sb("qT", [P, HALVES, STEP])
        pT = sb("pT", [P, HALVES, STEP])
        kT = sb("kT", [P, HALVES, WINDOW + STEP])
        v = sb("v", [P, 1 + NT, 2 * DIM])
        scores = [sb(f"scores{i}", [P, SPAN]) for i in range(2)]
        rest = [sb(f"rest{i}", [P, 2, SPAN]) for i in range(2)]
        exps = [sb(f"exps{i}", [P, 2, SPAN]) for i in range(2)]
        probs = [sb(f"probs{i}", [P, 2 * P]) for i in range(2)]
        probs_T = [sb(f"probs_T{i}", [P, 2, P]) for i in range(2)]
        top = [sb(f"top{i}", [P, 2, 8]) for i in range(2)]
        one = [sb(f"one{i}", [P, 8]) for i in range(2)]
        out = [sb(f"out{i}", [P, DIM]) for i in range(2)]
        PH, MAX, WPH, SUM, INV = range(5)
        tr_ps = ps("tr_ps", [P, 512])
        wide_ps = [ps(f"wide_ps{i}", [P, 512]) for i in range(2)]
        vo_ps = [ps(f"vo_ps{i}", [P, 512]) for i in range(2)]
        sc_ps = [ps(f"sc_ps{i}", [P, 512]) for i in range(2)]
        pt_ps = ps("pt_ps", [P, 512])
        consts, cleared, x_in, x_out, order, var_ready, rooted, h_ready = map(sem, (
            "consts", "cleared", "x_in", "x_out", "order", "var_ready", "rooted", "h_ready"))
        turned, hT_ready, wide_done, wide_out, carried, vo_done, vo_used = map(sem, (
            "turned", "hT_ready", "wide_done", "wide_out", "carried", "vo_done", "vo_used"))
        products_ready, scored, sc_used, rest_ready, exp_done, near_done, probs_ready, probs_turned, probs_T_ready, x_ready = map(sem, (
            "products_ready", "scored", "sc_used", "rest_ready", "exp_done", "near_done", "probs_ready", "probs_turned", "probs_T_ready", "x_ready"))
        passed = sem("passed")
        CONSTS = 16 * (13 + 3 * BATCH)

        sem.start()
        with nc.Block() as block:
            @block.sync
            def _(sync):
                for tile, name in ((ident, "ident"), (ones, "ones"), (means, "means"), (nears, "nears"), (col_bias, "col_bias"),
                                   (band, "band"), (keep, "keep")):
                    sync.dma_start(tile[tuple([slice(None)] * len(tile.shape))], d[name]).then_inc(consts, 16)
                for n in range(3):
                    sync.dma_start(w_cols[:, n, :, :], d["w_cols"][n].rearrange("(k p) f -> p k f", p=P)).then_inc(consts, 16)
                for n in range(2):
                    sync.dma_start(w_rows[:, n, :, :], d["w_rows"][n].rearrange("(k p) f -> p k f", p=P)).then_inc(consts, 16)
                sync.dma_start(row_bias[:, :], d["row_bias"].partition_broadcast(P)).then_inc(consts, 16)
                for b in range(BATCH):
                    for n, m in enumerate((MOD_SA, MOD_CA, MOD_GA)):
                        sync.dma_start(mods[:, b, n, :], d["mod"][1, b * GROUPS_PER_BATCH, m * DIM:(m + 1) * DIM].partition_broadcast(P)).then_inc(consts, 16)
                with sync.Fori(0, BATCH * STEPS) as it:
                    sync.wait_ge(x_out, at(it * 16))
                    sync.dma_start(x[:, :, :], step_rows(d["x2"], it)).then_inc(x_in, 16)
                    sync.wait_ge(x_ready, at((it + 1) * NT))
                    sync.dma_start(step_rows(d["x3"], it), x[:, :, :]).then_inc(x_out, 16)
                sync.wait_ge(x_out, at(BATCH * STEPS * 16))

            @block.tensor
            def _(pe):
                pe.wait_ge(consts, at(CONSTS))
                pe.wait_ge(cleared, at(5))
                with pe.Fori(0, BATCH * STEPS) as it:
                    pe.wait_ge(h_ready, at(it + 1))
                    for n in range(NT // 2):
                        pe.wait_ge(hT_ready, at(it * (NT // 2) + n))
                        for k in range(HALVES):
                            for s in range(2):
                                mm = pe.transpose(tr_ps[:, (k * 2 + s) * P:(k * 2 + s + 1) * P], h[:, n * 2 + s, k * P:(k + 1) * P], ident[:, :])
                        mm.then_inc(turned, 1)

                    def wide(n):
                        pe.wait_ge(wide_out, at(it * WIDE + n - 1 if n >= 2 else it * WIDE))
                        bank = wide_ps[n % 2]
                        if n < 2:
                            for j in range(NT):
                                mm = pe.matmul(bank[:, j * P:(j + 1) * P], h[:, j, n * P:(n + 1) * P], means[:, :], start=True, stop=True)
                        else:
                            which, m = (n - 2) // 2, n % 2
                            if n == 2:
                                pe.wait_ge(hT_ready, at((it + 1) * (NT // 2)))
                            if n == 6:
                                pe.wait_ge(wide_out, at(it * WIDE + 2))
                            moving = phT if which == 2 else hT
                            for k in range(HALVES):
                                mm = pe.matmul(bank[:, :], w_cols[:, which, k, m * P:(m + 1) * P], moving[:, k, 0:STEP], start=(k == 0), stop=(k == HALVES - 1))
                        mm.then_inc(wide_done, 1)

                    for n in range(WIDE):
                        wide(n)
                    for j in range(NT):
                        pe.wait_ge(vo_used, at(it * 2 * NT + j - 1 if j >= 2 else it * 2 * NT))
                        for which, src in ((0, hT), (1, phT)):
                            for k in range(HALVES):
                                mm = pe.matmul(vo_ps[j % 2][:, which * DIM:(which + 1) * DIM], src[:, k, j * P:(j + 1) * P], w_rows[:, which, k, :],
                                               start=(k == 0), stop=(k == HALVES - 1))
                        mm.then_inc(vo_done, 1)
                    pe.wait_ge(wide_out, at((it + 1) * WIDE))

                    def score(j):
                        pe.wait_ge(sc_used, at(it * NT + j - 1 if j >= 2 else it * NT))
                        for k in range(HALVES):
                            pe.matmul(sc_ps[j % 2][:, 0:SPAN], qT[:, k, j * P:(j + 1) * P], kT[:, k, j * P:j * P + SPAN], start=(k == 0), stop=(k == HALVES - 1))
                        if j == 0:
                            pe.wait_ge(products_ready, at(it + 1))
                        for k in range(HALVES):
                            mm = pe.matmul(sc_ps[j % 2][:, SPAN:SPAN + 1], pT[:, k, j * P:(j + 1) * P], ones[:, :], start=(k == 0), stop=(k == HALVES - 1))
                        mm.then_inc(scored, 1)

                    score(0)
                    score(1)
                    for j in range(NT):
                        pe.wait_ge(probs_ready, at(it * NT + j + 1))
                        pe.wait_ge(probs_T_ready, at(it * NT + j))
                        for c in range(2):
                            mm = pe.transpose(pt_ps[:, c * P:(c + 1) * P], probs[j % 2][:, c * P:(c + 1) * P], ident[:, :])
                        mm.then_inc(probs_turned, 1)
                        if j + 2 < NT:
                            score(j + 2)
                        pe.wait_ge(vo_used, at(it * 2 * NT + NT + j - 1))
                        if j == 0:
                            pe.wait_ge(vo_used, at(it * 2 * NT + NT))
                        pe.wait_ge(probs_T_ready, at(it * NT + j + 1))
                        for c in range(2):
                            mm = pe.matmul(vo_ps[j % 2][:, 0:DIM], probs_T[j % 2][:, c, :], v[:, j + c, 0:DIM], start=(c == 0), stop=(c == 1))
                        mm.then_inc(vo_done, 1)

            @block.scalar
            def _(act):
                act.wait_ge(consts, at(CONSTS))
                act.wait_ge(cleared, at(5))
                with act.Fori(0, BATCH * STEPS) as it:
                    act.wait_ge(var_ready, at(it + 1))
                    act.activation(ss[:, 1, :], ss[:, 0, :], ACT.Sqrt).then_inc(rooted, 1)
                    for n in range(NT // 2):
                        act.wait_ge(turned, at(it * (NT // 2) + n + 1))
                        act.copy(hT[:, :, n * 2 * P:(n + 1) * 2 * P], tr_ps[:, :].rearrange("p (k t) -> p k t", k=HALVES)).then_inc(hT_ready, 1)
                    act.copy(phT[:, :, 0:1], phT[:, :, STEP:STEP + 1]).then_inc(carried, 1)
                    act.copy(kT[:, :, 0:WINDOW], kT[:, :, STEP:STEP + WINDOW]).then_inc(carried, 1)
                    act.wait_ge(carried, at((it + 1) * 2))
                    for n in range(WIDE):
                        act.wait_ge(wide_done, at(it * WIDE + n + 1))
                        m = n % 2
                        if n < 2:
                            ins = act.copy(phT[:, m, 1:1 + STEP], wide_ps[m][:, :])
                        else:
                            which = (n - 2) // 2
                            to = (qT[:, m, :], kT[:, m, WINDOW:WINDOW + STEP], pT[:, m, :])[which]
                            ins = act.activation(to, wide_ps[m][:, :], ACT.Identity, bias=col_bias[:, which, m:m + 1])
                        ins.then_inc(wide_out, 1)
                    for j in range(NT):
                        act.wait_ge(rest_ready, at(it * NT + j + 1))
                        act.activation(exps[j % 2][:, 0, :], scores[j % 2][:, :], ACT.Exp, bias=one[j % 2][:, MAX:MAX + 1])
                        act.activation(exps[j % 2][:, 1, :], rest[j % 2][:, 1, :], ACT.Exp, bias=one[j % 2][:, MAX:MAX + 1])
                        act.activation(one[j % 2][:, WPH:WPH + 1], one[j % 2][:, PH:PH + 1], ACT.Exp, bias=one[j % 2][:, MAX:MAX + 1]).then_inc(exp_done, 1)
                        act.wait_ge(probs_turned, at(it * NT + j + 1))
                        act.copy(probs_T[j % 2][:, :, :].rearrange("p c q -> p (c q)"), pt_ps[:, 0:2 * P]).then_inc(probs_T_ready, 1)

            @block.gpsimd
            def _(pool):
                pool.wait_ge(consts, at(CONSTS))
                with pool.Fori(0, BATCH * STEPS) as it:
                    pool.wait_ge(wide_out, at((it + 1) * WIDE))
                    pool.tensor_tensor(pT[:, :, :], qT[:, :, :], pT[:, :, :], ALU.mult).then_inc(products_ready, 1)
                    for j in range(NT):
                        pool.wait_ge(exp_done, at(it * NT + j + 1))
                        pool.tensor_tensor(exps[j % 2][:, 0, :], exps[j % 2][:, 0, :], nears[:, :], ALU.mult).then_inc(near_done, 1)

            @block.vector
            def _(vec):
                for z in (probs[0][:, :], probs[1][:, :], v[:, :, :], phT[:, :, :], kT[:, :, :]):
                    vec.memset(z, 0.0).then_inc(cleared, 1)
                vec.wait_ge(cleared, at(5))
                vec.wait_ge(consts, at(CONSTS))
                with vec.Fori(0, BATCH) as b:
                    with vec.Fori(0, STEPS) as s:
                        it = b * STEPS + s
                        seq = Chain(vec, order, it * VEC_STEPS)
                        seq.wait()
                        vec.wait_ge(x_in, at((it + 1) * 16))
                        layernorm_steps(vec, seq, x[:, :, :], stats, moments, ss, NT, rooted, it + 1, var_ready, it + 1, out=h[:, :, :])
                        seq.wait()
                        seq.done(vec.tensor_tensor(h[:, :, :], h[:, :, :], batch_mods(mods, b, 1).broadcast_to([P, NT, DIM]), ALU.mult))
                        seq.wait()
                        seq.tell(vec.tensor_tensor(h[:, :, :], h[:, :, :], batch_mods(mods, b, 0).broadcast_to([P, NT, DIM]), ALU.add), h_ready, it + 1)
                        seq.wait()
                        seq.done(vec.tensor_copy(v[:, 0, 0:DIM], v[:, NT, 0:DIM]))
                        seq.wait()
                        for j in range(NT):
                            vec.wait_ge(vo_done, at(it * 2 * NT + j + 1))
                            seq.tell(vec.tensor_tensor(v[:, 1 + j, :], vo_ps[j % 2][:, :], row_bias[:, :], ALU.add), vo_used, it * 2 * NT + j + 1)

                        def choose(j):
                            i = j % 2
                            mask = band[:, bass.ds(s, 1), :].rearrange("p a c -> p (a c)") if j == 0 else band[:, 1, :]
                            vec.wait_ge(scored, at(it * NT + j + 1))
                            seq.done(vec.scalar_tensor_tensor(scores[i][:, :], sc_ps[i][:, 0:SPAN], DIM ** -0.5, mask, ALU.mult, ALU.add))
                            seq.tell(vec.tensor_scalar(one[i][:, PH:PH + 1], sc_ps[i][:, SPAN:SPAN + 1], DIM ** -0.5, None, ALU.mult), sc_used, it * NT + j + 1)
                            seq.wait()
                            vec.sem_inc(passed, 1)
                            seq.done(vec.max(top[i][:, 0, :], scores[i][:, :]))
                            seq.wait()
                            vec.sem_inc(passed, 1)
                            seq.done(vec.match_replace(rest[i][:, 0, :], top[i][:, 0, :], scores[i][:, :], TAKEN))
                            seq.wait()
                            vec.sem_inc(passed, 1)
                            seq.done(vec.max(top[i][:, 1, :], rest[i][:, 0, :]))
                            seq.done(vec.tensor_tensor(one[i][:, MAX:MAX + 1], one[i][:, PH:PH + 1], top[i][:, 0, 0:1], ALU.max))
                            seq.wait()
                            seq.done(vec.tensor_scalar(one[i][:, MAX:MAX + 1], one[i][:, MAX:MAX + 1], -1.0, None, ALU.mult))
                            seq.wait()
                            vec.sem_inc(passed, 1)
                            seq.tell(vec.match_replace(rest[i][:, 1, :], top[i][:, 1, :], rest[i][:, 0, :], TAKEN), rest_ready, it * NT + j + 1)

                        def weigh(j):
                            i = j % 2
                            vec.wait_ge(near_done, at(it * NT + j + 1))
                            vec.wait_ge(probs_turned, at(it * NT + j - 1 if j >= 2 else it * NT))
                            seq.tell(vec.scalar_tensor_tensor(probs[i][:, 2 * P - SPAN:], exps[i][:, 0, :], 1.0, exps[i][:, 1, :], ALU.mult, ALU.subtract,
                                                                accum_out=one[i][:, SUM:SUM + 1]), probs_ready, it * NT + j + 1)
                            seq.wait()
                            seq.done(vec.tensor_tensor(one[i][:, INV:INV + 1], one[i][:, SUM:SUM + 1], one[i][:, WPH:WPH + 1], ALU.add))
                            seq.wait()
                            seq.done(vec.reciprocal(one[i][:, INV:INV + 1], one[i][:, INV:INV + 1]))
                            if j == 0:
                                seq.wait()
                                seq.done(vec.tensor_tensor(one[i][:, INV:INV + 1], one[i][:, INV:INV + 1], keep[:, bass.ds(s, 1)], ALU.mult))

                        def finish(j):
                            i = j % 2
                            vec.wait_ge(vo_done, at(it * 2 * NT + NT + j + 1))
                            seq.tell(vec.scalar_tensor_tensor(out[i][:, :], v[:, 1 + j, DIM:2 * DIM], one[i][:, WPH:WPH + 1], vo_ps[i][:, 0:DIM],
                                                                ALU.mult, ALU.add), vo_used, it * 2 * NT + NT + j + 1)
                            seq.wait()
                            seq.done(vec.scalar_tensor_tensor(out[i][:, :], out[i][:, :], one[i][:, INV:INV + 1], batch_mods(mods, b, 2).rearrange("p a f -> p (a f)"),
                                                              ALU.mult, ALU.mult))
                            seq.wait()
                            seq.tell(vec.tensor_tensor(x[:, j, :], x[:, j, :], out[i][:, :], ALU.add), x_ready, it * NT + j + 1)

                        choose(0)
                        for j in range(NT):
                            if j + 1 < NT:
                                choose(j + 1)
                            weigh(j)
                            finish(j)
                        assert seq.steps == VEC_STEPS, seq.steps


FFN_EXPERTS, ALL_EXPERTS, DFF = 8, 12, 512
FC = DFF // P
TILES = TOKENS // P
ALL_STEPS = BATCH * STEPS
PICKS = 2
SLOT_TILES = PICKS * TILES + FFN_EXPERTS
SLOTS = SLOT_TILES * P
NO_SLOT = float(1 << 20)
INT = mybir.dt.uint32


def slot_rows(dram, tile):
    return dram.rearrange("(n p) f -> n p f", p=P)[bass.ds(tile, 1)].rearrange("a p f -> (a p) f")


def build_routing(nc, d, route):
    VEC_STEPS = 39
    picked, shares, pass_w = route["picked"], route["shares"], route["pass_w"]
    with ExitStack() as ctx:
        sb = lambda name, shape, dt=F32: ctx.enter_context(nc.sbuf_tensor("rt_" + name, shape, dt))
        ps = lambda name, shape: ctx.enter_context(nc.psum_tensor("rt_" + name, shape, F32))
        sem = Semaphores(nc, ctx, "rt_")
        ident = sb("ident", [P, P])
        zeros = sb("zeros", [P, 17 * DIM])
        gate_w = sb("gate_w", [P, HALVES, ALL_EXPERTS])
        gate_b = sb("gate_b", [P, ALL_EXPERTS])
        numbers = sb("numbers", [P, ALL_EXPERTS])
        mods = sb("mods", [P, BATCH, 2, DIM])
        x = sb("x", [P, NT, DIM])
        h = sb("h", [P, NT, DIM])
        stats = sb("stats", [P, NT, 6])
        moments = sb("moments", [P, 3, NT])
        ss = sb("scale_shift", [P, 2, NT])
        hT = sb("hT", [P, HALVES, STEP])
        logits = sb("logits", [P, NT, ALL_EXPERTS])
        best = sb("best", [P, NT, 8])
        best_at = sb("best_at", [P, NT, 8], INT)
        best_n = sb("best_n", [P, NT, 8])
        pair = sb("pair", [P, 2, NT])
        gap = sb("gap", [P, 2, NT])
        hot = sb("hot", [P, PICKS, NT, ALL_EXPERTS])
        weighted = sb("weighted", [P, PICKS, NT, ALL_EXPERTS])
        tr_ps = ps("tr_ps", [P, 512])
        lg_ps = ps("lg_ps", [P, NT, ALL_EXPERTS])
        consts, x_in, h_out, order, var_ready, rooted, h_ready, passed = map(sem, (
            "consts", "x_in", "h_out", "order", "var_ready", "rooted", "h_ready", "passed"))
        turned, hT_ready, routed, gap_ready, gap_exp, cleared, zeroed = map(sem, (
            "turned", "hT_ready", "routed", "gap_ready", "gap_exp", "cleared", "zeroed"))
        CONSTS = 16 * (4 + 2 * BATCH)
        ZERO_ROWS = P * 17

        sem.start()
        with nc.Block() as block:
            @block.sync
            def _(sync):
                sync.dma_start(ident[:, :], d["ident"]).then_inc(consts, 16)
                sync.dma_start(gate_w[:, :, :], d["gate1_wT"].rearrange("(k p) f -> p k f", p=P)).then_inc(consts, 16)
                sync.dma_start(gate_b[:, :], d["gate1_b"].partition_broadcast(P)).then_inc(consts, 16)
                sync.dma_start(numbers[:, :], d["numbers"]).then_inc(consts, 16)
                for b in range(BATCH):
                    for n, m in enumerate((MOD_SB, MOD_CB)):
                        sync.dma_start(mods[:, b, n, :], d["mod"][1, b * GROUPS_PER_BATCH, m * DIM:(m + 1) * DIM].partition_broadcast(P)).then_inc(consts, 16)
                sync.wait_ge(cleared, at(1))
                with sync.Fori(0, ALL_STEPS) as it:
                    sync.wait_ge(h_ready, at(it))
                    sync.dma_start(x[:, :, :], step_rows(d["x3"], it)).then_inc(x_in, 16)
                    sync.wait_ge(h_ready, at(it + 1))
                    sync.dma_start(step_rows(d["h3"], it), h[:, :, :]).then_inc(h_out, 16)
                for n in range(SLOTS // ZERO_ROWS):
                    sync.dma_start(d["xs"][n * ZERO_ROWS:(n + 1) * ZERO_ROWS, :].rearrange("(p t) f -> p (t f)", p=P), zeros[:, :]).then_inc(zeroed, 16)
                sync.wait_ge(h_out, at(ALL_STEPS * 16))
                sync.wait_ge(zeroed, at(SLOTS // ZERO_ROWS * 16))

            @block.tensor
            def _(pe):
                pe.wait_ge(consts, at(CONSTS))
                with pe.Fori(0, ALL_STEPS) as it:
                    pe.wait_ge(h_ready, at(it + 1))
                    for n in range(NT // 2):
                        pe.wait_ge(hT_ready, at(it * (NT // 2) + n))
                        for k in range(HALVES):
                            for s in range(2):
                                mm = pe.transpose(tr_ps[:, (k * 2 + s) * P:(k * 2 + s + 1) * P], h[:, n * 2 + s, k * P:(k + 1) * P], ident[:, :])
                        mm.then_inc(turned, 1)
                    pe.wait_ge(hT_ready, at((it + 1) * (NT // 2)))
                    for j in range(NT):
                        for k in range(HALVES):
                            mm = pe.matmul(lg_ps[:, j, :], hT[:, k, j * P:(j + 1) * P], gate_w[:, k, :], start=(k == 0), stop=(k == HALVES - 1), skip_group_check=True)
                    mm.then_inc(routed, 1)

            @block.scalar
            def _(act):
                with act.Fori(0, ALL_STEPS) as it:
                    act.wait_ge(var_ready, at(it + 1))
                    act.activation(ss[:, 1, :], ss[:, 0, :], ACT.Sqrt).then_inc(rooted, 1)
                    for n in range(NT // 2):
                        act.wait_ge(turned, at(it * (NT // 2) + n + 1))
                        act.copy(hT[:, :, n * 2 * P:(n + 1) * 2 * P], tr_ps[:, :].rearrange("p (k t) -> p k t", k=HALVES)).then_inc(hT_ready, 1)
                    act.wait_ge(gap_ready, at(it + 1))
                    act.activation(gap[:, 1, :], gap[:, 0, :], ACT.Exp).then_inc(gap_exp, 1)

            @block.gpsimd
            def _(pool):
                pool.memset(zeros[:, :], 0.0).then_inc(cleared, 1)

            @block.vector
            def _(vec):
                vec.wait_ge(consts, at(CONSTS))
                with vec.Fori(0, BATCH) as b:
                    with vec.Fori(0, STEPS) as s:
                        it = b * STEPS + s
                        tiles = bass.ds(it * NT, NT)
                        seq = Chain(vec, order, it * VEC_STEPS)
                        seq.wait()
                        vec.wait_ge(h_out, at(it * 16))
                        vec.wait_ge(x_in, at((it + 1) * 16))
                        layernorm_steps(vec, seq, x[:, :, :], stats, moments, ss, NT, rooted, it + 1, var_ready, it + 1, out=h[:, :, :])
                        seq.wait()
                        seq.done(vec.tensor_tensor(h[:, :, :], h[:, :, :], batch_mods(mods, b, 1).broadcast_to([P, NT, DIM]), ALU.mult))
                        seq.wait()
                        seq.tell(vec.tensor_tensor(h[:, :, :], h[:, :, :], batch_mods(mods, b, 0).broadcast_to([P, NT, DIM]), ALU.add), h_ready, it + 1)
                        vec.wait_ge(routed, at(it + 1))
                        seq.done(vec.tensor_tensor(logits[:, :, :], lg_ps[:, :, :], gate_b[:, :].unsqueeze(1).broadcast_to([P, NT, ALL_EXPERTS]), ALU.add))
                        seq.wait()
                        vec.sem_inc(passed, 1)
                        for j in range(NT):
                            seq.done(vec.max(best[:, j, :], logits[:, j, :]))
                        seq.wait()
                        vec.sem_inc(passed, 1)
                        for j in range(NT):
                            seq.done(vec.max_index(best_at[:, j, :], best[:, j, :], logits[:, j, :]))
                        seq.wait()
                        seq.done(vec.tensor_copy(best_n[:, :, :], best_at[:, :, :]))
                        seq.tell(vec.tensor_tensor(gap[:, 0, :], best[:, :, 1], best[:, :, 0], ALU.subtract), gap_ready, it + 1)
                        seq.wait()
                        for n in range(PICKS):
                            seq.done(vec.tensor_tensor(hot[:, n, :, :], numbers[:, :].unsqueeze(1).broadcast_to([P, NT, ALL_EXPERTS]),
                                                       spread(best_n[:, :, n], ALL_EXPERTS), ALU.is_equal))
                        vec.wait_ge(gap_exp, at(it + 1))
                        seq.done(vec.tensor_scalar(pair[:, 0, :], gap[:, 1, :], 1.0, None, ALU.add))
                        seq.wait()
                        seq.done(vec.reciprocal(pair[:, 0, :], pair[:, 0, :]))
                        seq.wait()
                        seq.done(vec.tensor_tensor(pair[:, 1, :], pair[:, 0, :], gap[:, 1, :], ALU.mult))
                        seq.wait()
                        for n in range(PICKS):
                            seq.done(vec.tensor_copy(picked[:, n, tiles, :], hot[:, n, :, 0:FFN_EXPERTS]))
                            seq.done(vec.tensor_tensor(weighted[:, n, :, :], hot[:, n, :, :], spread(pair[:, n, :], ALL_EXPERTS), ALU.mult))
                        seq.wait()
                        for n in range(PICKS):
                            seq.done(vec.tensor_reduce(shares[:, n, tiles], weighted[:, n, :, 0:FFN_EXPERTS], AX.X, ALU.add))
                        seq.wait()
                        seq.done(vec.tensor_tensor(weighted[:, 0, :, :], weighted[:, 0, :, :], weighted[:, 1, :, :], ALU.add))
                        seq.wait()
                        seq.done(vec.tensor_reduce(pass_w[:, tiles], weighted[:, 0, :, FFN_EXPERTS:], AX.X, ALU.add))
                        assert seq.steps == VEC_STEPS, seq.steps


def build_slots(nc, d, route):
    E = FFN_EXPERTS
    picked, slots, tile_expert = route["picked"], route["slots"], route["tile_expert"]
    with ExitStack() as ctx:
        sb = lambda name, shape, dt=F32: ctx.enter_context(nc.sbuf_tensor("sl_" + name, shape, dt))
        ps = lambda name, shape: ctx.enter_context(nc.psum_tensor("sl_" + name, shape, F32))
        sem = Semaphores(nc, ctx, "sl_")
        before = sb("before", [P, P])
        ones = sb("ones", [P, P])
        tile_starts = sb("tile_starts", [P, TILES])
        slot_tiles = sb("slot_tiles", [P, SLOT_TILES])
        either = sb("either", [P, TILES, E])
        running = [sb(f"running{i}", [P, TILES, E]) for i in range(2)]
        wider = sb("wider", [P, E, TILES])
        tiles_of = [sb(f"tiles_of{i}", [P, E]) for i in range(3)]
        place = sb("place", [P, TILES, E])
        mine = sb("mine", [P, TILES, E])
        slot_f = sb("slot_f", [P, PICKS, TILES])
        has = sb("has", [P, PICKS, TILES])
        passed_ends = sb("passed_ends", [P, SLOT_TILES, E - 1])
        expert_f = sb("expert_f", [P, SLOT_TILES])
        rank_ps = ps("rank_ps", [P, TILES, E])
        total_ps = ps("total_ps", [P, TILES, E])
        consts, order, either_ready, counted = map(sem, ("consts", "order", "either_ready", "counted"))
        sem.start()
        with nc.Block() as block:
            @block.sync
            def _(sync):
                sync.dma_start(before[:, :], d["before"]).then_inc(consts, 16)
                sync.dma_start(ones[:, :], d["ones_square"]).then_inc(consts, 16)
                sync.dma_start(tile_starts[:, :], d["tile_starts"]).then_inc(consts, 16)
                sync.dma_start(slot_tiles[:, :], d["slot_tiles"]).then_inc(consts, 16)

            @block.tensor
            def _(pe):
                pe.wait_ge(consts, at(64))
                pe.wait_ge(either_ready, at(1))
                pe.matmul(rank_ps[:, :, :], before[:, :], either[:, :, :], start=True, stop=True)
                pe.matmul(total_ps[:, :, :], ones[:, :], either[:, :, :], start=True, stop=True).then_inc(counted, 1)

            @block.vector
            def _(vec):
                seq = Chain(vec, order)
                vec.wait_ge(consts, at(64))
                seq.tell(vec.tensor_tensor(either[:, :, :], picked[:, 0, :, :], picked[:, 1, :, :], ALU.add), either_ready, 1)
                vec.wait_ge(counted, at(1))
                seq.done(vec.tensor_copy(running[0][:, :, :], total_ps[:, :, :]))
                reach, n = 1, 0
                while reach < TILES:
                    seq.wait()
                    a, b = running[n % 2], running[(n + 1) % 2]
                    seq.done(vec.tensor_copy(b[:, 0:reach, :], a[:, 0:reach, :]))
                    seq.done(vec.tensor_tensor(b[:, reach:, :], a[:, reach:, :], a[:, 0:TILES - reach, :], ALU.add))
                    reach, n = reach * 2, n + 1
                run = running[n % 2]
                seq.wait()
                seq.done(vec.tensor_tensor(wider[:, :, :], spread(run[:, TILES - 1, :], TILES), tile_starts[:, :].unsqueeze(1).broadcast_to([P, E, TILES]), ALU.is_gt))
                seq.wait()
                seq.done(vec.tensor_reduce(tiles_of[0][:, :], wider[:, :, :], AX.X, ALU.add))
                reach, m = 1, 0
                while reach < E:
                    seq.wait()
                    a, b = tiles_of[m % 2], tiles_of[(m + 1) % 2]
                    if m == 0:
                        seq.done(vec.tensor_copy(tiles_of[2][:, :], a[:, :]))
                    seq.done(vec.tensor_copy(b[:, 0:reach], a[:, 0:reach]))
                    seq.done(vec.tensor_tensor(b[:, reach:], a[:, reach:], a[:, 0:E - reach], ALU.add))
                    reach, m = reach * 2, m + 1
                ends = tiles_of[m % 2]
                first = tiles_of[2]
                seq.wait()
                seq.done(vec.tensor_tensor(first[:, :], ends[:, :], first[:, :], ALU.subtract))
                seq.wait()
                seq.done(vec.tensor_scalar(first[:, :], first[:, :], float(P), None, ALU.mult))
                seq.done(vec.tensor_tensor(place[:, :, :], run[:, :, :], total_ps[:, :, :], ALU.subtract))
                seq.wait()
                seq.done(vec.tensor_tensor(place[:, :, :], place[:, :, :], rank_ps[:, :, :], ALU.add))
                seq.wait()
                seq.done(vec.tensor_tensor(place[:, :, :], place[:, :, :], first[:, :].unsqueeze(1).broadcast_to([P, TILES, E]), ALU.add))
                for k in range(PICKS):
                    seq.wait()
                    seq.done(vec.tensor_tensor(mine[:, :, :], place[:, :, :], picked[:, k, :, :], ALU.mult))
                    seq.wait()
                    seq.done(vec.tensor_reduce(slot_f[:, k, :], mine[:, :, :], AX.X, ALU.add))
                    seq.done(vec.tensor_reduce(has[:, k, :], picked[:, k, :, :], AX.X, ALU.add))
                seq.wait()
                seq.done(vec.tensor_scalar(has[:, :, :], has[:, :, :], -NO_SLOT, NO_SLOT, ALU.mult, ALU.add))
                seq.wait()
                seq.done(vec.tensor_tensor(slot_f[:, :, :], slot_f[:, :, :], has[:, :, :], ALU.add))
                seq.wait()
                seq.done(vec.tensor_copy(slots[:, :, :], slot_f[:, :, :]))
                seq.done(vec.tensor_tensor(passed_ends[:, :, :], spread(slot_tiles[:, :], E - 1), ends[:, 0:E - 1].unsqueeze(1).broadcast_to([P, SLOT_TILES, E - 1]), ALU.is_ge))
                seq.wait()
                seq.done(vec.tensor_reduce(expert_f[:, :], passed_ends[:, :, :], AX.X, ALU.add))
                seq.wait()
                seq.done(vec.tensor_copy(tile_expert[:, :], expert_f[0:1, :]))
                seq.wait()


def build_dispatch(nc, d, route):
    slots = route["slots"]
    with ExitStack() as ctx:
        sb = lambda name, shape, dt=F32: ctx.enter_context(nc.sbuf_tensor("dp_" + name, shape, dt))
        sem = Semaphores(nc, ctx, "dp_")
        h = [sb(f"h{i}", [P, NT, DIM]) for i in range(2)]
        to = [[sb(f"to{i}_{n}", [P, 1], INT) for n in range(NT * PICKS)] for i in range(2)]
        h_in = [sem(f"h_in{i}") for i in range(2)]
        sent = [sem.from_zero(f"sent{i}") for i in range(2)]
        gone = [sem(f"gone{i}") for i in range(2)]
        to_ready, passed = sem("to_ready"), sem("passed")
        ROUNDS = ALL_STEPS // 2
        sem.start()
        with nc.Block() as block:
            @block.sync
            def _(sync):
                with sync.Fori(0, ROUNDS) as r:
                    for i in range(2):
                        sync.wait_ge(gone[i], at(r))
                        sync.dma_start(h[i][:, :, :], step_rows(d["h3"], r * 2 + i)).then_inc(h_in[i], 16)

            @block.vector
            def _(vec):
                with vec.Fori(0, ROUNDS) as r:
                    for i in range(2):
                        vec.wait_ge(gone[i], at(r))
                        for k in range(PICKS):
                            for j in range(NT):
                                vec.tensor_copy(to[i][k * NT + j][:, :], slots[:, k, bass.ds((r * 2 + i) * NT + j, 1)]).then_inc(to_ready, 1)

            @block.gpsimd
            def _(pool):
                with pool.Fori(0, ROUNDS) as r:
                    for i in range(2):
                        pool.wait_ge(h_in[i], at((r + 1) * 16))
                        pool.wait_ge(to_ready, at((r * 2 + i + 1) * (NT * PICKS)))
                        pool.sem_inc(passed, 1)
                        for k in range(PICKS):
                            for j in range(NT):
                                pool.indirect_dma_start(d["xs"], bass.IndirectOffsetOnAxis(ap=to[i][k * NT + j][:, :], axis=0), h[i][:, j, :], None,
                                                        bounds_check=SLOTS - 1, oob_is_err=False).then_inc(sent[i], 16)
                    for i in range(2):
                        pool.wait_ge(sent[i], (r + 1) * (NT * PICKS * 16))
                        pool.sem_inc(gone[i], 1)


def build_slot_experts(nc, d, route):
    tile_expert = route["tile_expert"]
    N = 2
    with ExitStack() as ctx:
        sb = lambda name, shape, dt=F32: ctx.enter_context(nc.sbuf_tensor("se_" + name, shape, dt))
        ps = lambda name, shape: ctx.enter_context(nc.psum_tensor("se_" + name, shape, F32))
        sem = Semaphores(nc, ctx, "se_")
        ident = sb("ident", [P, P])
        w1 = sb("w1", [P, FFN_EXPERTS, HALVES * DFF])
        w2 = sb("w2", [P, FFN_EXPERTS, FC * DIM])
        xs = [[sb(f"xs{i}_{n}", [P, DIM]) for n in range(N)] for i in range(2)]
        xT = [sb(f"xT{n}", [P, HALVES, P]) for n in range(N)]
        act1 = [sb(f"act1_{n}", [P, DFF]) for n in range(N)]
        aT = [sb(f"aT{n}", [P, FC, P]) for n in range(N)]
        y = [[sb(f"y{i}_{n}", [P, DIM]) for n in range(N)] for i in range(2)]
        xt_ps = [ps(f"xt_ps{n}", [P, HALVES * P]) for n in range(N)]
        up_ps = [ps(f"up_ps{n}", [P, DFF]) for n in range(N)]
        at_ps = [ps(f"at_ps{n}", [P, FC * P]) for n in range(N)]
        y_ps = [ps(f"y_ps{n}", [P, DIM]) for n in range(N)]
        consts = sem("consts")
        xs_in = [sem(f"xs_in{i}") for i in range(2)]
        y_out = [sem.from_zero(f"y_out{i}") for i in range(2)]
        y_gone = [sem(f"y_gone{i}") for i in range(2)]
        x_turned, xT_ready, up_done, act_ready, a_turned, aT_ready, down_done, y_ready = map(sem, (
            "x_turned", "xT_ready", "up_done", "act_ready", "a_turned", "aT_ready", "down_done", "y_ready"))
        CONSTS = 16 * (1 + 2 * FFN_EXPERTS)
        ROUNDS = SLOT_TILES // (2 * N)
        sem.start()
        with nc.Block() as block:
            @block.sync
            def _(sync):
                sync.dma_start(ident[:, :], d["ident"]).then_inc(consts, 16)
                for e in range(FFN_EXPERTS):
                    sync.dma_start(w1[:, e, :].rearrange("p (k f) -> p k f", k=HALVES), d["ffn1_w1T"][e].rearrange("(k p) f -> p k f", p=P)).then_inc(consts, 16)
                    sync.dma_start(w2[:, e, :].rearrange("p (c f) -> p c f", c=FC), d["ffn1_w2T"][e].rearrange("(c p) f -> p c f", p=P)).then_inc(consts, 16)
                with sync.Fori(0, ROUNDS) as r:
                    for i in range(2):
                        for n in range(N):
                            sync.wait_ge(x_turned, at((r * 2 + i) * N - N + n + 1 if i > 0 else r * (2 * N)))
                            sync.dma_start(xs[i][n][:, :], slot_rows(d["xs"], (r * 2 + i) * N + n)).then_inc(xs_in[i], 16)

            @block.tensor
            def _(pe):
                pe.wait_ge(consts, at(CONSTS))
                with pe.Fori(0, ROUNDS) as r:
                    for i in range(2):
                        turn = (r * 2 + i) * N
                        pe.wait_ge(xs_in[i], at((r + 1) * (16 * N)))
                        for n in range(N):
                            pe.wait_ge(xT_ready, at(turn))
                            for k in range(HALVES):
                                mm = pe.transpose(xt_ps[n][:, k * P:(k + 1) * P], xs[i][n][:, k * P:(k + 1) * P], ident[:, :])
                            mm.then_inc(x_turned, 1)
                        experts = [pe.value_load(tile_expert[0:1, bass.ds(turn + n, 1)], min_val=0, max_val=FFN_EXPERTS - 1) for n in range(N)]
                        for n in range(N):
                            pe.wait_ge(xT_ready, at(turn + n + 1))
                            pe.wait_ge(act_ready, at(turn))
                            for k in range(HALVES):
                                mm = pe.matmul(up_ps[n][:, :], xT[n][:, k, :], w1[:, bass.ds(experts[n], 1), k * DFF:(k + 1) * DFF].rearrange("p a f -> p (a f)"),
                                               start=(k == 0), stop=(k == HALVES - 1))
                            mm.then_inc(up_done, 1)
                        for n in range(N):
                            pe.wait_ge(act_ready, at(turn + n + 1))
                            pe.wait_ge(aT_ready, at(turn))
                            for c in range(FC):
                                mm = pe.transpose(at_ps[n][:, c * P:(c + 1) * P], act1[n][:, c * P:(c + 1) * P], ident[:, :])
                            mm.then_inc(a_turned, 1)
                        for n in range(N):
                            pe.wait_ge(aT_ready, at(turn + n + 1))
                            pe.wait_ge(y_ready, at(turn))
                            for c in range(FC):
                                mm = pe.matmul(y_ps[n][:, :], aT[n][:, c, :], w2[:, bass.ds(experts[n], 1), c * DIM:(c + 1) * DIM].rearrange("p a f -> p (a f)"),
                                               start=(c == 0), stop=(c == FC - 1))
                            mm.then_inc(down_done, 1)

            @block.scalar
            def _(act):
                with act.Fori(0, ROUNDS) as r:
                    for i in range(2):
                        turn = (r * 2 + i) * N
                        for n in range(N):
                            act.wait_ge(x_turned, at(turn + n + 1))
                            act.wait_ge(up_done, at(turn))
                            act.copy(xT[n][:, :, :].rearrange("p k t -> p (k t)"), xt_ps[n][:, :]).then_inc(xT_ready, 1)
                        for n in range(N):
                            act.wait_ge(up_done, at(turn + n + 1))
                            act.wait_ge(a_turned, at(turn))
                            act.activation(act1[n][:, :], up_ps[n][:, :], ACT.Silu).then_inc(act_ready, 1)

            @block.vector
            def _(vec):
                with vec.Fori(0, ROUNDS) as r:
                    for i in range(2):
                        turn = (r * 2 + i) * N
                        for n in range(N):
                            vec.wait_ge(a_turned, at(turn + n + 1))
                            vec.wait_ge(down_done, at(turn))
                            vec.tensor_copy(aT[n][:, :, :].rearrange("p c t -> p (c t)"), at_ps[n][:, :]).then_inc(aT_ready, 1)
                        for n in range(N):
                            vec.wait_ge(y_gone[i], at(r))
                            vec.wait_ge(down_done, at(turn + n + 1))
                            vec.tensor_copy(y[i][n][:, :], y_ps[n][:, :]).then_inc(y_ready, 1)

            @block.gpsimd
            def _(pool):
                with pool.Fori(0, ROUNDS) as r:
                    for i in range(2):
                        for n in range(N):
                            pool.wait_ge(y_ready, at((r * 2 + i) * N + n + 1))
                            pool.dma_start(slot_rows(d["ys"], (r * 2 + i) * N + n), y[i][n][:, :]).then_inc(y_out[i], 16)
                        pool.wait_ge(y_out[i], (r + 1) * (16 * N))
                        pool.sem_inc(y_gone[i], 1)


def build_combine(nc, d, route):
    slots, shares, pass_w = route["slots"], route["shares"], route["pass_w"]
    VEC_STEPS = 30
    with ExitStack() as ctx:
        sb = lambda name, shape, dt=F32: ctx.enter_context(nc.sbuf_tensor("cb_" + name, shape, dt))
        sem = Semaphores(nc, ctx, "cb_")
        both = range(2)
        gb = sb("gb", [P, BATCH, DIM])
        x = [sb(f"x{i}", [P, NT, DIM]) for i in both]
        h = [sb(f"h{i}", [P, NT, DIM]) for i in both]
        y = [sb(f"y{i}", [P, PICKS * NT, DIM]) for i in both]
        share = [sb(f"share{i}", [P, PICKS + 1, NT]) for i in both]
        to = [[sb(f"to{i}_{n}", [P, 1], INT) for n in range(NT * PICKS)] for i in both]
        consts, cleared, order, to_ready, passed = map(sem, ("consts", "cleared", "order", "to_ready", "passed"))
        rows_in = [sem(f"rows_in{i}") for i in both]
        fetched = [sem.from_zero(f"fetched{i}") for i in both]
        x_ready = [sem(f"x_ready{i}") for i in both]
        x_out = [sem(f"x_out{i}") for i in both]
        ROUNDS = STEPS // 2
        sem.start()
        with nc.Block() as block:
            @block.sync
            def _(sync):
                for b in range(BATCH):
                    sync.dma_start(gb[:, b, :], d["mod"][1, b * GROUPS_PER_BATCH, MOD_GB * DIM:(MOD_GB + 1) * DIM].partition_broadcast(P)).then_inc(consts, 16)
                with sync.Fori(0, BATCH * ROUNDS) as r:
                    for i in both:
                        sync.wait_ge(x_out[i], at(r * 16))
                        sync.dma_start(x[i][:, :, :], step_rows(d["x3"], r * 2 + i)).then_inc(rows_in[i], 16)
                        sync.dma_start(h[i][:, :, :], step_rows(d["h3"], r * 2 + i)).then_inc(rows_in[i], 16)
                    for i in both:
                        sync.wait_ge(x_ready[i], at(r + 1))
                        sync.dma_start(step_rows(d["out"], r * 2 + i), x[i][:, :, :]).then_inc(x_out[i], 16)
                for i in both:
                    sync.wait_ge(x_out[i], at(BATCH * ROUNDS * 16))

            @block.gpsimd
            def _(pool):
                pool.wait_ge(cleared, at(2))
                with pool.Fori(0, BATCH * ROUNDS) as r:
                    for i in both:
                        pool.wait_ge(to_ready, at((r * 2 + i + 1) * (NT * PICKS)))
                        pool.sem_inc(passed, 1)
                        for k in range(PICKS):
                            for j in range(NT):
                                pool.indirect_dma_start(y[i][:, k * NT + j, :], None, d["ys"], bass.IndirectOffsetOnAxis(ap=to[i][k * NT + j][:, :], axis=0),
                                                        bounds_check=SLOTS - 1, oob_is_err=False).then_inc(fetched[i], 16)

            @block.vector
            def _(vec):
                for i in both:
                    vec.memset(y[i][:, :, :], 0.0).then_inc(cleared, 1)
                vec.wait_ge(consts, at(16 * BATCH))
                with vec.Fori(0, BATCH) as b:
                    with vec.Fori(0, ROUNDS) as rr:
                        r = b * ROUNDS + rr
                        seq = Chain(vec, order, r * VEC_STEPS)
                        for i in both:
                            vec.wait_ge(x_ready[i], at(r))
                            tiles = bass.ds((r * 2 + i) * NT, NT)
                            for k in range(PICKS):
                                for j in range(NT):
                                    vec.tensor_copy(to[i][k * NT + j][:, :], slots[:, k, bass.ds((r * 2 + i) * NT + j, 1)]).then_inc(to_ready, 1)
                            seq.done(vec.tensor_copy(share[i][:, 0:PICKS, :], shares[:, :, tiles]))
                            seq.done(vec.tensor_copy(share[i][:, PICKS, :], pass_w[:, tiles]))
                        seq.wait()
                        for i in both:
                            vec.wait_ge(rows_in[i], at((r + 1) * 32))
                            for j in range(NT):
                                seq.done(vec.tensor_scalar(h[i][:, j, :], h[i][:, j, :], share[i][:, PICKS, j:j + 1], None, ALU.mult))
                            vec.wait_ge(fetched[i], (r + 1) * (NT * PICKS * 16))
                            for k in range(PICKS):
                                seq.wait()
                                for j in range(NT):
                                    seq.done(vec.scalar_tensor_tensor(h[i][:, j, :], y[i][:, k * NT + j, :], share[i][:, k, j:j + 1], h[i][:, j, :], ALU.mult, ALU.add))
                            seq.wait()
                            seq.done(vec.tensor_tensor(h[i][:, :, :], h[i][:, :, :], gb[:, bass.ds(b, 1), :].broadcast_to([P, NT, DIM]), ALU.mult))
                            seq.wait()
                            seq.tell(vec.tensor_tensor(x[i][:, :, :], x[i][:, :, :], h[i][:, :, :], ALU.add), x_ready[i], r + 1)
                        assert seq.steps == VEC_STEPS, seq.steps


def build_mixture(nc, d):
    with ExitStack() as ctx:
        sb = lambda name, shape, dt=F32: ctx.enter_context(nc.sbuf_tensor("mx_" + name, shape, dt))
        route = {
            "picked": sb("picked", [P, PICKS, TILES, FFN_EXPERTS]), "shares": sb("shares", [P, PICKS, TILES]),
            "pass_w": sb("pass_w", [P, TILES]), "slots": sb("slots", [P, PICKS, TILES], INT),
            "tile_expert": sb("tile_expert", [1, SLOT_TILES], INT),
        }
        build_routing(nc, d, route)
        build_slots(nc, d, route)
        build_dispatch(nc, d, route)
        build_slot_experts(nc, d, route)
        build_combine(nc, d, route)


def build_program(nc, d):
    with ExitStack() as ctx:
        sb = lambda name, shape: ctx.enter_context(nc.sbuf_tensor(name, shape, F32))
        build_modulation(nc, d)
        with nc.sbuf_tensor("gamma_last", [P, HALVES, CHUNKS], F32) as gamma_last:
            build_delta_chunks(nc, d, gamma_last)
            build_state_scan(nc, d, gamma_last)
        build_delta_outputs(nc, d)
        with ExitStack() as ffn:
            chosen = ffn.enter_context(nc.sbuf_tensor("chosen", [EXPERTS, BATCH, SEQ], F32))
            merged = ffn.enter_context(nc.sbuf_tensor("merged", [P, HALVES, EXPERTS, BATCH], F32))
            expert_out = ffn.enter_context(nc.sbuf_tensor("expert_out", [EXPERTS, BATCH, DIM], F32))
            build_token_choice(nc, d, merged, chosen)
            build_experts(nc, d, merged, expert_out)
            build_scatter(nc, d, chosen, expert_out)
        build_window_attention(nc, d)
        build_mixture(nc, d)


def constants():
    import numpy as np
    token, key = np.arange(P)[:, None], np.arange(SPAN)[None]
    other = np.arange(P)[None]
    in_window = (key >= token) & (key < token + WINDOW)
    band = np.where(in_window, 0.0, NEG)
    first = np.where(in_window & (key >= WINDOW), 0.0, NEG)
    keep = np.ones((P, STEPS))
    keep[0, 0] = 0.0
    same_phrase = (token // PHRASE == other // PHRASE) & (token <= other)
    tables = {
        "ident": np.eye(P),
        "block_mask": np.kron(np.eye(P // HEAD), np.ones((HEAD, HEAD))),
        "chunk_mask": np.arange(P)[:, None] // CHUNK == np.arange(TILE_CHUNKS)[None],
        "ones": np.ones((P, 1)),
        "means": np.where(same_phrase, 1.0 / (other % PHRASE + 1), 0.0),
        "nears": 1.0 + (key == token + WINDOW - 1),
        "band": np.stack([first] + [band] * (STEPS - 1), axis=1),
        "keep": keep,
        "before": token < other,
        "ones_square": np.ones((P, P)),
        "tile_starts": np.tile(P * np.arange(TILES), (P, 1)),
        "slot_tiles": np.tile(np.arange(SLOT_TILES), (P, 1)),
        "numbers": np.tile(np.arange(ALL_EXPERTS), (P, 1)),
    }
    return {name: np.ascontiguousarray(table, dtype=np.float32) for name, table in tables.items()}


def kernel(**inputs):
    import numpy as np
    import concourse.bacc as bacc
    from concourse.bass_utils import run_bass_kernel_spmd as run

    a = {name: np.asarray(value) for name, value in inputs.items()}
    L0, L1 = "L0_attn_", "L1_attn_"
    halves = lambda v: v.reshape(HALVES, P)
    layouts = {
        "cT": np.stack([a[f"L{l}_c"].T.reshape(HALVES, P, BATCH).transpose(1, 0, 2).reshape(P, HALVES * BATCH) for l in range(2)]),
        "wmod": np.stack([a["L0_wmod"], a["L1_wmod"]]),
        "x": a["L0_attn_x"].reshape(TOKENS, DIM),
        "w_proj": np.concatenate([a[L0 + n] for n in ("Wq", "Wk", "Wv", "Wgate", "Walpha", "Wbeta")], axis=1),
        "dt_bias": a[L0 + "dt_bias"], "A_log": a[L0 + "A_log"], "rms_w": a[L0 + "rms_w"], "w_out": a[L0 + "Wout"],
        "gate0_wT": a["L0_ffn_gate_w"].T, "gate0_b": a["L0_ffn_gate_b"].reshape(EXPERTS, 1),
        "w1_all": a["L0_ffn_w1"], "w2_all": a["L0_ffn_w2"],
        "w1_bias": a["L0_ffn_w1"][:, DIM, :].reshape(EXPERTS, P, HC).transpose(1, 0, 2),
        "w_cols": np.stack([a[L1 + n + "_w"].T for n in ("q", "k", "pk")]),
        "w_rows": np.stack([a[L1 + n + "_w"].T for n in ("v", "pv")]),
        "col_bias": np.stack([halves(a[L1 + n + "_b"]) for n in ("q", "k", "pk")]).transpose(2, 0, 1),
        "row_bias": np.concatenate([a[L1 + n + "_b"] for n in ("v", "pv")]),
        "gate1_wT": a["L1_ffn_gate_w"].T, "gate1_b": a["L1_ffn_expert_bias"],
        "ffn1_w1T": a["L1_ffn_w1"].transpose(0, 2, 1), "ffn1_w2T": a["L1_ffn_w2"].transpose(0, 2, 1),
    }
    layouts.update(constants())

    nc = bacc.Bacc("TRN2", target_bir_lowering=False, num_devices=1)
    arrays, d = {}, {}
    for name, value in layouts.items():
        value = np.ascontiguousarray(value)
        arrays[f"in_{name}"] = value
        d[name] = nc.dram_tensor(f"in_{name}", value.shape, F32, kind="ExternalInput").ap()
    scratch = {
        "mod": (2, GROUPS, MODS), "qk": (TOKENS, 2 * DIM), "vw": (TOKENS, 2 * DIM), "gate": (TOKENS, DIM),
        "qkd": (TOKENS, DIM), "inverse": (TOKENS, DIM), "vk": (TOKENS, 2 * DIM), "u": (TOKENS, DIM), "qs": (TOKENS, DIM),
        "x1": (TOKENS, DIM), "x2": (TOKENS, DIM), "x3": (TOKENS, DIM), "h3": (TOKENS, DIM),
        "xs": (SLOTS, DIM), "ys": (SLOTS, DIM),
    }
    for name, shape in scratch.items():
        d[name] = nc.dram_tensor(f"scratch_{name}", shape, F32, kind="Internal").ap()
    d["out"] = nc.dram_tensor("out", (TOKENS, DIM), F32, kind="ExternalOutput").ap()
    build_program(nc, d)
    result = run(nc, [arrays], core_ids=[0])
    return result.results[0]["out"].reshape(BATCH, SEQ, DIM)
```

```python
import concourse.bass as bass
from concourse import mybir
from concourse.alu_op_type import AluOpType as ALU
from contextlib import ExitStack

F32 = mybir.dt.float32
ACT = mybir.ActivationFunctionType
AX = mybir.AxisListType
AP = bass.AP

BATCH, SEQ, DIM = 2, 4096, 256
TOKENS = BATCH * SEQ
P = 128
HALVES = DIM // P
HEADS, HEAD = 16, 16
CHUNK = 16
GROUPS = TOKENS // (P * CHUNK)
GROUPS_PER_BATCH = GROUPS // BATCH
CHUNKS = TOKENS // CHUNK
MODS = 6 * DIM
MOD_SA, MOD_CA, MOD_GA, MOD_SB, MOD_CB, MOD_GB = range(6)


START = 1


def at(signals):
    return signals + START


class Semaphores:

    def __init__(self, nc, ctx, prefix):
        self.nc, self.prefix, self.all, self.unstarted = nc, prefix, [], []
        ctx.callback(self.clear)

    def __call__(self, name):
        self.all.append(self.nc.alloc_semaphore(self.prefix + name))
        return self.all[-1]

    def from_zero(self, name):
        self.unstarted.append(self.nc.alloc_semaphore(self.prefix + name))
        return self.unstarted[-1]

    def clear(self):
        self.nc.clear_and_free_semaphores(self.all + self.unstarted)
        self.nc.all_engine_barrier()

    def start(self):
        with self.nc.Block() as block:
            @block.sync
            def _(sync):
                for s in self.all:
                    sync.sem_inc(s, START)


class Chain:

    def __init__(self, engine, sem, start=0):
        self.engine, self.sem, self.start, self.steps = engine, sem, start, 0
        self.last = (sem, start)

    def wait(self):
        self.engine.wait_ge(self.last[0], at(self.last[1]))

    def done(self, instruction):
        self.steps += 1
        self.last = (self.sem, self.start + self.steps)
        return instruction.then_inc(self.sem, 1)

    def tell(self, instruction, sem, value):
        self.last = (sem, value)
        return instruction.then_inc(sem, 1)


def spread(ap, size):
    return ap.unsqueeze(len(ap.shape)).broadcast_to(list(ap.shape) + [size])


def view(ap, *dims, offset=0):
    return AP(ap.tensor, ap.offset + offset, [list(ap.ap[0])] + [list(d) for d in dims])


def chunk_rows(dram, g):
    return dram.rearrange("(g p t) f -> g p (t f)", g=GROUPS, p=P)[bass.ds(g, 1)].rearrange("a p f -> (a p) f")


def mod_row(d, layer, g, m):
    return d["mod"][layer, bass.ds(g, 1), m * DIM:(m + 1) * DIM].rearrange("a f -> (a f)").partition_broadcast(P)


def build_modulation(nc, d):
    with ExitStack() as ctx:
        sb = lambda name, shape: ctx.enter_context(nc.sbuf_tensor(name, shape, F32))
        sem = Semaphores(nc, ctx, "")
        c_raw = sb("mod_c", [P, 2, HALVES * BATCH])
        c_silu = sb("mod_c_silu", [P, 2, HALVES * BATCH])
        weights = sb("mod_weights", [P, 2, HALVES, MODS])
        rows = sb("mod_rows", [BATCH, 2, MODS])
        tmp = sb("mod_tmp", [BATCH, 2, 2, DIM])
        out_ps = ctx.enter_context(nc.psum_tensor("mod_ps", [BATCH, 2, 4 * 512], F32))
        loaded, silued, multiplied, copied = (sem(f"mod_{n}") for n in ("loaded", "silued", "multiplied", "copied"))
        order, gated, stored = (sem(f"mod_{n}") for n in ("order", "gated", "stored"))

        sem.start()
        with nc.Block() as block:
            @block.sync
            def _(sync):
                for l in range(2):
                    sync.dma_start(c_raw[:, l, :], d["cT"][l]).then_inc(loaded, 16)
                    sync.dma_start(weights[:, l, :, :], d["wmod"][l].rearrange("(k p) n -> p k n", p=P)).then_inc(loaded, 16)
                sync.wait_ge(gated, at(1))
                for l in range(2):
                    for b in range(BATCH):
                        for g in range(GROUPS_PER_BATCH):
                            sync.dma_start(d["mod"][l, b * GROUPS_PER_BATCH + g:b * GROUPS_PER_BATCH + g + 1, :],
                                           rows[b:b + 1, l, :]).then_inc(stored, 16)
                all_steps = d["mod_steps"].shape[0]
                for step in range(all_steps):
                    b = step * BATCH // all_steps
                    sync.dma_start(d["mod_steps"][step:step + 1, :], rows[b:b + 1, 1, :]).then_inc(stored, 16)
                sync.wait_ge(stored, at(16 * (2 * GROUPS + all_steps)))

            @block.scalar
            def _(act):
                act.wait_ge(loaded, at(64))
                act.activation(c_silu[:, :, :], c_raw[:, :, :], ACT.Silu).then_inc(silued, 1)
                act.wait_ge(multiplied, at(1))
                for l in range(2):
                    ins = act.copy(rows[:, l, :], out_ps[:, l, 0:MODS])
                    ins.then_inc(copied, 1)

            @block.tensor
            def _(pe):
                pe.wait_ge(silued, at(1))
                for l in range(2):
                    for n in range(MODS // 512):
                        for k in range(HALVES):
                            mm = pe.matmul(out_ps[:, l, n * 512:(n + 1) * 512], c_silu[:, l, k * BATCH:(k + 1) * BATCH],
                                           weights[:, l, k, n * 512:(n + 1) * 512], start=(k == 0), stop=(k == HALVES - 1))
                mm.then_inc(multiplied, 1)

            @block.vector
            def _(vec):
                seq = Chain(vec, order)
                vec.wait_ge(copied, at(2))
                part = rows[:, :, :].rearrange("b l (m f) -> b l m f", m=6)
                for m in (MOD_CA, MOD_CB):
                    seq.wait()
                    seq.done(vec.tensor_scalar(part[:, :, m, :], part[:, :, m, :], 1.0, None, ALU.add))
                for m in (MOD_GA, MOD_GB):
                    seq.wait()
                    seq.done(vec.scalar_tensor_tensor(tmp[:, 0], part[:, :, m, :], -1.0, part[:, :, m, :], ALU.mult, ALU.max))
                    seq.wait()
                    seq.done(vec.tensor_scalar(tmp[:, 0], tmp[:, 0], 0.25, 2.0, ALU.max, ALU.mult))
                    seq.wait()
                    seq.done(vec.tensor_scalar(tmp[:, 1], part[:, :, m, :], 0.0, 0.5, ALU.is_ge, ALU.subtract))
                    seq.wait()
                    ins = vec.tensor_tensor(part[:, :, m, :], tmp[:, 0], tmp[:, 1], ALU.mult)
                    if m == MOD_GB:
                        seq.tell(ins, gated, 1)
                    else:
                        seq.done(ins)


def layernorm_moments(vec, seq, x, stats, moments, scale_shift, tiles, variances_ready, variances_value):
    for j in range(tiles):
        seq.done(vec.bn_stats(stats[:, j, :], x[:, j, :]))
    mean_even, mean_odd, spread_even, spread_odd = (stats[:, :, n] for n in (1, 4, 2, 5))
    mean, gap, total, var = moments[:, 0, :], moments[:, 1, :], moments[:, 2, :], scale_shift[:, 0, :]
    seq.wait()
    seq.done(vec.tensor_tensor(gap, mean_even, mean_odd, ALU.subtract))
    seq.done(vec.tensor_tensor(mean, mean_even, mean_odd, ALU.add))
    seq.done(vec.tensor_tensor(total, spread_even, spread_odd, ALU.add))
    seq.wait()
    seq.done(vec.tensor_tensor(gap, gap, gap, ALU.mult))
    seq.done(vec.tensor_scalar(mean, mean, 0.5, None, ALU.mult))
    seq.wait()
    seq.done(vec.tensor_scalar(gap, gap, 0.25, 1e-5, ALU.mult, ALU.add))
    seq.wait()
    seq.tell(vec.scalar_tensor_tensor(var, total, 1.0 / DIM, gap, ALU.mult, ALU.add), variances_ready, variances_value)


def layernorm_scale(vec, seq, x, moments, scale_shift, tiles, rooted, rooted_value, out=None):
    out = x if out is None else out
    vec.wait_ge(rooted, at(rooted_value))
    seq.done(vec.reciprocal(scale_shift[:, 0, :], scale_shift[:, 1, :]))
    seq.wait()
    for j in range(tiles):
        seq.done(vec.tensor_scalar(out[:, j, :], x[:, j, :], moments[:, 0, j:j + 1], scale_shift[:, 0, j:j + 1],
                                   ALU.subtract, ALU.mult))


def layernorm_steps(vec, seq, x, stats, moments, scale_shift, tiles, rooted, rooted_value, variances_ready, variances_value, out=None):
    layernorm_moments(vec, seq, x, stats, moments, scale_shift, tiles, variances_ready, variances_value)
    layernorm_scale(vec, seq, x, moments, scale_shift, tiles, rooted, rooted_value, out)


PROJ = 4 * DIM + 2 * HEADS
AB = 2 * HEADS
TILE_CHUNKS = P // CHUNK
TILES_OF_GROUP = CHUNK
PAIRS = CHUNK * CHUNK * HEADS


def build_delta_chunks(nc, d, gamma_last):
    T = CHUNK
    VEC_STEPS = 175
    NORM_STEPS = 40
    with ExitStack() as ctx:
        sb = lambda name, shape: ctx.enter_context(nc.sbuf_tensor(name, shape, F32))
        ps = lambda name, shape: ctx.enter_context(nc.psum_tensor(name, shape, F32))
        sem = Semaphores(nc, ctx, "dc_")
        weights = sb("dc_weights", [P, HALVES, PROJ])
        ident = sb("dc_ident", [P, P])
        dt_bias = sb("dc_dt_bias", [P, HEADS])
        rate = sb("dc_rate", [P, 2, HEADS])
        mod = sb("dc_mod", [P, 2, DIM])
        h = sb("dc_h", [P, T, DIM])
        stats = sb("dc_stats", [P, T, 6])
        moments = sb("dc_moments", [P, 3, T])
        ss = sb("dc_scale_shift", [P, 2, T])
        hT = [sb(f"dc_hT{i}", [P, HALVES, P]) for i in range(2)]
        qk = sb("dc_qk", [P, T, 2 * DIM])
        vk = sb("dc_vk", [P, T, 2 * DIM])
        gate = [sb(f"dc_gate{i}", [P, DIM]) for i in range(2)]
        ab = sb("dc_ab", [P, T, AB])
        scratch = sb("dc_scratch", [P, T * DIM])
        norms = sb("dc_norms", [P, 2, 2, T * HEADS])
        decay = sb("dc_decay", [P, PAIRS])
        kk = sb("dc_kk", [P, PAIRS])
        qkd = sb("dc_qkd", [P, PAIRS])
        small = sb("dc_small", [P, 10, T * HEADS])
        Z, AZ, EZ, SQ, W2, ACC, DT, ALPHA, BETA, GAMMA = range(10)
        last = sb("dc_last", [P, HEADS, HEAD])
        chunk_mask = sb("dc_chunk_mask", [P, TILE_CHUNKS])
        inverse = [sb(f"dc_inverse{i}", [P, HEADS, T]) for i in range(2)]
        blocks = [sb(f"dc_blocks{i}", [P, HEADS, TILE_CHUNKS, T]) for i in range(2)]
        sides = [sb(f"dc_sides{i}", [P, 2, DIM]) for i in range(2)]
        vw = [sb(f"dc_vw{i}", [P, 2, DIM]) for i in range(2)]
        tr_ps = [ps(f"dc_tr_ps{i}", [P, 512]) for i in range(2)]
        qk_ps = [ps(f"dc_qk_ps{i}", [P, 512]) for i in range(2)]
        vg_ps = [ps(f"dc_vg_ps{i}", [P, 512]) for i in range(2)]
        ab_ps = [ps(f"dc_ab_ps{i}", [P, 512]) for i in range(2)]
        consts, cleared, x_in, var_ready, rooted = map(sem, ("consts", "cleared", "x_in", "var_ready", "rooted"))
        h_ready, turned, hT_ready, projected, copied, gate_ready, gate_out = map(sem, (
            "h_ready", "turned", "hT_ready", "projected", "copied", "gate_ready", "gate_out0"))
        gate_out = [gate_out, sem("gate_out1")]
        order, norms_ready, norms_rooted, z_ready, z_abs, z_exp, dt_ready, rate_ready = map(sem, (
            "order", "norms_ready", "norms_rooted", "z_ready", "z_abs", "z_exp", "dt_ready", "rate_ready"))
        qk_out_ready, vk_out_ready, g_out_ready, out_done, last_ready, last_turned, last_copied = map(sem, (
            "qk_out_ready", "vk_out_ready", "g_out_ready", "out_done", "last_ready", "last_turned", "last_copied"))
        solved_ready = sem("solved_ready")
        tile_in, blocks_ready, tile_solved, tile_copied, tile_out = ([sem(f"{n}{i}") for i in range(2)] for n in (
            "tile_in", "blocks_ready", "tile_solved", "tile_copied", "tile_out"))
        v_copied, qk_stored = sem("v_copied"), sem("qk_stored")

        qk_v = d["qk"].rearrange("(g p t) f -> g p (t f)", g=GROUPS, p=P)
        vk_v = d["vk"].rearrange("(g p t) f -> g p (t f)", g=GROUPS, p=P)
        gate_v = d["gate"].rearrange("(g p t) f -> g p t f", g=GROUPS, p=P)
        TURNS = 2 * T
        PAIRED = TILES_OF_GROUP // 2
        tile_rows = lambda dram, tile: dram.rearrange("(i p) f -> i p f", p=P)[bass.ds(tile, 1)].rearrange("a p f -> (a p) f")

        sem.start()
        with nc.Block() as block:
            @block.sync
            def _(sync):
                sync.dma_start(weights[:, :, :], d["w_proj"].rearrange("(k p) n -> p k n", p=P)).then_inc(consts, 16)
                sync.dma_start(ident[:, :], d["ident"]).then_inc(consts, 16)
                sync.dma_start(dt_bias[:, :], d["dt_bias"].partition_broadcast(P)).then_inc(consts, 16)
                sync.dma_start(rate[:, 0, :], d["A_log"].partition_broadcast(P)).then_inc(consts, 16)
                sync.dma_start(chunk_mask[:, :], d["chunk_mask"]).then_inc(consts, 16)

                def load_tiles(before):
                    sync.wait_ge(out_done, at((before + 1) * 48))
                    for n in range(TILES_OF_GROUP):
                        i, tile, pair = n % 2, before * TILES_OF_GROUP + n, before * PAIRED + n // 2
                        sync.wait_ge(tile_solved[i], at(pair))
                        sync.dma_start(inverse[i][:, :, :].rearrange("p h t -> p (h t)"), tile_rows(d["inverse"], tile)).then_inc(tile_in[i], 16)
                        sync.dma_start(sides[i][:, :, :].rearrange("p a f -> p (a f)"), tile_rows(d["vk"], tile)).then_inc(tile_in[i], 16)

                def load_rows(g):
                    sync.wait_ge(turned, at(g * TURNS))
                    sync.dma_start(h[:, :, :].rearrange("p t f -> p (t f)"), chunk_rows(d["x"], g)).then_inc(x_in, 16)
                    for n, m in enumerate((MOD_SA, MOD_CA)):
                        sync.dma_start(mod[:, n, :], mod_row(d, 0, g, m)).then_inc(x_in, 16)

                def group(g, before, more):
                    for j in range(T):
                        sync.wait_ge(gate_ready, at(g * T + j + 1))
                        sync.dma_start(gate_v[bass.ds(g, 1), :, j, :].rearrange("a p f -> (a p) f"), gate[j % 2][:, :]).then_inc(gate_out[j % 2], 16)
                    if more:
                        load_rows(g + 1)
                    if before is not None:
                        load_tiles(before)
                    sync.wait_ge(qk_out_ready, at(g + 1))
                    sync.dma_start(qk_v[bass.ds(g, 1)].rearrange("a p f -> (a p) f"), qk[:, :, :].rearrange("p t f -> p (t f)")).then_inc(qk_stored, 16)
                    sync.wait_ge(g_out_ready, at(g + 1))
                    sync.dma_start(chunk_rows(d["qkd"], g), qkd[:, :]).then_inc(out_done, 16)
                    sync.wait_ge(solved_ready, at(g + 1))
                    sync.dma_start(chunk_rows(d["inverse"], g), kk[:, :]).then_inc(out_done, 16)
                    sync.wait_ge(vk_out_ready, at(g + 1))
                    sync.dma_start(vk_v[bass.ds(g, 1)].rearrange("a p f -> (a p) f"), vk[:, :, :].rearrange("p t f -> p (t f)")).then_inc(out_done, 16)

                load_rows(0)
                group(0, None, more=True)
                with sync.Fori(1, GROUPS - 1) as g:
                    group(g, g - 1, more=True)
                group(GROUPS - 1, GROUPS - 2, more=False)
                load_tiles(GROUPS - 1)
                for stored in gate_out:
                    sync.wait_ge(stored, at(16 * GROUPS * T // 2))
                sync.wait_ge(qk_stored, at(16 * GROUPS))
                sync.wait_ge(out_done, at(48 * GROUPS))

            @block.tensor
            def _(pe):
                pe.wait_ge(consts, at(80))

                def turn(g, n):
                    if n == 0:
                        pe.wait_ge(h_ready, at(g + 1))
                    if n >= 2:
                        pe.wait_ge(hT_ready, at(g * TURNS + n - 1))
                    else:
                        pe.wait_ge(hT_ready, at(g * TURNS))
                        pe.wait_ge(last_copied, at(g))
                    for k in range(HALVES):
                        mm = pe.transpose(tr_ps[n % 2][:, k * P:(k + 1) * P], h[:, n % T, k * P:(k + 1) * P], ident[:, :])
                    mm.then_inc(turned, 1)

                def project(g, n, solved):
                    pe.wait_ge(hT_ready, at(g * TURNS + n + 1))
                    i, j = n % 2, n % T
                    if n < T:
                        parts = (qk_ps, 0, 512), (ab_ps, 1024, PROJ)
                        pe.wait_ge(copied, at((g * T + j - 1) * 2 if j >= 2 else g * T * 2))
                        if j < 2 and solved is not None:
                            pe.wait_ge(tile_copied[i], at(solved * PAIRED))
                    else:
                        parts = (vg_ps, 512, 1024),
                        pe.wait_ge(v_copied, at(g * T + j - 1 if j >= 2 else g * T))
                        pe.wait_ge(gate_ready, at(g * T + j - 1 if j >= 2 else g * T))
                    for out, a, b in parts:
                        for k in range(HALVES):
                            mm = pe.matmul(out[i][:, 0:b - a], hT[i][:, k, :], weights[:, k, a:b], start=(k == 0), stop=(k == HALVES - 1))
                    mm.then_inc(projected, 1)

                def solve_tiles(before, projections):
                    pe.wait_ge(copied, at(projections * T * 2))
                    for n in range(TILES_OF_GROUP):
                        i, pair = n % 2, before * PAIRED + n // 2
                        pe.wait_ge(tile_copied[i], at(pair))
                        pe.wait_ge(tile_in[i], at((pair + 1) * 32))
                        pe.wait_ge(blocks_ready[i], at(pair + 1))
                        for h in range(HEADS):
                            mm = pe.matmul(qk_ps[i][:, :].rearrange("p (a f) -> p a f", a=2)[:, :, h * HEAD:(h + 1) * HEAD],
                                           blocks[i][:, h, :, :].rearrange("p c t -> p (c t)"), sides[i][:, :, h * HEAD:(h + 1) * HEAD], start=True, stop=True)
                        mm.then_inc(tile_solved[i], 1)

                def group(g, before):
                    turn(g, 0)
                    for n in range(TURNS):
                        if n + 1 < TURNS:
                            turn(g, n + 1)
                        project(g, n, before)
                    if before is not None:
                        solve_tiles(before, g + 1)
                    pe.wait_ge(last_ready, at(g + 1))
                    pe.wait_ge(hT_ready, at((g + 1) * TURNS))
                    for k in range(HALVES):
                        mm = pe.transpose(tr_ps[0][:, k * P:(k + 1) * P], last[:, k * 8:(k + 1) * 8, :].rearrange("p h j -> p (h j)"), ident[:, :])
                    mm.then_inc(last_turned, 1)

                group(0, None)
                with pe.Fori(1, GROUPS) as g:
                    group(g, g - 1)
                solve_tiles(GROUPS - 1, GROUPS)

            @block.scalar
            def _(act):
                act.wait_ge(consts, at(80))
                act.activation(rate[:, 1, :], rate[:, 0, :], ACT.Exp).then_inc(rate_ready, 1)

                def solve_tiles(before):
                    for n in range(TILES_OF_GROUP + 1):
                        if n < TILES_OF_GROUP:
                            i, pair = n % 2, before * PAIRED + n // 2
                            act.wait_ge(tile_solved[i], at(pair))
                            act.wait_ge(tile_in[i], at((pair + 1) * 32))
                            for c in range(TILE_CHUNKS):
                                ins = act.activation(blocks[i][:, :, c, :], inverse[i][:, :, :], ACT.Copy, scale=chunk_mask[:, c:c + 1])
                            ins.then_inc(blocks_ready[i], 1)
                        if n > 0:
                            m = n - 1
                            i, pair = m % 2, before * PAIRED + m // 2
                            act.wait_ge(tile_out[i], at(pair * 16))
                            act.wait_ge(tile_solved[i], at(pair + 1))
                            act.copy(vw[i][:, :, :].rearrange("p a f -> p (a f)"), qk_ps[i][:, :]).then_inc(tile_copied[i], 1)
                            act.wait_ge(tile_copied[i], at(pair + 1))
                            act.dma_start(tile_rows(d["vw"], before * TILES_OF_GROUP + m), vw[i][:, :, :].rearrange("p a f -> p (a f)")).then_inc(tile_out[i], 16)

                def project(g, half):
                    for j in range(T + 1):
                        n = half * T + j
                        if j < T:
                            act.wait_ge(turned, at(g * TURNS + n + 1))
                            act.wait_ge(projected, at(g * TURNS + n - 1 if n >= 2 else g * TURNS))
                            act.copy(hT[n % 2][:, :, :].rearrange("p k t -> p (k t)"), tr_ps[n % 2][:, 0:2 * P]).then_inc(hT_ready, 1)
                        if j > 0:
                            i = j - 1
                            act.wait_ge(projected, at(g * TURNS + n))
                            if half == 0:
                                act.copy(qk[:, i, :], qk_ps[i % 2][:, :]).then_inc(copied, 1)
                                act.copy(ab[:, i, :], ab_ps[i % 2][:, 0:AB]).then_inc(copied, 1)
                            else:
                                if i == 0:
                                    act.wait_ge(out_done, at(g * 48))
                                act.copy(vk[:, i, 0:DIM], vg_ps[i % 2][:, 0:DIM]).then_inc(v_copied, 1)
                                act.wait_ge(gate_out[i % 2], at((g * (T // 2) + i // 2) * 16))
                                act.copy(gate[i % 2][:, :], vg_ps[i % 2][:, DIM:2 * DIM]).then_inc(gate_ready, 1)

                def root(g):
                    act.wait_ge(var_ready, at(g + 1))
                    act.activation(ss[:, 1, :], ss[:, 0, :], ACT.Sqrt).then_inc(rooted, 1)

                def group(g, before, more):
                    act.wait_ge(qk_stored, at(g * 16))
                    project(g, 0)
                    act.wait_ge(norms_ready, at(g + 1))
                    act.activation(norms[:, 1, :, :], norms[:, 0, :, :], ACT.Sqrt).then_inc(norms_rooted, 1)
                    act.wait_ge(z_ready, at(g + 1))
                    act.activation(small[:, AZ, :], small[:, Z, :], ACT.Abs).then_inc(z_abs, 1)
                    act.wait_ge(z_abs, at(g + 1))
                    act.activation(small[:, EZ, :], small[:, AZ, :], ACT.Exp, scale=-1.0).then_inc(z_exp, 1)
                    project(g, 1)
                    act.wait_ge(dt_ready, at(g + 1))
                    act.activation(small[:, ALPHA, :], small[:, DT, :], ACT.Exp, scale=-1.0).then_inc(z_exp, 1)
                    act.activation(small[:, BETA, :].rearrange("p (t h) -> p t h", t=T), ab[:, :, HEADS:AB], ACT.Sigmoid).then_inc(z_exp, 1)
                    if before is not None:
                        solve_tiles(before)
                    act.wait_ge(last_turned, at(g + 1))
                    act.copy(gamma_last[:, :, bass.ds(g * P, P)], tr_ps[0][:, 0:2 * P].rearrange("p (k c) -> p k c", k=HALVES)).then_inc(last_copied, 1)
                    if more:
                        root(g + 1)

                root(0)
                group(0, None, more=True)
                with act.Fori(1, GROUPS - 1) as g:
                    group(g, g - 1, more=True)
                group(GROUPS - 1, GROUPS - 2, more=False)
                solve_tiles(GROUPS - 1)
                act.wait_ge(last_copied, at(GROUPS))
                for i in range(2):
                    act.wait_ge(tile_out[i], at(GROUPS * PAIRED * 16))

            @block.vector
            def _(vec):
                for z in (kk, qkd, decay):
                    vec.memset(z[:, :], 0.0).then_inc(cleared, 1)
                vec.wait_ge(cleared, at(3))
                vec.memset(view(decay[:, :], [DIM + 1, T], [T, HEADS]), 1.0).then_inc(cleared, 1)
                vec.wait_ge(cleared, at(4))
                vec.wait_ge(rate_ready, at(1))
                vec.wait_ge(consts, at(80))

                def normalize(seq, g):
                    seq.wait()
                    vec.wait_ge(x_in, at((g + 1) * 48))
                    layernorm_steps(vec, seq, h[:, :, :], stats, moments, ss, T, rooted, g + 1, var_ready, g + 1)
                    seq.wait()
                    seq.done(vec.tensor_tensor(h[:, :, :], h[:, :, :], mod[:, 1:2, :].broadcast_to([P, T, DIM]), ALU.mult))
                    seq.wait()
                    seq.tell(vec.tensor_tensor(h[:, :, :], h[:, :, :], mod[:, 0:1, :].broadcast_to([P, T, DIM]), ALU.add), h_ready, g + 1)

                def group(g, more):
                    seq = Chain(vec, order, g * VEC_STEPS + NORM_STEPS)
                    seq.wait()
                    vec.wait_ge(copied, at((g + 1) * T * 2))
                    sc = scratch[:, :].rearrange("p (t f) -> p t f", t=T)
                    for a in range(2):
                        part = qk[:, :, a * DIM:(a + 1) * DIM]
                        seq.wait()
                        seq.done(vec.tensor_tensor(sc, part, part, ALU.mult))
                        seq.wait()
                        ins = vec.tensor_reduce(norms[:, 0, a, :], scratch[:, :].rearrange("p (n e) -> p n e", e=HEAD), AX.X, ALU.add)
                        if a == 0:
                            seq.done(ins)
                        else:
                            seq.tell(ins, norms_ready, g + 1)

                    def sm(n):
                        return small[:, n, :].rearrange("p (t h) -> p t h", t=T)
                    seq.wait()
                    seq.tell(vec.tensor_tensor(sm(Z), ab[:, :, 0:HEADS], dt_bias[:, :].unsqueeze(1).broadcast_to([P, T, HEADS]), ALU.add), z_ready, g + 1)
                    vec.wait_ge(norms_rooted, at(g + 1))
                    seq.done(vec.tensor_scalar(norms[:, 1, :, :], norms[:, 1, :, :], 1e-12, None, ALU.max))
                    seq.wait()
                    seq.done(vec.reciprocal(norms[:, 1, :, :], norms[:, 1, :, :]))
                    seq.wait()
                    seq.done(vec.tensor_scalar(norms[:, 1, 0, :], norms[:, 1, 0, :], HEAD ** -0.5, None, ALU.mult))
                    for a in range(2):
                        part = qk[:, :, a * DIM:(a + 1) * DIM].rearrange("p t (h e) -> p t h e", h=HEADS)
                        seq.wait()
                        seq.done(vec.tensor_tensor(part, part, spread(norms[:, 1, a, :].rearrange("p (t h) -> p t h", t=T), HEAD), ALU.mult))
                    vec.wait_ge(z_exp, at(g * 3 + 1))
                    seq.done(vec.tensor_scalar(sm(SQ), sm(EZ), 2.0, None, ALU.add))
                    seq.wait()
                    seq.done(vec.reciprocal(sm(SQ), sm(SQ)))
                    seq.wait()
                    seq.done(vec.tensor_tensor(sm(SQ), sm(EZ), sm(SQ), ALU.mult))
                    seq.wait()
                    seq.done(vec.tensor_tensor(sm(W2), sm(SQ), sm(SQ), ALU.mult))
                    seq.wait()
                    seq.done(vec.tensor_scalar(sm(ACC), sm(W2), 1.0 / 15.0, None, ALU.mult))
                    for n in (13, 11, 9, 7, 5, 3):
                        seq.wait()
                        seq.done(vec.scalar_tensor_tensor(sm(ACC), sm(ACC), 1.0 / n, sm(W2), ALU.add, ALU.mult))
                    seq.wait()
                    seq.done(vec.scalar_tensor_tensor(sm(ACC), sm(ACC), 1.0, sm(SQ), ALU.add, ALU.mult))
                    seq.wait()
                    seq.done(vec.tensor_scalar(sm(Z), sm(Z), 0.0, None, ALU.max))
                    seq.wait()
                    seq.done(vec.scalar_tensor_tensor(sm(DT), sm(ACC), 2.0, sm(Z), ALU.mult, ALU.add))
                    seq.wait()
                    seq.tell(vec.tensor_tensor(sm(DT), sm(DT), rate[:, 1:2, :].broadcast_to([P, T, HEADS]), ALU.mult), dt_ready, g + 1)

                    lag_v = lambda m, lag: view(m[:, :], [DIM + 1, T - lag], [T, HEADS], offset=lag)
                    for lag in range(T):
                        n = T - lag
                        for a, m in ((0, qkd), (1, kk)):
                            if a == 1 and lag == 0:
                                continue
                            if lag == 0:
                                vec.wait_ge(out_done, at(g * 48))
                            seq.wait()
                            seq.done(vec.tensor_tensor(sc[:, 0:n, :], qk[:, lag:T, a * DIM:(a + 1) * DIM], qk[:, 0:n, DIM:2 * DIM], ALU.mult))
                            seq.wait()
                            seq.done(vec.tensor_reduce(lag_v(m, lag), scratch[:, 0:n * DIM].rearrange("p (n h e) -> p n h e", n=n, e=HEAD), AX.X, ALU.add))

                    vec.wait_ge(z_exp, at(g * 3 + 3))
                    for lag in range(1, T):
                        seq.wait()
                        seq.done(vec.tensor_tensor(lag_v(decay, lag), view(decay[:, :], [DIM + 1, T - lag], [T, HEADS], offset=lag - 1),
                                                   sm(ALPHA)[:, lag:T, :], ALU.mult))
                    seq.wait()
                    seq.done(vec.tensor_tensor(sm(GAMMA), view(decay[:, :], [1, T], [T, HEADS]),
                                               sm(ALPHA)[:, 0:1, :].broadcast_to([P, T, HEADS]), ALU.mult))
                    seq.wait()
                    seq.tell(vec.tensor_copy(last[:, :, :], spread(sm(GAMMA)[:, T - 1, :], HEAD)), last_ready, g + 1)
                    def heads_of(buf, a):
                        return buf[:, :, a * DIM:(a + 1) * DIM].rearrange("p t (h e) -> p t h e", h=HEADS)
                    seq.wait()
                    seq.done(vec.tensor_tensor(sm(SQ), sm(BETA), sm(GAMMA), ALU.mult))
                    seq.wait()
                    seq.done(vec.tensor_tensor(heads_of(vk, 1), heads_of(qk, 1), spread(sm(SQ), HEAD), ALU.mult))
                    seq.wait()
                    seq.done(vec.tensor_scalar(sm(GAMMA), sm(GAMMA), -1.0, None, ALU.mult))
                    seq.wait()
                    seq.done(vec.tensor_tensor(heads_of(qk, 0), heads_of(qk, 0), spread(sm(GAMMA), HEAD), ALU.mult))
                    seq.wait()
                    seq.tell(vec.tensor_tensor(heads_of(qk, 1), heads_of(qk, 1), view(decay[:, :], [DIM, T], [T, HEADS], [0, HEAD], offset=T - 1), ALU.mult), qk_out_ready, g + 1)
                    if more:
                        normalize(seq, g + 1)
                    seq.wait()
                    seq.tell(vec.tensor_tensor(qkd[:, :], qkd[:, :], decay[:, :], ALU.mult), g_out_ready, g + 1)
                    seq.wait()
                    seq.done(vec.tensor_tensor(kk[:, :], kk[:, :], decay[:, :], ALU.mult))
                    seq.wait()
                    rows = kk[:, :].rearrange("p (s h t) -> p s h t", s=T, h=HEADS)
                    seq.done(vec.tensor_scalar(sm(ACC), sm(BETA), -1.0, None, ALU.mult))
                    seq.wait()
                    seq.done(vec.tensor_tensor(rows, rows, view(small[:, ACC, :], [0, T], [1, HEADS], [HEADS, T]), ALU.mult))
                    seq.wait()
                    seq.done(vec.memset(view(kk[:, :], [DIM + 1, T], [T, HEADS]), 1.0))

                    for r in range(1, T - 1):
                        n = T - 1 - r
                        product = view(scratch[:, :], [HEADS * n, r], [n, HEADS], [1, n])
                        rest = view(kk[:, :], [DIM, r], [T, HEADS], [1, n], offset=r + 1)
                        seq.wait()
                        seq.done(vec.tensor_tensor(product, view(kk[:, :], [0, r], [T, HEADS], [1, n], offset=r * DIM + r + 1),
                                                   view(kk[:, :], [DIM, r], [T, HEADS], [0, n], offset=r), ALU.mult))
                        seq.wait()
                        ins = vec.tensor_tensor(rest, rest, product, ALU.add)
                        if r == T - 2:
                            seq.tell(ins, solved_ready, g + 1)
                        else:
                            seq.done(ins)

                    seq.wait()
                    vec.wait_ge(v_copied, at((g + 1) * T))
                    seq.tell(vec.tensor_tensor(heads_of(vk, 0), heads_of(vk, 0), spread(sm(BETA), HEAD), ALU.mult), vk_out_ready, g + 1)
                    return seq.steps

                first = Chain(vec, order)
                normalize(first, 0)
                assert first.steps == NORM_STEPS, first.steps
                assert group(0, more=True) == VEC_STEPS
                with vec.Fori(1, GROUPS - 1) as g:
                    group(g, more=True)
                group(GROUPS - 1, more=False)


BATCH_TILES = SEQ // P


def build_state_scan(nc, d, gamma_last):
    N = TILE_CHUNKS
    with ExitStack() as ctx:
        sb = lambda name, shape: ctx.enter_context(nc.sbuf_tensor("ss_" + name, shape, F32))
        ps = lambda name, shape: ctx.enter_context(nc.psum_tensor("ss_" + name, shape, F32))
        sem = Semaphores(nc, ctx, "ss_")
        both = range(2)
        ident = sb("ident", [P, P])
        block_mask = sb("block_mask", [P, P])
        wq_rows = [sb(f"wq_rows{i}", [P, BATCH, 2, DIM]) for i in both]
        k_rows = [sb(f"k_rows{i}", [CHUNK, BATCH, N, DIM]) for i in both]
        u_rows = [sb(f"u_rows{i}", [2 * CHUNK, BATCH, N, DIM]) for i in both]
        solved = [sb(f"solved{i}", [2 * CHUNK, BATCH, N, DIM]) for i in both]
        wq = [sb(f"wq{i}", [P, BATCH, HALVES, N, 2 * CHUNK]) for i in both]
        gammas = [sb(f"gammas{i}", [P, BATCH, HALVES, N]) for i in both]
        state = [sb(f"state{b}", [P, HALVES, P]) for b in range(BATCH)]
        decayed = [sb(f"decayed{b}", [P, HALVES, P]) for b in range(BATCH)]
        update = [sb(f"update{b}", [P, HALVES, P]) for b in range(BATCH)]
        turn_ps = [ps(f"turn_ps{b}", [P, 2, HALVES, P]) for b in range(BATCH)]
        read_ps = [ps(f"read_ps{b}", [2 * CHUNK, 512]) for b in range(BATCH)]
        write_ps = [ps(f"write_ps{b}", [P, 512]) for b in range(BATCH)]
        consts, cleared = map(sem, ("consts", "cleared"))
        rows_in = [sem(f"rows_in{i}") for i in both]
        out_done = [sem(f"out_done{i}") for i in both]
        turned, wq_ready, gammas_ready = map(sem, ("turned", "wq_ready", "gammas_ready"))
        state_read = [sem(f"state_read{b}") for b in range(BATCH)]
        u_ready = [sem(f"u_ready{b}") for b in range(BATCH)]
        state_written = [sem(f"state_written{b}") for b in range(BATCH)]
        state_ready = [sem(f"state_ready{b}") for b in range(BATCH)]
        masked = [sem(f"masked{b}") for b in range(BATCH)]
        decay_ready = [sem(f"decay_ready{b}") for b in range(BATCH)]

        vw_v = d["vw"].rearrange("(b i p) f -> b i p f", b=BATCH, p=P)
        qk_v = d["qk"].rearrange("(b i p) f -> b i p f", b=BATCH, p=P)
        vw_c = d["vw"].rearrange("(b i c t) f -> b i t c f", b=BATCH, c=N, t=CHUNK)
        qk_c = d["qk"].rearrange("(b i c t) f -> b i t c f", b=BATCH, c=N, t=CHUNK)
        u_c = d["u"].rearrange("(b i c t) f -> b i t c f", b=BATCH, c=N, t=CHUNK)
        qs_c = d["qs"].rearrange("(b i c t) f -> b i t c f", b=BATCH, c=N, t=CHUNK)
        PAIR = BATCH_TILES // 2
        LOADS = 4 * BATCH * 16
        TURN_AT = N // 2

        sem.start()
        with nc.Block() as block:
            @block.sync
            def _(sync):
                sync.dma_start(ident[:, :], d["ident"]).then_inc(consts, 16)
                sync.dma_start(block_mask[:, :], d["block_mask"]).then_inc(consts, 16)
                sync.wait_ge(cleared, at(2))

                def load(tile, i):
                    for b in range(BATCH):
                        sync.dma_start(wq_rows[i][:, b, 0, :], vw_v[b, bass.ds(tile, 1), :, DIM:2 * DIM].rearrange("a p f -> (a p) f")).then_inc(rows_in[i], 16)
                        sync.dma_start(wq_rows[i][:, b, 1, :], qk_v[b, bass.ds(tile, 1), :, 0:DIM].rearrange("a p f -> (a p) f")).then_inc(rows_in[i], 16)
                        sync.dma_start(k_rows[i][:, b, :, :], qk_c[b, bass.ds(tile, 1), :, :, DIM:2 * DIM].rearrange("a t c f -> (a t) c f")).then_inc(rows_in[i], 16)
                        sync.dma_start(u_rows[i][0:CHUNK, b, :, :], vw_c[b, bass.ds(tile, 1), :, :, 0:DIM].rearrange("a t c f -> (a t) c f")).then_inc(rows_in[i], 16)

                def store(tile, i):
                    for b in range(BATCH):
                        sync.dma_start(u_c[b, bass.ds(tile, 1)].rearrange("a t c f -> (a t) c f"), solved[i][0:CHUNK, b, :, :]).then_inc(out_done[i], 16)
                        sync.dma_start(qs_c[b, bass.ds(tile, 1)].rearrange("a t c f -> (a t) c f"), solved[i][CHUNK:2 * CHUNK, b, :, :]).then_inc(out_done[i], 16)

                def tile_pair(ii, more):
                    for i in both:
                        tile = ii * 2 + i
                        for b in range(BATCH):
                            sync.wait_ge(state_written[b], at((tile + 1) * N))
                        if more:
                            load(tile + 2, i)
                        store(tile, i)

                for i in both:
                    load(i, i)
                with sync.Fori(0, PAIR - 1) as ii:
                    tile_pair(ii, more=True)
                tile_pair(PAIR - 1, more=False)
                for i in both:
                    sync.wait_ge(out_done[i], at(PAIR * BATCH * 32))

            @block.tensor
            def _(pe):
                pe.wait_ge(consts, at(32))

                def turn(tile, i, pair):
                    pe.wait_ge(rows_in[i], at((pair + 1) * LOADS))
                    pe.wait_ge(wq_ready, at(tile * BATCH))
                    for b in range(BATCH):
                        for a in range(2):
                            for k in range(HALVES):
                                mm = pe.transpose(turn_ps[b][:, a, k, :], wq_rows[i][:, b, a, k * P:(k + 1) * P], ident[:, :])
                        mm.then_inc(turned, 1)

                def tile_pair(ii, more):
                    for i in both:
                        tile = ii * 2 + i
                        pe.wait_ge(wq_ready, at((tile + 1) * BATCH))
                        for c in range(N):
                            for b in range(BATCH):
                                pe.wait_ge(state_ready[b], at(tile * N + c + 1))
                                for k in range(HALVES):
                                    mm = pe.matmul(read_ps[b][:, k * P:(k + 1) * P], wq[i][:, b, k, c, :], state[b][:, k, :], start=(k == 0), stop=(k == HALVES - 1), skip_group_check=True)
                                mm.then_inc(state_read[b], 1)
                            if c == TURN_AT and (more or i == 0):
                                turn(tile + 1, 1 - i, ii + i)
                            for b in range(BATCH):
                                pe.wait_ge(u_ready[b], at(tile * N + c + 1))
                                for k in range(HALVES):
                                    mm = pe.matmul(write_ps[b][:, k * P:(k + 1) * P], k_rows[i][:, b, c, k * P:(k + 1) * P], solved[i][0:CHUNK, b, c, k * P:(k + 1) * P], start=(k == 0), stop=(k == HALVES - 1), skip_group_check=True)
                                mm.then_inc(state_written[b], 1)

                turn(0, 0, 0)
                with pe.Fori(0, PAIR - 1) as ii:
                    tile_pair(ii, more=True)
                tile_pair(PAIR - 1, more=False)

            @block.scalar
            def _(act):
                def copy_turned(tile, i):
                    for b in range(BATCH):
                        act.wait_ge(turned, at(tile * BATCH + b + 1))
                        act.copy(wq[i][:, b, :, :, 0:CHUNK], turn_ps[b][:, 0, :, :].rearrange("p k (c t) -> p k c t", c=N))
                        act.copy(wq[i][:, b, :, :, CHUNK:2 * CHUNK], turn_ps[b][:, 1, :, :].rearrange("p k (c t) -> p k c t", c=N)).then_inc(wq_ready, 1)

                def tile_pair(ii, more):
                    for i in both:
                        tile = ii * 2 + i
                        act.wait_ge(gammas_ready, at((tile + 1) * BATCH))
                        for c in range(N):
                            for b in range(BATCH):
                                act.wait_ge(state_ready[b], at(tile * N + c + 1))
                                for k in range(HALVES):
                                    ins = act.activation(decayed[b][:, k, :], state[b][:, k, :], ACT.Copy, scale=gammas[i][:, b, k, c:c + 1])
                                ins.then_inc(decay_ready[b], 1)
                            if c == TURN_AT and (more or i == 0):
                                copy_turned(tile + 1, 1 - i)

                copy_turned(0, 0)
                with act.Fori(0, PAIR - 1) as ii:
                    tile_pair(ii, more=True)
                tile_pair(PAIR - 1, more=False)

            @block.vector
            def _(vec):
                for i in both:
                    vec.memset(u_rows[i][:, :, :, :], 0.0).then_inc(cleared, 1)
                for b in range(BATCH):
                    vec.memset(state[b][:, :, :], 0.0).then_inc(state_ready[b], 1)
                vec.wait_ge(consts, at(32))

                def take_gammas(tile, i, used):
                    for b in range(BATCH):
                        vec.wait_ge(decay_ready[b], at(used * N))
                        vec.tensor_copy(gammas[i][:, b, :, :], gamma_last[:, :, bass.ds(tile * N + b * (CHUNKS // BATCH), N)]).then_inc(gammas_ready, 1)

                def tile_pair(ii, more):
                    for i in both:
                        tile = ii * 2 + i
                        vec.wait_ge(rows_in[i], at((ii + 1) * LOADS))
                        vec.wait_ge(out_done[i], at(ii * (BATCH * 32)))
                        for c in range(N):
                            for b in range(BATCH):
                                vec.wait_ge(state_read[b], at(tile * N + c + 1))
                                vec.tensor_tensor(solved[i][:, b, c, :], u_rows[i][:, b, c, :], read_ps[b][:, 0:DIM], ALU.subtract).then_inc(u_ready[b], 1)
                            if c == TURN_AT and (more or i == 0):
                                take_gammas(tile + 1, 1 - i, tile)
                            for b in range(BATCH):
                                vec.wait_ge(state_written[b], at(tile * N + c + 1))
                                vec.tensor_tensor(update[b][:, :, :], write_ps[b][:, 0:DIM].rearrange("p (k f) -> p k f", k=HALVES),
                                                  block_mask[:, :].unsqueeze(1).broadcast_to([P, HALVES, P]), ALU.mult).then_inc(masked[b], 1)
                                vec.wait_ge(decay_ready[b], at(tile * N + c + 1))
                                vec.wait_ge(masked[b], at(tile * N + c + 1))
                                vec.tensor_tensor(state[b][:, :, :], update[b][:, :, :], decayed[b][:, :, :], ALU.add).then_inc(state_ready[b], 1)

                take_gammas(0, 0, 0)
                with vec.Fori(0, PAIR - 1) as ii:
                    tile_pair(ii, more=True)
                tile_pair(PAIR - 1, more=False)


def flat(tile):
    return tile.rearrange("p t f -> p (t f)")


def build_delta_outputs(nc, d):
    T = CHUNK
    LATE = T // 2
    VEC_STEPS = 13
    with ExitStack() as ctx:
        sb = lambda name, shape: ctx.enter_context(nc.sbuf_tensor("do_" + name, shape, F32))
        ps = lambda name, shape: ctx.enter_context(nc.psum_tensor("do_" + name, shape, F32))
        sem = Semaphores(nc, ctx, "do_")
        ident = sb("ident", [P, P])
        w_out = sb("w_out", [P, HALVES, DIM])
        rms_w = sb("rms_w", [P, HEAD])
        both = range(2)
        u = [sb(f"u{i}", [P, T, DIM]) for i in both]
        o = [sb(f"o{i}", [P, T, DIM]) for i in both]
        qkd = [sb(f"qkd{i}", [P, PAIRS]) for i in both]
        gate = [sb(f"gate{i}", [P, T, DIM]) for i in both]
        x = [sb(f"x{i}", [P, T, DIM]) for i in both]
        ga = [sb(f"ga{i}", [P, DIM]) for i in both]
        scratch = [sb(f"scratch{i}", [P, T * DIM]) for i in both]
        rms = sb("rms", [P, 2, T * HEADS])
        oT = [sb(f"oT{i}", [P, HALVES, P]) for i in range(2)]
        gated = [sb(f"gated{i}", [P, DIM]) for i in range(2)]
        tr_ps = [ps(f"tr_ps{i}", [P, 512]) for i in range(2)]
        late_ps = ps("late_ps", [P, LATE * DIM])
        y_ps = [ps(f"y_ps{i}", [P, 512]) for i in range(2)]
        consts, order, gate_silu, gate_scaled, rms_ready, rms_rooted, o_ready = map(sem, (
            "consts", "order", "gate_silu", "gate_scaled", "rms_ready", "rms_rooted", "o_ready"))
        turned, oT_ready, projected, y_used, x_ready = map(sem, ("turned", "oT_ready", "projected", "y_used", "x_ready"))
        first_in, rows_in, x_out = ([sem(f"{n}{i}") for i in both] for n in ("first_in", "rows_in", "x_out"))

        product_ready, summed = sem("product_ready"), sem("summed")

        sem.start()
        with nc.Block() as block:
            @block.sync
            def _(sync):
                sync.dma_start(ident[:, :], d["ident"]).then_inc(consts, 16)
                sync.dma_start(w_out[:, :, :], d["w_out"].rearrange("(k p) n -> p k n", p=P)).then_inc(consts, 16)
                sync.dma_start(rms_w[:, :], d["rms_w"].partition_broadcast(P)).then_inc(consts, 16)

                def load(g):
                    i = g % 2
                    sync.dma_start(qkd[i][:, :], chunk_rows(d["qkd"], g)).then_inc(first_in[i], 16)
                    for tile, name in ((u, "u"), (o, "qs")):
                        sync.dma_start(flat(tile[i][:, :, :]), chunk_rows(d[name], g)).then_inc(first_in[i], 16)
                    sync.dma_start(flat(gate[i][:, :, :]), chunk_rows(d["gate"], g)).then_inc(rows_in[i], 16)
                    if g >= 2:
                        sync.wait_ge(x_out[i], at(g // 2 * 16))
                    sync.dma_start(flat(x[i][:, :, :]), chunk_rows(d["x"], g)).then_inc(rows_in[i], 16)
                    sync.dma_start(ga[i][:, :], mod_row(d, 0, g, MOD_GA)).then_inc(rows_in[i], 16)

                load(0)
                load(1)
                for g in range(GROUPS):
                    sync.wait_ge(x_ready, at((g + 1) * T))
                    sync.dma_start(chunk_rows(d["x1"], g), flat(x[g % 2][:, :, :])).then_inc(x_out[g % 2], 16)
                    if g + 2 < GROUPS:
                        load(g + 2)
                for i in both:
                    sync.wait_ge(x_out[i], at(GROUPS // 2 * 16))

            @block.scalar
            def _(act):
                with act.Fori(0, GROUPS // 2) as r:
                    for parity in both:
                        g = r * 2 + parity
                        act.wait_ge(rows_in[parity], at((r + 1) * 48))
                        act.activation(gate[parity][:, :, :], gate[parity][:, :, :], ACT.Silu).then_inc(gate_silu, 1)
                        act.wait_ge(rms_ready, at(g + 1))
                        act.activation(rms[:, 1, :], rms[:, 0, :], ACT.Sqrt).then_inc(rms_rooted, 1)
                        for j in range(T):
                            act.wait_ge(turned, at(g * T + j + 1))
                            act.wait_ge(projected, at(g * T + j - 1 if j >= 2 else g * T))
                            act.copy(flat(oT[j % 2][:, :, :]), tr_ps[j % 2][:, 0:2 * P]).then_inc(oT_ready, 1)

            @block.gpsimd
            def _(pool):
                pool.wait_ge(consts, at(48))
                with pool.Fori(0, GROUPS // 2) as r:
                    for parity in both:
                        g = r * 2 + parity
                        pool.wait_ge(gate_silu, at(g + 1))
                        rows = gate[parity][:, :, :].rearrange("p t (h e) -> p (t h) e", e=HEAD)
                        pool.tensor_tensor(rows, rows, rms_w[:, :].unsqueeze(1).broadcast_to([P, T * HEADS, HEAD]), ALU.mult).then_inc(gate_scaled, 1)

            @block.tensor
            def _(pe):
                pe.wait_ge(consts, at(48))
                with pe.Fori(0, GROUPS // 2) as r:
                    for parity in both:
                        g = r * 2 + parity
                        for lag in range(T):
                            pe.wait_ge(product_ready, at(g * T + lag + 1))
                            for t in range(T - LATE, T, 2):
                                if t + 1 < lag:
                                    continue
                                skip = 1 if t < lag else 0
                                to = (t - (T - LATE) + skip) * DIM
                                mm = pe.matmul(late_ps[:, to:to + (2 - skip) * DIM], ident[:, :], scratch[lag % 2][:, (t + skip - lag) * DIM:(t + 2 - lag) * DIM],
                                               start=(lag == 0), stop=(lag == t + 1), skip_group_check=True)
                            mm.then_inc(summed, 1)
                        pe.wait_ge(o_ready, at(g + 1))
                        for j in range(T + 1):
                            if j < T:
                                pe.wait_ge(oT_ready, at(g * T + j - 1 if j >= 2 else g * T))
                                for k in range(HALVES):
                                    mm = pe.transpose(tr_ps[j % 2][:, k * P:(k + 1) * P], o[parity][:, j, k * P:(k + 1) * P], ident[:, :])
                                mm.then_inc(turned, 1)
                            if j > 0:
                                i = j - 1
                                pe.wait_ge(oT_ready, at(g * T + i + 1))
                                pe.wait_ge(y_used, at(g * T + i - 1 if i >= 2 else g * T))
                                for k in range(HALVES):
                                    mm = pe.matmul(y_ps[i % 2][:, 0:DIM], oT[i % 2][:, k, :], w_out[:, k, :], start=(k == 0), stop=(k == HALVES - 1))
                                mm.then_inc(projected, 1)

            @block.vector
            def _(vec):
                vec.wait_ge(consts, at(48))
                with vec.Fori(0, GROUPS // 2) as r:
                    for parity in both:
                        g = r * 2 + parity
                        seq = Chain(vec, order, g * VEC_STEPS)
                        seq.wait()
                        vec.wait_ge(first_in[parity], at((r + 1) * 48))
                        heads4 = lambda ap: ap.rearrange("p t (h e) -> p t h e", h=HEADS)
                        sc = [buf[:, :].rearrange("p (t f) -> p t f", t=T) for buf in scratch]
                        for lag in range(T):
                            n = T - lag
                            m = view(qkd[parity][:, :], [DIM + 1, n], [T, HEADS], [0, HEAD], offset=lag)
                            seq.wait()
                            vec.wait_ge(summed, at(g * T + lag - 1 if lag >= 2 else g * T))
                            seq.tell(vec.tensor_tensor(heads4(sc[lag % 2][:, 0:n, :]), heads4(u[parity][:, 0:n, :]), m, ALU.mult), product_ready, g * T + lag + 1)
                            if lag < T - LATE:
                                seq.wait()
                                seq.done(vec.tensor_tensor(o[parity][:, lag:T - LATE, :], o[parity][:, lag:T - LATE, :], sc[lag % 2][:, 0:T - LATE - lag, :], ALU.add))
                        vec.wait_ge(summed, at((g + 1) * T))
                        late = flat(o[parity][:, T - LATE:, :])
                        seq.done(vec.tensor_tensor(late, late, late_ps[:, :], ALU.add))
                        seq.wait()
                        seq.done(vec.tensor_tensor(sc[0], o[parity][:, :, :], o[parity][:, :, :], ALU.mult))
                        seq.wait()
                        seq.done(vec.tensor_reduce(rms[:, 0, :], scratch[0][:, :].rearrange("p (n e) -> p n e", e=HEAD), AX.X, ALU.add))
                        seq.wait()
                        seq.tell(vec.tensor_scalar(rms[:, 0, :], rms[:, 0, :], 1.0 / HEAD, 1e-6, ALU.mult, ALU.add), rms_ready, g + 1)
                        vec.wait_ge(rms_rooted, at(g + 1))
                        seq.done(vec.reciprocal(rms[:, 1, :], rms[:, 1, :]))
                        seq.wait()
                        seq.done(vec.tensor_tensor(heads4(o[parity][:, :, :]), heads4(o[parity][:, :, :]), spread(rms[:, 1, :].rearrange("p (t h) -> p t h", t=T), HEAD), ALU.mult))
                        seq.wait()
                        vec.wait_ge(gate_scaled, at(g + 1))
                        seq.tell(vec.tensor_tensor(o[parity][:, :, :], o[parity][:, :, :], gate[parity][:, :, :], ALU.mult), o_ready, g + 1)
                        vec.wait_ge(rows_in[parity], at((r + 1) * 48))
                        for j in range(T):
                            vec.wait_ge(projected, at(g * T + j + 1))
                            seq.tell(vec.tensor_tensor(gated[j % 2][:, :], y_ps[j % 2][:, 0:DIM], ga[parity][:, :], ALU.mult), y_used, g * T + j + 1)
                            seq.wait()
                            vec.tensor_tensor(x[parity][:, j, :], x[parity][:, j, :], gated[j % 2][:, :], ALU.add).then_inc(x_ready, 1)
                        vec.wait_ge(x_ready, at((g + 1) * T))
                        assert seq.steps == VEC_STEPS, seq.steps


EXPERTS, TOP, HIDDEN = 32, 8, 1024
HC = HIDDEN // P


def build_token_choice(nc, d, merged, chosen):
    T = CHUNK
    VEC_STEPS = 41
    with ExitStack() as ctx:
        sb = lambda name, shape: ctx.enter_context(nc.sbuf_tensor("tc_" + name, shape, F32))
        ps = lambda name, shape: ctx.enter_context(nc.psum_tensor("tc_" + name, shape, F32))
        sem = Semaphores(nc, ctx, "tc_")
        ident = sb("ident", [P, P])
        gate_w = sb("gate_w", [P, HALVES, EXPERTS])
        gate_b = sb("gate_b", [EXPERTS, 1])
        h = sb("h", [P, GROUPS, T, DIM])
        both = range(2)
        mod = [sb(f"mod{i}", [P, 2, DIM]) for i in both]
        hm = [sb(f"hm{i}", [P, T, DIM]) for i in both]
        stats = sb("stats", [P, T, 6])
        moments = sb("moments", [P, 3, T])
        ss = sb("scale_shift", [P, 2, T])
        hT = [sb(f"hT{i}", [P, HALVES, P]) for i in range(2)]
        probs = sb("probs", [EXPERTS, BATCH, SEQ])
        stat = sb("stat", [EXPERTS, BATCH, 4])
        top = sb("top", [EXPERTS, BATCH, TOP])
        chosen_T = sb("chosen_T", [P, GROUPS * T, EXPERTS])
        tr_ps = [ps(f"tr_ps{i}", [P, 512]) for i in range(2)]
        lg_ps = [ps(f"lg_ps{i}", [EXPERTS, 512]) for i in range(2)]
        ch_ps = [ps(f"ch_ps{i}", [P, 512]) for i in range(2)]
        mg_ps = ps("mg_ps", [P, BATCH, HALVES, EXPERTS])
        consts, order, var_ready, rooted, h_ready, turned, hT_ready = map(sem, (
            "consts", "order", "var_ready", "rooted", "h_ready", "turned", "hT_ready"))
        routed, logits_out, peak_ready, exp_done, chosen_ready, chosen_turned, chosen_copied, summed, merged_out = map(sem, (
            "routed", "logits_out", "peak_ready", "exp_done", "chosen_ready", "chosen_turned", "chosen_copied", "summed", "merged_out"))
        rows_in = [sem(f"rows_in{i}") for i in both]
        Q = 4

        sem.start()
        with nc.Block() as block:
            @block.sync
            def _(sync):
                sync.dma_start(ident[:, :], d["ident"]).then_inc(consts, 16)
                sync.dma_start(gate_w[:, :, :], d["gate0_wT"].rearrange("(k p) n -> p k n", p=P)).then_inc(consts, 16)
                sync.dma_start(gate_b[:, :], d["gate0_b"]).then_inc(consts, 16)
                for g in range(GROUPS):
                    i = g % 2
                    if g >= 2:
                        sync.wait_ge(turned, at((g - 1) * T))
                    sync.dma_start(flat(hm[i][:, :, :]), chunk_rows(d["x1"], g)).then_inc(rows_in[i], 16)
                    for n, m in enumerate((MOD_SB, MOD_CB)):
                        sync.dma_start(mod[i][:, n, :], mod_row(d, 0, g, m)).then_inc(rows_in[i], 16)

            @block.tensor
            def _(pe):
                pe.wait_ge(consts, at(48))
                with pe.Fori(0, GROUPS // 2) as r:
                    for parity in both:
                        g = r * 2 + parity
                        pe.wait_ge(h_ready, at(g + 1))
                        for j in range(T + 1):
                            if j < T:
                                pe.wait_ge(hT_ready, at(g * T + j - 1 if j >= 2 else g * T))
                                for k in range(HALVES):
                                    mm = pe.transpose(tr_ps[j % 2][:, k * P:(k + 1) * P], hm[parity][:, j, k * P:(k + 1) * P], ident[:, :])
                                mm.then_inc(turned, 1)
                            if j > 0:
                                i = j - 1
                                bank, place = i // Q, i % Q
                                pe.wait_ge(hT_ready, at(g * T + i + 1))
                                if place == 0:
                                    pe.wait_ge(logits_out, at(g * (T // Q) + bank - 1 if bank >= 2 else g * (T // Q)))
                                for k in range(HALVES):
                                    mm = pe.matmul(lg_ps[bank % 2][:, place * P:(place + 1) * P], gate_w[:, k, :], hT[i % 2][:, k, :],
                                                   start=(k == 0), stop=(k == HALVES - 1))
                                mm.then_inc(routed, 1)
                for b in range(BATCH):
                    pe.wait_ge(chosen_ready, at(b + 1))
                    for gg in range(GROUPS_PER_BATCH):
                        n = b * GROUPS_PER_BATCH + gg
                        if n >= 2:
                            pe.wait_ge(chosen_copied, at(n - 1))
                        for j in range(T):
                            mm = pe.transpose(ch_ps[n % 2][:, j * EXPERTS:(j + 1) * EXPERTS],
                                              chosen[:, b, gg * P * T + j:(gg + 1) * P * T:T], ident[0:EXPERTS, 0:EXPERTS])
                        mm.then_inc(chosen_turned, 1)
                for b in range(BATCH):
                    pe.wait_ge(chosen_copied, at((b + 1) * GROUPS_PER_BATCH))
                    for k in range(HALVES):
                        tiles = GROUPS_PER_BATCH * T
                        for n in range(tiles):
                            gg, j = b * GROUPS_PER_BATCH + n // T, n % T
                            mm = pe.matmul(mg_ps[:, b, k, :], h[:, gg, j, k * P:(k + 1) * P], chosen_T[:, gg * T + j, :],
                                           start=(n == 0), stop=(n == tiles - 1), skip_group_check=True)
                mm.then_inc(summed, 1)

            @block.scalar
            def _(act):
                act.wait_ge(consts, at(48))
                with act.Fori(0, GROUPS // 2) as r:
                    for parity in both:
                        g = r * 2 + parity
                        act.wait_ge(var_ready, at(g + 1))
                        act.activation(ss[:, 1, :], ss[:, 0, :], ACT.Sqrt).then_inc(rooted, 1)
                        for j in range(T):
                            act.wait_ge(turned, at(g * T + j + 1))
                            act.wait_ge(routed, at(g * T + j - 1 if j >= 2 else g * T))
                            act.copy(flat(hT[j % 2][:, :, :]), tr_ps[j % 2][:, 0:2 * P]).then_inc(hT_ready, 1)
                            if j % Q == Q - 1:
                                bank = j // Q
                                act.wait_ge(routed, at(g * T + j + 1))
                                out = probs[:, :, :].rearrange("e b s -> e (b s)")[:, bass.ds(g * (P * T) + bank * Q, (P - 1) * T + Q)]
                                out = AP(out.tensor, out.offset, [list(out.ap[0]), [1, Q], [T, P]])
                                act.activation(out, lg_ps[bank % 2][:, :].rearrange("e (q p) -> e q p", q=Q), ACT.Identity, bias=gate_b[:, :]).then_inc(logits_out, 1)
                for b in range(BATCH):
                    act.wait_ge(peak_ready, at(b + 1))
                    act.activation(probs[:, b, :], probs[:, b, :], ACT.Exp, bias=stat[:, b, 0:1], accum_out=stat[:, b, 1:2]).then_inc(exp_done, 1)
                for n in range(GROUPS):
                    act.wait_ge(chosen_turned, at(n + 1))
                    act.copy(chosen_T[:, n * T:(n + 1) * T, :].rearrange("p t e -> p (t e)"), ch_ps[n % 2][:, :]).then_inc(chosen_copied, 1)
                act.wait_ge(summed, at(1))
                for b in range(BATCH):
                    for k in range(HALVES):
                        act.copy(merged[:, k, :, b], mg_ps[:, b, k, :]).then_inc(merged_out, 1)
                act.wait_ge(merged_out, at(BATCH * HALVES))

            @block.vector
            def _(vec):
                with vec.Fori(0, GROUPS // 2) as r:
                    for parity in both:
                        g = r * 2 + parity
                        seq = Chain(vec, order, g * VEC_STEPS)
                        seq.wait()
                        vec.wait_ge(rows_in[parity], at((r + 1) * 48))
                        layernorm_steps(vec, seq, hm[parity][:, :, :], stats, moments, ss, T, rooted, g + 1, var_ready, g + 1)
                        seq.wait()
                        seq.done(vec.tensor_tensor(hm[parity][:, :, :], hm[parity][:, :, :], mod[parity][:, 1:2, :].broadcast_to([P, T, DIM]), ALU.mult))
                        seq.wait()
                        seq.done(vec.tensor_tensor(hm[parity][:, :, :], hm[parity][:, :, :], mod[parity][:, 0:1, :].broadcast_to([P, T, DIM]), ALU.add))
                        seq.wait()
                        seq.tell(vec.tensor_copy(h[:, bass.ds(g, 1), :, :].rearrange("p a t f -> p (a t f)"), flat(hm[parity][:, :, :])), h_ready, g + 1)
                        assert seq.steps == VEC_STEPS, seq.steps
                vec.wait_ge(logits_out, at(GROUPS * T // Q))
                for b in range(BATCH):
                    vec.tensor_reduce(stat[:, b, 0:1], probs[:, b, :], AX.X, ALU.max, negate=True).then_inc(peak_ready, 1)
                seq = Chain(vec, order, GROUPS * VEC_STEPS)
                for b in range(BATCH):
                    vec.wait_ge(exp_done, at(b + 1))
                    seq.done(vec.reciprocal(stat[:, b, 2:3], stat[:, b, 1:2]))
                    seq.wait()
                    seq.done(vec.tensor_scalar(probs[:, b, :], probs[:, b, :], stat[:, b, 2:3], None, ALU.mult))
                    seq.wait()
                    seq.done(vec.max(top[:, b, :], probs[:, b, :]))
                    seq.wait()
                    seq.done(vec.match_replace(chosen[:, b, :], top[:, b, :], probs[:, b, :], 0.0))
                    seq.wait()
                    seq.tell(vec.tensor_tensor(chosen[:, b, :], probs[:, b, :], chosen[:, b, :], ALU.subtract), chosen_ready, b + 1)


def build_experts(nc, d, merged, expert_out):
    DEPTH = 4
    with ExitStack() as ctx:
        sb = lambda name, shape: ctx.enter_context(nc.sbuf_tensor("ex_" + name, shape, F32))
        ps = lambda name, shape: ctx.enter_context(nc.psum_tensor("ex_" + name, shape, F32))
        sem = Semaphores(nc, ctx, "ex_")
        ident = sb("ident", [P, P])
        w1 = [sb(f"w1_{i}", [P, HALVES, HIDDEN]) for i in range(DEPTH)]
        w2 = [sb(f"w2_{i}", [P, HC, DIM]) for i in range(DEPTH)]
        w1_bias = sb("w1_bias", [P, EXPERTS, HC])
        w2_bias = sb("w2_bias", [EXPERTS, DIM])
        hidden = [sb(f"hidden{i}", [P, HC, BATCH]) for i in range(2)]
        gelu = [sb(f"gelu{i}", [P, HC, BATCH]) for i in range(2)]
        picked = sb("picked", [P, 2, HALVES, BATCH])
        rows_ready, rows_turned, picked_ready = map(sem, ("rows_ready", "rows_turned", "picked_ready"))
        passed = sem("passed")
        outs = sb("outs", [BATCH, EXPERTS, DIM])
        rows = [sb(f"rows{i}", [BATCH, HIDDEN]) for i in range(2)]
        rows_ps = [ps(f"rows_ps{i}", [BATCH, HIDDEN]) for i in range(2)]
        h_ps = [ps(f"h_ps{i}", [P, HC, BATCH]) for i in range(2)]
        o_ps = [ps(f"o_ps{i}", [BATCH, DIM]) for i in range(2)]
        consts, w1_done, h_ready, gelu_ready, w2_done, outs_ready, outs_turned, finished = map(sem, (
            "consts", "w1_done", "h_ready", "gelu_ready", "w2_done", "outs_ready", "outs_turned", "finished"))
        w1_in = [sem(f"w1_in{i}") for i in range(DEPTH)]
        w2_in = [sem(f"w2_in{i}") for i in range(DEPTH)]
        ROUNDS = EXPERTS // DEPTH

        sem.start()
        with nc.Block() as block:
            @block.sync
            def _(sync):
                sync.dma_start(ident[:, :], d["ident"]).then_inc(consts, 16)
                sync.dma_start(w1_bias[:, :, :], d["w1_bias"]).then_inc(consts, 16)
                sync.dma_start(w2_bias[:, :], d["w2_all"][:, HIDDEN, :]).then_inc(consts, 16)

                def load_w1(e, i):
                    sync.dma_start(w1[i][:, :, :], d["w1_all"][bass.ds(e, 1), 0:DIM, :].rearrange("a (k p) n -> (a p) k n", p=P)).then_inc(w1_in[i], 16)

                def load_w2(e, i):
                    sync.dma_start(w2[i][:, :, :], d["w2_all"][bass.ds(e, 1), 0:HIDDEN, :].rearrange("a (p c) n -> (a p) c n", p=P)).then_inc(w2_in[i], 16)

                for i in range(DEPTH):
                    load_w1(i, i)
                    load_w2(i, i)
                with sync.Fori(0, ROUNDS - 1) as r:
                    for i in range(DEPTH):
                        sync.wait_ge(w1_done, at(r * DEPTH + i + 1))
                        load_w1((r + 1) * DEPTH + i, i)
                        sync.wait_ge(w2_done, at(r * DEPTH + i + 1))
                        load_w2((r + 1) * DEPTH + i, i)
                sync.wait_ge(outs_ready, at(EXPERTS))
                for b in range(BATCH):
                    sync.dma_start(expert_out[:, b, :], outs[b:b + 1, :, :]).then_inc(outs_turned, 16)

            @block.tensor
            def _(pe):
                pe.wait_ge(consts, at(48))
                with pe.Fori(0, ROUNDS) as r:
                    for i in range(DEPTH + 2):
                        if i < DEPTH:
                            e = r * DEPTH + i
                            pe.wait_ge(w1_in[i], at((r + 1) * 16))
                            pe.wait_ge(picked_ready, at(r * DEPTH + i + 1))
                            pe.wait_ge(rows_ready, at(r * DEPTH + i - 1 if i >= 2 else r * DEPTH))
                            for n in range(HIDDEN // 512):
                                for k in range(HALVES):
                                    mm = pe.matmul(rows_ps[i % 2][:, n * 512:(n + 1) * 512], picked[:, i % 2, k, :], w1[i][:, k, n * 512:(n + 1) * 512],
                                                   start=(k == 0), stop=(k == HALVES - 1))
                            mm.then_inc(w1_done, 1)
                        if 0 < i <= DEPTH:
                            n = i - 1
                            pe.wait_ge(rows_ready, at(r * DEPTH + n + 1))
                            pe.wait_ge(h_ready, at(r * DEPTH + n - 1 if n >= 2 else r * DEPTH))
                            pe.sem_inc(passed, 1)
                            for c in range(HC):
                                mm = pe.transpose(h_ps[n % 2][:, c, :], rows[n % 2][:, c:HIDDEN:HC], ident[0:BATCH, 0:BATCH])
                            mm.then_inc(rows_turned, 1)
                        if i > 1:
                            n = i - 2
                            pe.wait_ge(w2_in[n], at((r + 1) * 16))
                            pe.wait_ge(gelu_ready, at(r * DEPTH + n + 1))
                            pe.wait_ge(outs_ready, at(r * DEPTH + n - 1 if n >= 2 else r * DEPTH))
                            for c in range(HC):
                                mm = pe.matmul(o_ps[n % 2][:, :], gelu[n % 2][:, c, :], w2[n][:, c, :], start=(c == 0), stop=(c == HC - 1))
                            mm.then_inc(w2_done, 1)

            @block.scalar
            def _(act):
                with act.Fori(0, ROUNDS) as r:
                    for i in range(DEPTH):
                        act.wait_ge(w1_done, at(r * DEPTH + i - 1 if i >= 2 else r * DEPTH))
                        act.copy(picked[:, i % 2, :, :], merged[:, :, bass.ds(r * DEPTH + i, 1), :].rearrange("p k a b -> p k (a b)")).then_inc(picked_ready, 1)
                    for i in range(DEPTH):
                        act.wait_ge(h_ready, at(r * DEPTH + i + 1))
                        act.wait_ge(w2_done, at(r * DEPTH + i - 1 if i >= 2 else r * DEPTH))
                        act.activation(gelu[i % 2][:, :, :], hidden[i % 2][:, :, :], ACT.Gelu).then_inc(gelu_ready, 1)

            @block.vector
            def _(vec):
                vec.wait_ge(consts, at(48))
                with vec.Fori(0, ROUNDS) as r:
                    for i in range(DEPTH + 2):
                        if i < DEPTH:
                            vec.wait_ge(w1_done, at(r * DEPTH + i + 1))
                            vec.wait_ge(rows_turned, at(r * DEPTH + i - 1 if i >= 2 else r * DEPTH))
                            vec.tensor_copy(rows[i % 2][:, :], rows_ps[i % 2][:, :]).then_inc(rows_ready, 1)
                        if 0 < i <= DEPTH:
                            n = i - 1
                            vec.wait_ge(rows_turned, at(r * DEPTH + n + 1))
                            vec.wait_ge(gelu_ready, at(r * DEPTH + n - 1 if n >= 2 else r * DEPTH))
                            vec.tensor_tensor(hidden[n % 2][:, :, :], h_ps[n % 2][:, :, :],
                                              spread(w1_bias[:, bass.ds(r * DEPTH + n, 1), :].rearrange("p a c -> p (a c)"), BATCH), ALU.add).then_inc(h_ready, 1)
                        if i > 1:
                            n = i - 2
                            vec.wait_ge(w2_done, at(r * DEPTH + n + 1))
                            vec.tensor_copy(outs[:, bass.ds(r * DEPTH + n, 1), :].rearrange("b a f -> b (a f)"), o_ps[n % 2][:, :]).then_inc(outs_ready, 1)
                vec.wait_ge(outs_turned, at(16 * BATCH))
                for b in range(BATCH):
                    vec.tensor_tensor(expert_out[:, b, :], expert_out[:, b, :], w2_bias[:, :], ALU.add).then_inc(finished, 1)
                vec.wait_ge(finished, at(BATCH))


def build_scatter(nc, d, chosen, expert_out):
    T = CHUNK
    with ExitStack() as ctx:
        sb = lambda name, shape: ctx.enter_context(nc.sbuf_tensor("sc_" + name, shape, F32))
        ps = lambda name, shape: ctx.enter_context(nc.psum_tensor("sc_" + name, shape, F32))
        sem = Semaphores(nc, ctx, "sc_")
        x = [sb(f"x{i}", [P, T, DIM]) for i in range(2)]
        gb = [sb(f"gb{i}", [P, DIM]) for i in range(2)]
        weights = [sb(f"weights{i}", [EXPERTS, P * T]) for i in range(2)]
        outs = [sb(f"outs{i}", [EXPERTS, DIM]) for i in range(2)]
        gated = [sb(f"gated{i}", [P, 2, DIM]) for i in range(2)]
        y_ps = [ps(f"y_ps{i}", [P, 2, DIM]) for i in range(2)]
        copied, summed, y_used, x_ready = map(sem, ("copied", "summed", "y_used", "x_ready"))
        rows_in = [sem(f"rows_in{i}") for i in range(2)]
        x_out = [sem(f"x_out{i}") for i in range(2)]
        PAIRS_OF_TILES = T // 2
        ROUNDS = GROUPS // 2

        sem.start()
        with nc.Block() as block:
            @block.sync
            def _(sync):
                with sync.Fori(0, ROUNDS) as r:
                    for i in range(2):
                        g = r * 2 + i
                        sync.wait_ge(x_out[i], at(r * 16))
                        sync.dma_start(flat(x[i][:, :, :]), chunk_rows(d["x1"], g)).then_inc(rows_in[i], 16)
                        sync.dma_start(gb[i][:, :], mod_row(d, 0, g, MOD_GB)).then_inc(rows_in[i], 16)
                    for i in range(2):
                        g = r * 2 + i
                        sync.wait_ge(x_ready, at((g + 1) * PAIRS_OF_TILES))
                        sync.dma_start(chunk_rows(d["x2"], g), flat(x[i][:, :, :])).then_inc(x_out[i], 16)
                for i in range(2):
                    sync.wait_ge(x_out[i], at(ROUNDS * 16))

            @block.scalar
            def _(act):
                with act.Fori(0, ROUNDS) as r:
                    for i in range(2):
                        g = r * 2 + i
                        act.wait_ge(summed, at(r * 2 * PAIRS_OF_TILES))
                        act.copy(weights[i][:, :], chosen[:, :, :].rearrange("e b s -> e (b s)")[:, bass.ds(g * (P * T), P * T)]).then_inc(copied, 1)
                        act.copy(outs[i][:, :], expert_out[:, bass.ds(r, 1), :].rearrange("e b f -> e (b f)")).then_inc(copied, 1)

            @block.tensor
            def _(pe):
                with pe.Fori(0, ROUNDS) as r:
                    for i in range(2):
                        g = r * 2 + i
                        pe.wait_ge(copied, at((g + 1) * 2))
                        for jj in range(PAIRS_OF_TILES):
                            n = g * PAIRS_OF_TILES + jj
                            pe.wait_ge(y_used, at(n - 1 if jj >= 2 else g * PAIRS_OF_TILES))
                            for s in range(2):
                                j = jj * 2 + s
                                mm = pe.matmul(y_ps[jj % 2][:, s, :], weights[i][:, j:P * T:T], outs[i][:, :], start=True, stop=True)
                            mm.then_inc(summed, 1)

            @block.vector
            def _(vec):
                with vec.Fori(0, ROUNDS) as r:
                    for i in range(2):
                        g = r * 2 + i
                        vec.wait_ge(rows_in[i], at((r + 1) * 32))
                        for jj in range(PAIRS_OF_TILES):
                            n = g * PAIRS_OF_TILES + jj
                            vec.wait_ge(summed, at(n + 1))
                            vec.tensor_tensor(gated[jj % 2][:, :, :], y_ps[jj % 2][:, :, :], gb[i][:, :].unsqueeze(1).broadcast_to([P, 2, DIM]), ALU.mult).then_inc(y_used, 1)
                            vec.wait_ge(y_used, at(n + 1))
                            vec.tensor_tensor(x[i][:, jj * 2:jj * 2 + 2, :], x[i][:, jj * 2:jj * 2 + 2, :], gated[jj % 2][:, :, :], ALU.add).then_inc(x_ready, 1)


WINDOW, TOPK, PHRASE = 64, 16, 32
SPAN = WINDOW + P
NT = 4
STEP = NT * P
STEPS = SEQ // STEP
ALL_STEPS = BATCH * STEPS
NEG = -1e30
TAKEN = -3e38

FFN_EXPERTS, ALL_EXPERTS, DFF = 8, 12, 512
FC = DFF // P
TILES = TOKENS // P
PICKS = 2
SLOT_TILES = PICKS * TILES + FFN_EXPERTS
SLOTS = SLOT_TILES * P
ZERO_TILES = 4
NO_SLOT = float(1 << 20)
INT = mybir.dt.uint32


def step_rows(dram, step):
    return dram.rearrange("(s n p) f -> s p n f", n=NT, p=P)[bass.ds(step, 1)].rearrange("a p n f -> (a p) n f")


def step_mod(d, step, m):
    return d["mod_steps"][bass.ds(step, 1), m * DIM:(m + 1) * DIM].rearrange("a f -> (a f)").partition_broadcast(P)


def run_steps(engine, step):
    for i in range(2):
        step(i, i, 0, True, True)
    with engine.Fori(1, ALL_STEPS // 2 - 1) as r:
        for i in range(2):
            step(r * 2 + i, i, r, True, True)
    for i in range(2):
        step(ALL_STEPS - 2 + i, i, ALL_STEPS // 2 - 1, i == 0, False)


def is_first(it):
    return isinstance(it, int) and it == 0


def build_window_attention(nc, d, logits):
    NORM_STEPS, CARRY_STEPS = 16, 1
    MOMENT_STEPS, SCALE_STEPS = 10, 6
    VEC_STEPS = 54 + MOMENT_STEPS + SCALE_STEPS
    WIDE = 8
    with ExitStack() as ctx:
        sb = lambda name, shape, dt=F32: ctx.enter_context(nc.sbuf_tensor("wa_" + name, shape, dt))
        ps = lambda name, shape: ctx.enter_context(nc.psum_tensor("wa_" + name, shape, F32))
        sem = Semaphores(nc, ctx, "wa_")
        ident = sb("ident", [P, P])
        ones = sb("ones", [P, 1])
        means = sb("means", [P, P])
        nears = sb("nears", [P, SPAN])
        w_cols = sb("w_cols", [P, 3, HALVES, DIM])
        w_rows = sb("w_rows", [P, 2, HALVES, DIM])
        col_bias = sb("col_bias", [P, 3, HALVES])
        row_bias = sb("row_bias", [P, 2 * DIM])
        band = sb("band", [P, ALL_STEPS, SPAN])
        keep = sb("keep", [P, ALL_STEPS])
        both = range(2)
        mod = [sb(f"mod{i}", [P, 2, DIM]) for i in both]
        ga = [sb(f"ga{i}", [P, DIM]) for i in both]
        x = [sb(f"x{i}", [P, NT, DIM]) for i in both]
        h = [sb(f"h{i}", [P, NT, DIM]) for i in both]
        h3 = sb("h3", [P, NT, DIM])
        h3T = sb("h3T", [P, HALVES, STEP])
        mod3 = [sb(f"mod3_{i}", [P, 2, DIM]) for i in both]
        moments3 = sb("moments3", [P, 3, NT])
        ss3 = sb("scale_shift3", [P, 2, NT])
        zeros = sb("zeros", [P, ZERO_TILES * DIM])
        gate_w = sb("gate_w", [P, HALVES, ALL_EXPERTS])
        gate_b = sb("gate_b", [P, ALL_EXPERTS])
        stats = sb("stats", [P, NT, 6])
        moments = sb("moments", [P, 3, NT])
        ss = sb("scale_shift", [P, 2, NT])
        hT = sb("hT", [P, HALVES, STEP])
        phT = sb("phT", [P, HALVES, 1 + STEP])
        qT = [sb(f"qT{i}", [P, HALVES, STEP]) for i in both]
        pT = [sb(f"pT{i}", [P, HALVES, STEP]) for i in both]
        kT = [sb(f"kT{i}", [P, HALVES, WINDOW + STEP]) for i in both]
        v = [sb(f"v{i}", [P, 1 + NT, 2 * DIM]) for i in both]
        scores = [sb(f"scores{i}", [P, SPAN]) for i in range(NT)]
        rest = [sb(f"rest{i}", [P, 2, SPAN]) for i in range(NT)]
        exps = [sb(f"exps{i}", [P, 2, SPAN]) for i in range(NT)]
        probs = [sb(f"probs{i}", [P, 2 * P]) for i in range(2)]
        probs_T = [sb(f"probs_T{i}", [P, 2, P]) for i in range(2)]
        top = [sb(f"top{i}", [P, 2, 8]) for i in range(NT)]
        one = [sb(f"one{i}", [P, 8]) for i in range(NT)]
        out = [sb(f"out{i}", [P, DIM]) for i in range(2)]
        PH, MAX, WPH, SUM, INV = range(5)
        tr_ps = ps("tr_ps", [P, 512])
        wide_ps = [ps(f"wide_ps{i}", [P, 512]) for i in range(2)]
        v_ps = [tr_ps, ps("v_ps", [P, 512])]
        o_ps = ps("o_ps", [P, 512])
        sc_ps = [ps(f"sc_ps{i}", [P, 512]) for i in range(2)]
        pt_ps = ps("pt_ps", [P, 512])
        consts, cleared, order, var_ready, rooted, h_ready = map(sem, ("consts", "cleared", "order", "var_ready", "rooted", "h_ready"))
        h_in, x_in, x_out = ([sem(f"{n}{i}") for i in both] for n in ("h_in", "x_in", "x_out"))
        turned, hT_ready, wide_done, wide_out, carried, v_done, v_used, o_done, o_used = map(sem, (
            "turned", "hT_ready", "wide_done", "wide_out", "carried", "v_done", "v_used", "o_done", "o_used"))
        products_ready, scored, sc_used, rest_ready, exp_done, near_done, probs_ready, probs_turned, probs_T_ready, x_ready = map(sem, (
            "products_ready", "scored", "sc_used", "rest_ready", "exp_done", "near_done", "probs_ready", "probs_turned", "probs_T_ready", "x_ready"))
        passed = sem("passed")
        CONSTS = 16 * 15
        CLEARED = 8
        var3_ready, rooted3, h3_ready, h3_out, h3_turned, h3T_ready, routed, logits_used, zeros_ready, zeroed = map(sem, (
            "var3_ready", "rooted3", "h3_ready", "h3_out", "h3_turned", "h3T_ready", "routed", "logits_used", "zeros_ready", "zeroed"))

        sem.start()
        with nc.Block() as block:
            @block.sync
            def _(sync):
                for tile, name in ((ident, "ident"), (ones, "ones"), (means, "means"), (nears, "nears"), (col_bias, "col_bias"),
                                   (band, "band"), (keep, "keep")):
                    sync.dma_start(tile[tuple([slice(None)] * len(tile.shape))], d[name]).then_inc(consts, 16)
                for n in range(3):
                    sync.dma_start(w_cols[:, n, :, :], d["w_cols"][n].rearrange("(k p) f -> p k f", p=P)).then_inc(consts, 16)
                for n in range(2):
                    sync.dma_start(w_rows[:, n, :, :], d["w_rows"][n].rearrange("(k p) f -> p k f", p=P)).then_inc(consts, 16)
                sync.dma_start(row_bias[:, :], d["row_bias"].partition_broadcast(P)).then_inc(consts, 16)
                sync.dma_start(gate_w[:, :, :], d["gate1_wT"].rearrange("(k p) f -> p k f", p=P)).then_inc(consts, 16)
                sync.dma_start(gate_b[:, :], d["gate1_b"].partition_broadcast(P)).then_inc(consts, 16)

                def load_h(it, i):
                    sync.dma_start(h[i][:, :, :], step_rows(d["x2"], it)).then_inc(h_in[i], 16)
                    for n, m in enumerate((MOD_SA, MOD_CA)):
                        sync.dma_start(mod[i][:, n, :], step_mod(d, it, m)).then_inc(h_in[i], 16)

                def load_x(it, i):
                    sync.dma_start(x[i][:, :, :], step_rows(d["x2"], it)).then_inc(x_in[i], 16)
                    sync.dma_start(ga[i][:, :], step_mod(d, it, MOD_GA)).then_inc(x_in[i], 16)
                    for n, m in enumerate((MOD_SB, MOD_CB)):
                        sync.dma_start(mod3[i][:, n, :], step_mod(d, it, m)).then_inc(x_in[i], 16)

                def step(it, i, r, front, norm):
                    if norm:
                        sync.wait_ge(wide_done, at(it * WIDE + HALVES))
                        load_h(it + 2, i)
                    if not is_first(it):
                        sync.wait_ge(h3_ready, at(it))
                        sync.dma_start(step_rows(d["h3"], it - 1), h3[:, :, :]).then_inc(h3_out, 16)
                    if front:
                        sync.wait_ge(x_out[1 - i], at((r + i) * 16))
                        load_x(it + 1, 1 - i)
                    sync.wait_ge(x_ready, at((it + 1) * NT))
                    sync.dma_start(step_rows(d["x3"], it), x[i][:, :, :]).then_inc(x_out[i], 16)

                load_h(0, 0)
                load_h(1, 1)
                load_x(0, 0)
                run_steps(sync, step)
                sync.wait_ge(h3_ready, at(ALL_STEPS))
                sync.dma_start(step_rows(d["h3"], ALL_STEPS - 1), h3[:, :, :]).then_inc(h3_out, 16)
                for i in both:
                    sync.wait_ge(x_out[i], at(ALL_STEPS // 2 * 16))
                sync.wait_ge(h3_out, at(ALL_STEPS * 16))

            @block.tensor
            def _(pe):
                pe.wait_ge(consts, at(CONSTS))
                pe.wait_ge(cleared, at(CLEARED))

                def turn(it, i):
                    pe.wait_ge(v_used, at(it * NT))
                    pe.wait_ge(h_ready, at(it + 1))
                    for n in range(NT // 2):
                        pe.wait_ge(hT_ready, at(it * (NT // 2) + n))
                        for k in range(HALVES):
                            for t in range(2):
                                mm = pe.transpose(tr_ps[:, (k * 2 + t) * P:(k * 2 + t + 1) * P], h[i][:, n * 2 + t, k * P:(k + 1) * P], ident[:, :])
                        mm.then_inc(turned, 1)

                def wide(it, i, n):
                    pe.wait_ge(wide_out, at(it * WIDE + n - 1 if n >= 2 else it * WIDE))
                    bank = wide_ps[n % 2]
                    if n < HALVES:
                        for j in range(NT):
                            mm = pe.matmul(bank[:, j * P:(j + 1) * P], h[i][:, j, n * P:(n + 1) * P], means[:, :], start=True, stop=True)
                    else:
                        which, m = (n - 2) // 2, n % 2
                        if n == 2:
                            pe.wait_ge(hT_ready, at((it + 1) * (NT // 2)))
                        moving = phT if which == 2 else hT
                        for k in range(HALVES):
                            mm = pe.matmul(bank[:, :], w_cols[:, which, k, m * P:(m + 1) * P], moving[:, k, 0:STEP], start=(k == 0), stop=(k == HALVES - 1))
                    mm.then_inc(wide_done, 1)

                def values(it, j):
                    pe.wait_ge(v_used, at(it * NT + j - 1 if j >= 2 else it * NT))
                    for which, src in ((0, hT), (1, phT)):
                        for k in range(HALVES):
                            mm = pe.matmul(v_ps[j % 2][:, which * DIM:(which + 1) * DIM], src[:, k, j * P:(j + 1) * P], w_rows[:, which, k, :],
                                           start=(k == 0), stop=(k == HALVES - 1))
                    mm.then_inc(v_done, 1)

                def score(it, i, j):
                    pe.wait_ge(sc_used, at(it * NT + j - 1 if j >= 2 else it * NT))
                    for k in range(HALVES):
                        pe.matmul(sc_ps[j % 2][:, 0:SPAN], qT[i][:, k, j * P:(j + 1) * P], kT[i][:, k, j * P:j * P + SPAN], start=(k == 0), stop=(k == HALVES - 1))
                    if j == 0:
                        pe.wait_ge(products_ready, at(it + 1))
                    for k in range(HALVES):
                        mm = pe.matmul(sc_ps[j % 2][:, SPAN:SPAN + 1], pT[i][:, k, j * P:(j + 1) * P], ones[:, :], start=(k == 0), stop=(k == HALVES - 1))
                    mm.then_inc(scored, 1)

                def turn_h3(it, steps_used):
                    pe.wait_ge(v_used, at(steps_used * NT))
                    pe.wait_ge(h3_ready, at(it + 1))
                    for n in range(NT // 2):
                        pe.wait_ge(h3T_ready, at(it * (NT // 2) + n))
                        for k in range(HALVES):
                            for t in range(2):
                                mm = pe.transpose(tr_ps[:, (k * 2 + t) * P:(k * 2 + t + 1) * P], h3[:, n * 2 + t, k * P:(k + 1) * P], ident[:, :])
                        mm.then_inc(h3_turned, 1)

                def expert_logits(it):
                    pe.wait_ge(h3T_ready, at((it + 1) * (NT // 2)))
                    for j in range(NT):
                        for k in range(HALVES):
                            mm = pe.matmul(v_ps[1][:, j * ALL_EXPERTS:(j + 1) * ALL_EXPERTS], h3T[:, k, j * P:(j + 1) * P], gate_w[:, k, :],
                                           start=(k == 0), stop=(k == HALVES - 1), skip_group_check=True)
                    mm.then_inc(routed, 1)

                def step(it, i, r, front, norm):
                    pe.wait_ge(wide_out, at((it + 1) * WIDE))
                    score(it, i, 0)
                    score(it, i, 1)
                    if front:
                        turn(it + 1, 1 - i)
                        wide(it + 1, 1 - i, 0)
                        wide(it + 1, 1 - i, 1)
                    score(it, i, 2)
                    for j in range(NT):
                        pe.wait_ge(probs_ready, at(it * NT + j + 1))
                        pe.wait_ge(probs_T_ready, at(it * NT + j))
                        for c in range(2):
                            mm = pe.transpose(pt_ps[:, c * P:(c + 1) * P], probs[j % 2][:, c * P:(c + 1) * P], ident[:, :])
                        mm.then_inc(probs_turned, 1)
                        if j == 0:
                            score(it, i, 3)
                        if front and j < NT - 1:
                            wide(it + 1, 1 - i, 2 * j + 2)
                            wide(it + 1, 1 - i, 2 * j + 3)
                        elif front:
                            for n in range(NT):
                                if n == 1 and not is_first(it):
                                    pe.wait_ge(logits_used, at(it))
                                values(it + 1, n)
                        if j == 1 and not is_first(it):
                            turn_h3(it - 1, it + 1)
                        if j == 2 and not is_first(it):
                            expert_logits(it - 1)
                        pe.wait_ge(v_used, at((it + 1) * NT))
                        pe.wait_ge(o_used, at(it * NT + j))
                        pe.wait_ge(probs_T_ready, at(it * NT + j + 1))
                        for c in range(2):
                            mm = pe.matmul(o_ps[:, 0:DIM], probs_T[j % 2][:, c, :], v[i][:, j + c, 0:DIM], start=(c == 0), stop=(c == 1))
                        mm.then_inc(o_done, 1)

                turn(0, 0)
                for n in range(WIDE):
                    wide(0, 0, n)
                for j in range(NT):
                    values(0, j)
                run_steps(pe, step)
                turn_h3(ALL_STEPS - 1, ALL_STEPS)
                expert_logits(ALL_STEPS - 1)

            @block.scalar
            def _(act):
                act.wait_ge(consts, at(CONSTS))
                act.wait_ge(cleared, at(CLEARED))

                def root(it):
                    act.wait_ge(var_ready, at(it + 1))
                    act.activation(ss[:, 1, :], ss[:, 0, :], ACT.Sqrt).then_inc(rooted, 1)

                def root3(it):
                    act.wait_ge(var3_ready, at(it + 1))
                    act.activation(ss3[:, 1, :], ss3[:, 0, :], ACT.Sqrt).then_inc(rooted3, 1)

                def copy_h3(it):
                    for n in range(NT // 2):
                        act.wait_ge(h3_turned, at(it * (NT // 2) + n + 1))
                        act.copy(h3T[:, :, n * 2 * P:(n + 1) * 2 * P], tr_ps[:, :].rearrange("p (k t) -> p k t", k=HALVES)).then_inc(h3T_ready, 1)

                def copy_turned(it):
                    for n in range(NT // 2):
                        act.wait_ge(turned, at(it * (NT // 2) + n + 1))
                        act.copy(hT[:, :, n * 2 * P:(n + 1) * 2 * P], tr_ps[:, :].rearrange("p (k t) -> p k t", k=HALVES)).then_inc(hT_ready, 1)

                def carry(it, i):
                    act.copy(phT[:, :, 0:1], phT[:, :, STEP:STEP + 1]).then_inc(carried, 1)
                    act.copy(kT[i][:, :, 0:WINDOW], kT[1 - i][:, :, STEP:STEP + WINDOW]).then_inc(carried, 1)
                    act.wait_ge(carried, at((it + 1) * 2))

                def copy_wide(it, i, n):
                    act.wait_ge(wide_done, at(it * WIDE + n + 1))
                    m = n % 2
                    if n < 2:
                        ins = act.copy(phT[:, m, 1:1 + STEP], wide_ps[m][:, :])
                    else:
                        which = (n - 2) // 2
                        to = (qT[i][:, m, :], kT[i][:, m, WINDOW:WINDOW + STEP], pT[i][:, m, :])[which]
                        ins = act.activation(to, wide_ps[m][:, :], ACT.Identity, bias=col_bias[:, which, m:m + 1])
                    ins.then_inc(wide_out, 1)

                def exponents(it, j):
                    act.wait_ge(rest_ready, at(it * NT + j + 1))
                    act.activation(exps[j][:, 0, :], scores[j][:, :], ACT.Exp, bias=one[j][:, MAX:MAX + 1])
                    act.activation(exps[j][:, 1, :], rest[j][:, 1, :], ACT.Exp, bias=one[j][:, MAX:MAX + 1])
                    act.activation(one[j][:, WPH:WPH + 1], one[j][:, PH:PH + 1], ACT.Exp, bias=one[j][:, MAX:MAX + 1]).then_inc(exp_done, 1)

                def step(it, i, r, front, norm):
                    if front:
                        copy_turned(it + 1)
                    exponents(it, 0)
                    if front:
                        carry(it + 1, 1 - i)
                        copy_wide(it + 1, 1 - i, 0)
                        copy_wide(it + 1, 1 - i, 1)
                    for j in range(NT):
                        act.wait_ge(probs_turned, at(it * NT + j + 1))
                        act.copy(probs_T[j % 2][:, :, :].rearrange("p c q -> p (c q)"), pt_ps[:, 0:2 * P]).then_inc(probs_T_ready, 1)
                        if j + 1 < NT:
                            exponents(it, j + 1)
                        if j == 0 and not is_first(it):
                            root3(it - 1)
                        if front and j < NT - 1:
                            copy_wide(it + 1, 1 - i, 2 * j + 2)
                            copy_wide(it + 1, 1 - i, 2 * j + 3)
                        if j == 1 and not is_first(it):
                            copy_h3(it - 1)
                        if norm and j == 2:
                            root(it + 2)

                act.wait_ge(zeros_ready, at(1))
                for n in range(SLOT_TILES // ZERO_TILES):
                    rows = d["xs"][n * ZERO_TILES * P:(n + 1) * ZERO_TILES * P, :]
                    act.dma_start(rows.rearrange("(p t) f -> p (t f)", p=P), zeros[:, :]).then_inc(zeroed, 16)
                root(0)
                root(1)
                copy_turned(0)
                carry(0, 0)
                for n in range(WIDE):
                    copy_wide(0, 0, n)
                run_steps(act, step)
                root3(ALL_STEPS - 1)
                copy_h3(ALL_STEPS - 1)
                act.wait_ge(zeroed, at(SLOT_TILES // ZERO_TILES * 16))

            @block.gpsimd
            def _(pool):
                pool.memset(zeros[:, :], 0.0).then_inc(zeros_ready, 1)
                pool.wait_ge(consts, at(CONSTS))

                def products(it, i):
                    pool.wait_ge(wide_out, at((it + 1) * WIDE))
                    pool.tensor_tensor(pT[i][:, :, :], qT[i][:, :, :], pT[i][:, :, :], ALU.mult).then_inc(products_ready, 1)

                def step(it, i, r, front, norm):
                    for j in range(NT):
                        pool.wait_ge(exp_done, at(it * NT + j + 1))
                        pool.tensor_tensor(exps[j][:, 0, :], exps[j][:, 0, :], nears[:, :], ALU.mult).then_inc(near_done, 1)
                    if front:
                        products(it + 1, 1 - i)

                products(0, 0)
                run_steps(pool, step)

            @block.vector
            def _(vec):
                for z in (probs[0][:, :], probs[1][:, :], v[0][:, :, :], v[1][:, :, :], phT[:, :, :], kT[0][:, :, :], kT[1][:, :, :]):
                    vec.memset(z, 0.0).then_inc(cleared, 1)
                vec.wait_ge(cleared, at(7))
                vec.wait_ge(consts, at(CONSTS))
                vec.sem_inc(cleared, 1)

                def moments_of(seq, it, i, r):
                    seq.wait()
                    vec.wait_ge(h_in[i], at((r + 1) * 48))
                    layernorm_moments(vec, seq, h[i][:, :, :], stats, moments, ss, NT, var_ready, it + 1)

                def normalize(seq, it, i):
                    layernorm_scale(vec, seq, h[i][:, :, :], moments, ss, NT, rooted, it + 1)
                    seq.wait()
                    seq.done(vec.tensor_tensor(h[i][:, :, :], h[i][:, :, :], mod[i][:, 1:2, :].broadcast_to([P, NT, DIM]), ALU.mult))
                    seq.wait()
                    seq.tell(vec.tensor_tensor(h[i][:, :, :], h[i][:, :, :], mod[i][:, 0:1, :].broadcast_to([P, NT, DIM]), ALU.add), h_ready, it + 1)

                def take_values(seq, it, i):
                    seq.done(vec.tensor_copy(v[i][:, 0, 0:DIM], v[1 - i][:, NT, 0:DIM]))
                    seq.wait()
                    for j in range(NT):
                        vec.wait_ge(v_done, at(it * NT + j + 1))
                        seq.tell(vec.tensor_tensor(v[i][:, 1 + j, :], v_ps[j % 2][:, :], row_bias[:, :], ALU.add), v_used, it * NT + j + 1)

                def moments_of_x(seq, it, i):
                    seq.wait()
                    layernorm_moments(vec, seq, x[i][:, :, :], stats, moments3, ss3, NT, var3_ready, it + 1)

                def normalize_x(seq, it, i):
                    vec.wait_ge(h3_out, at(it * 16))
                    layernorm_scale(vec, seq, x[i][:, :, :], moments3, ss3, NT, rooted3, it + 1, out=h3[:, :, :])
                    seq.wait()
                    seq.done(vec.tensor_tensor(h3[:, :, :], h3[:, :, :], mod3[i][:, 1:2, :].broadcast_to([P, NT, DIM]), ALU.mult))
                    seq.wait()
                    seq.tell(vec.tensor_tensor(h3[:, :, :], h3[:, :, :], mod3[i][:, 0:1, :].broadcast_to([P, NT, DIM]), ALU.add), h3_ready, it + 1)

                def take_logits(seq, it):
                    vec.wait_ge(routed, at(it + 1))
                    seq.tell(vec.tensor_tensor(logits[:, bass.ds(it * NT, NT), :], v_ps[1][:, 0:NT * ALL_EXPERTS].rearrange("p (n e) -> p n e", n=NT),
                                               gate_b[:, :].unsqueeze(1).broadcast_to([P, NT, ALL_EXPERTS]), ALU.add), logits_used, it + 1)

                def step(it, n, r, front, norm):
                    start = (2 if front else 1) * NORM_STEPS + CARRY_STEPS
                    seq = Chain(vec, order, start if is_first(it) else it * VEC_STEPS + start - SCALE_STEPS)
                    seq.wait()

                    def choose(j):
                        i = j
                        mask = band[:, bass.ds(it, 1), :].rearrange("p a c -> p (a c)") if j == 0 else band[:, 1, :]
                        vec.wait_ge(scored, at(it * NT + j + 1))
                        seq.done(vec.scalar_tensor_tensor(scores[i][:, :], sc_ps[j % 2][:, 0:SPAN], DIM ** -0.5, mask, ALU.mult, ALU.add))
                        seq.tell(vec.tensor_scalar(one[i][:, PH:PH + 1], sc_ps[j % 2][:, SPAN:SPAN + 1], DIM ** -0.5, None, ALU.mult), sc_used, it * NT + j + 1)
                        seq.wait()
                        vec.sem_inc(passed, 1)
                        seq.done(vec.max(top[i][:, 0, :], scores[i][:, :]))
                        seq.wait()
                        vec.sem_inc(passed, 1)
                        seq.done(vec.match_replace(rest[i][:, 0, :], top[i][:, 0, :], scores[i][:, :], TAKEN))
                        seq.wait()
                        vec.sem_inc(passed, 1)
                        seq.done(vec.max(top[i][:, 1, :], rest[i][:, 0, :]))
                        seq.done(vec.tensor_tensor(one[i][:, MAX:MAX + 1], one[i][:, PH:PH + 1], top[i][:, 0, 0:1], ALU.max))
                        seq.wait()
                        seq.done(vec.tensor_scalar(one[i][:, MAX:MAX + 1], one[i][:, MAX:MAX + 1], -1.0, None, ALU.mult))
                        seq.wait()
                        vec.sem_inc(passed, 1)
                        seq.tell(vec.match_replace(rest[i][:, 1, :], top[i][:, 1, :], rest[i][:, 0, :], TAKEN), rest_ready, it * NT + j + 1)

                    def weigh(j):
                        i = j % 2
                        vec.wait_ge(near_done, at(it * NT + j + 1))
                        vec.wait_ge(probs_turned, at(it * NT + j - 1 if j >= 2 else it * NT))
                        seq.tell(vec.scalar_tensor_tensor(probs[i][:, 2 * P - SPAN:], exps[j][:, 0, :], 1.0, exps[j][:, 1, :], ALU.mult, ALU.subtract,
                                                            accum_out=one[j][:, SUM:SUM + 1]), probs_ready, it * NT + j + 1)
                        seq.wait()
                        seq.done(vec.tensor_tensor(one[j][:, INV:INV + 1], one[j][:, SUM:SUM + 1], one[j][:, WPH:WPH + 1], ALU.add))
                        seq.wait()
                        seq.done(vec.reciprocal(one[j][:, INV:INV + 1], one[j][:, INV:INV + 1]))
                        if j == 0:
                            seq.wait()
                            seq.done(vec.tensor_tensor(one[j][:, INV:INV + 1], one[j][:, INV:INV + 1], keep[:, bass.ds(it, 1)], ALU.mult))

                    def finish(j):
                        i = j % 2
                        vec.wait_ge(o_done, at(it * NT + j + 1))
                        seq.tell(vec.scalar_tensor_tensor(out[i][:, :], v[n][:, 1 + j, DIM:2 * DIM], one[j][:, WPH:WPH + 1], o_ps[:, 0:DIM],
                                                            ALU.mult, ALU.add), o_used, it * NT + j + 1)
                        seq.wait()
                        seq.done(vec.scalar_tensor_tensor(out[i][:, :], out[i][:, :], one[j][:, INV:INV + 1], ga[n][:, :], ALU.mult, ALU.mult))
                        seq.wait()
                        seq.tell(vec.tensor_tensor(x[n][:, j, :], x[n][:, j, :], out[i][:, :], ALU.add), x_ready, it * NT + j + 1)

                    choose(0)
                    choose(1)
                    vec.wait_ge(x_in[n], at((r + 1) * 64))
                    before = not is_first(it)
                    for j in range(NT):
                        weigh(j)
                        if j + 2 < NT:
                            choose(j + 2)
                        if norm and j == 2:
                            moments_of(seq, it + 2, n, r + 1)
                        if j > 0:
                            finish(j - 1)
                        if before and j == 0:
                            normalize_x(seq, it - 1, 1 - n)
                        if before and j == 3:
                            take_logits(seq, it - 1)
                    if norm:
                        normalize(seq, it + 2, n)
                    if front:
                        take_values(seq, it + 1, 1 - n)
                    finish(NT - 1)
                    moments_of_x(seq, it, n)
                    if norm and before:
                        assert seq.steps == VEC_STEPS, seq.steps

                seq = Chain(vec, order)
                moments_of(seq, 0, 0, 0)
                normalize(seq, 0, 0)
                assert seq.steps == NORM_STEPS, seq.steps
                moments_of(seq, 1, 1, 0)
                normalize(seq, 1, 1)
                take_values(seq, 0, 0)
                run_steps(vec, step)
                last = ALL_STEPS - 1
                seq = Chain(vec, order, ALL_STEPS * VEC_STEPS - SCALE_STEPS)
                vec.wait_ge(var3_ready, at(ALL_STEPS))
                normalize_x(seq, last, 1)
                take_logits(seq, last)
                vec.wait_ge(logits_used, at(ALL_STEPS))


def slot_rows(dram, tile):
    return dram.rearrange("(n p) f -> n p f", p=P)[bass.ds(tile, 1)].rearrange("a p f -> (a p) f")


def build_slots(nc, d, route):
    E = FFN_EXPERTS
    logits, shares, pass_w, slots, tile_expert = (route[n] for n in ("logits", "shares", "pass_w", "slots", "tile_expert"))
    with ExitStack() as ctx:
        sb = lambda name, shape, dt=F32: ctx.enter_context(nc.sbuf_tensor("sl_" + name, shape, dt))
        ps = lambda name, shape: ctx.enter_context(nc.psum_tensor("sl_" + name, shape, F32))
        sem = Semaphores(nc, ctx, "sl_")
        before = sb("before", [P, P])
        ones = sb("ones", [P, P])
        tile_starts = sb("tile_starts", [P, TILES])
        slot_tiles = sb("slot_tiles", [P, SLOT_TILES])
        numbers = sb("numbers", [P, ALL_EXPERTS])
        best = sb("best", [P, TILES, 8])
        best_at = sb("best_at", [P, TILES, 8], INT)
        best_n = sb("best_n", [P, TILES, 8])
        pair = sb("pair", [P, PICKS, TILES])
        gap = sb("gap", [P, 2, TILES])
        hot = sb("hot", [P, PICKS, TILES, ALL_EXPERTS])
        weighted = sb("weighted", [P, PICKS, TILES, ALL_EXPERTS])
        picked = hot[:, :, :, 0:E]
        either = sb("either", [P, TILES, E])
        running = [sb(f"running{i}", [P, TILES, E]) for i in range(2)]
        wider = sb("wider", [P, E, TILES])
        tiles_of = [sb(f"tiles_of{i}", [P, E]) for i in range(3)]
        place = sb("place", [P, TILES, E])
        mine = sb("mine", [P, TILES, E])
        slot_f = sb("slot_f", [P, PICKS, TILES])
        has = sb("has", [P, PICKS, TILES])
        passed_ends = sb("passed_ends", [P, SLOT_TILES, E - 1])
        expert_f = sb("expert_f", [P, SLOT_TILES])
        rank_ps = ps("rank_ps", [P, TILES, E])
        total_ps = ps("total_ps", [P, TILES, E])
        consts, order, either_ready, counted, gap_ready, gap_exp, found = map(sem, (
            "consts", "order", "either_ready", "counted", "gap_ready", "gap_exp", "found"))
        sem.start()
        with nc.Block() as block:
            @block.sync
            def _(sync):
                sync.dma_start(before[:, :], d["before"]).then_inc(consts, 16)
                sync.dma_start(ones[:, :], d["ones_square"]).then_inc(consts, 16)
                sync.dma_start(tile_starts[:, :], d["tile_starts"]).then_inc(consts, 16)
                sync.dma_start(slot_tiles[:, :], d["slot_tiles"]).then_inc(consts, 16)
                sync.dma_start(numbers[:, :], d["numbers"]).then_inc(consts, 16)

            @block.scalar
            def _(act):
                act.wait_ge(gap_ready, at(1))
                act.activation(gap[:, 1, :], gap[:, 0, :], ACT.Exp).then_inc(gap_exp, 1)

            @block.tensor
            def _(pe):
                pe.wait_ge(consts, at(80))
                pe.wait_ge(either_ready, at(1))
                pe.matmul(rank_ps[:, :, :], before[:, :], either[:, :, :], start=True, stop=True)
                pe.matmul(total_ps[:, :, :], ones[:, :], either[:, :, :], start=True, stop=True).then_inc(counted, 1)

            @block.vector
            def _(vec):
                for n in range(TILES):
                    vec.max(best[:, n, :], logits[:, n, :]).then_inc(found, 1)
                vec.wait_ge(found, at(TILES))
                for n in range(TILES):
                    vec.max_index(best_at[:, n, :], best[:, n, :], logits[:, n, :]).then_inc(found, 1)
                vec.wait_ge(found, at(2 * TILES))
                seq = Chain(vec, order)
                vec.wait_ge(consts, at(80))
                seq.tell(vec.tensor_tensor(gap[:, 0, :], best[:, :, 1], best[:, :, 0], ALU.subtract), gap_ready, 1)
                seq.done(vec.tensor_copy(best_n[:, :, :], best_at[:, :, :]))
                seq.wait()
                for n in range(PICKS):
                    seq.done(vec.tensor_tensor(hot[:, n, :, :], numbers[:, :].unsqueeze(1).broadcast_to([P, TILES, ALL_EXPERTS]),
                                               spread(best_n[:, :, n], ALL_EXPERTS), ALU.is_equal))
                vec.wait_ge(gap_exp, at(1))
                seq.done(vec.tensor_scalar(pair[:, 0, :], gap[:, 1, :], 1.0, None, ALU.add))
                seq.wait()
                seq.done(vec.reciprocal(pair[:, 0, :], pair[:, 0, :]))
                seq.wait()
                seq.done(vec.tensor_tensor(pair[:, 1, :], pair[:, 0, :], gap[:, 1, :], ALU.mult))
                seq.wait()
                for n in range(PICKS):
                    seq.done(vec.tensor_tensor(weighted[:, n, :, :], hot[:, n, :, :], spread(pair[:, n, :], ALL_EXPERTS), ALU.mult))
                seq.wait()
                for n in range(PICKS):
                    seq.done(vec.tensor_reduce(shares[:, n, :], weighted[:, n, :, 0:E], AX.X, ALU.add))
                seq.wait()
                seq.done(vec.tensor_tensor(weighted[:, 0, :, :], weighted[:, 0, :, :], weighted[:, 1, :, :], ALU.add))
                seq.wait()
                seq.done(vec.tensor_reduce(pass_w[:, :], weighted[:, 0, :, E:], AX.X, ALU.add))
                seq.tell(vec.tensor_tensor(either[:, :, :], picked[:, 0, :, :], picked[:, 1, :, :], ALU.add), either_ready, 1)
                vec.wait_ge(counted, at(1))
                seq.done(vec.tensor_copy(running[0][:, :, :], total_ps[:, :, :]))
                reach, n = 1, 0
                while reach < TILES:
                    seq.wait()
                    a, b = running[n % 2], running[(n + 1) % 2]
                    seq.done(vec.tensor_copy(b[:, 0:reach, :], a[:, 0:reach, :]))
                    seq.done(vec.tensor_tensor(b[:, reach:, :], a[:, reach:, :], a[:, 0:TILES - reach, :], ALU.add))
                    reach, n = reach * 2, n + 1
                run = running[n % 2]
                seq.wait()
                seq.done(vec.tensor_tensor(wider[:, :, :], spread(run[:, TILES - 1, :], TILES), tile_starts[:, :].unsqueeze(1).broadcast_to([P, E, TILES]), ALU.is_gt))
                seq.wait()
                seq.done(vec.tensor_reduce(tiles_of[0][:, :], wider[:, :, :], AX.X, ALU.add))
                reach, m = 1, 0
                while reach < E:
                    seq.wait()
                    a, b = tiles_of[m % 2], tiles_of[(m + 1) % 2]
                    if m == 0:
                        seq.done(vec.tensor_copy(tiles_of[2][:, :], a[:, :]))
                    seq.done(vec.tensor_copy(b[:, 0:reach], a[:, 0:reach]))
                    seq.done(vec.tensor_tensor(b[:, reach:], a[:, reach:], a[:, 0:E - reach], ALU.add))
                    reach, m = reach * 2, m + 1
                ends = tiles_of[m % 2]
                first = tiles_of[2]
                seq.wait()
                seq.done(vec.tensor_tensor(first[:, :], ends[:, :], first[:, :], ALU.subtract))
                seq.wait()
                seq.done(vec.tensor_scalar(first[:, :], first[:, :], float(P), None, ALU.mult))
                seq.done(vec.tensor_tensor(place[:, :, :], run[:, :, :], total_ps[:, :, :], ALU.subtract))
                seq.wait()
                seq.done(vec.tensor_tensor(place[:, :, :], place[:, :, :], rank_ps[:, :, :], ALU.add))
                seq.wait()
                seq.done(vec.tensor_tensor(place[:, :, :], place[:, :, :], first[:, :].unsqueeze(1).broadcast_to([P, TILES, E]), ALU.add))
                for k in range(PICKS):
                    seq.wait()
                    seq.done(vec.tensor_tensor(mine[:, :, :], place[:, :, :], picked[:, k, :, :], ALU.mult))
                    seq.wait()
                    seq.done(vec.tensor_reduce(slot_f[:, k, :], mine[:, :, :], AX.X, ALU.add))
                    seq.done(vec.tensor_reduce(has[:, k, :], picked[:, k, :, :], AX.X, ALU.add))
                seq.wait()
                seq.done(vec.tensor_scalar(has[:, :, :], has[:, :, :], -NO_SLOT, NO_SLOT, ALU.mult, ALU.add))
                seq.wait()
                seq.done(vec.tensor_tensor(slot_f[:, :, :], slot_f[:, :, :], has[:, :, :], ALU.add))
                seq.wait()
                seq.done(vec.tensor_copy(slots[:, :, :], slot_f[:, :, :]))
                seq.done(vec.tensor_tensor(passed_ends[:, :, :], spread(slot_tiles[:, :], E - 1), ends[:, 0:E - 1].unsqueeze(1).broadcast_to([P, SLOT_TILES, E - 1]), ALU.is_ge))
                seq.wait()
                seq.done(vec.tensor_reduce(expert_f[:, :], passed_ends[:, :, :], AX.X, ALU.add))
                seq.wait()
                seq.done(vec.tensor_copy(tile_expert[:, :], expert_f[0:1, :]))
                seq.wait()


def build_dispatch(nc, d, route):
    slots = route["slots"]
    with ExitStack() as ctx:
        sb = lambda name, shape, dt=F32: ctx.enter_context(nc.sbuf_tensor("dp_" + name, shape, dt))
        sem = Semaphores(nc, ctx, "dp_")
        h = [sb(f"h{i}", [P, NT, DIM]) for i in range(2)]
        to = [[sb(f"to{i}_{n}", [P, 1], INT) for n in range(NT * PICKS)] for i in range(2)]
        h_in = [sem(f"h_in{i}") for i in range(2)]
        sent = [sem.from_zero(f"sent{i}") for i in range(2)]
        gone = [sem(f"gone{i}") for i in range(2)]
        to_ready, passed, weights_in = sem("to_ready"), sem("passed"), sem("weights_in")
        w1, w2 = route["w1"], route["w2"]
        ROUNDS = ALL_STEPS // 2
        sem.start()
        with nc.Block() as block:
            @block.sync
            def _(sync):
                with sync.Fori(0, ROUNDS) as r:
                    for i in range(2):
                        sync.wait_ge(gone[i], at(r))
                        sync.dma_start(h[i][:, :, :], step_rows(d["h3"], r * 2 + i)).then_inc(h_in[i], 16)

            @block.scalar
            def _(act):
                for e in range(FFN_EXPERTS):
                    act.dma_start(w1[:, e, :].rearrange("p (k f) -> p k f", k=HALVES), d["ffn1_w1T"][e].rearrange("(k p) f -> p k f", p=P)).then_inc(weights_in, 16)
                    act.dma_start(w2[:, e, :].rearrange("p (c f) -> p c f", c=FC), d["ffn1_w2T"][e].rearrange("(c p) f -> p c f", p=P)).then_inc(weights_in, 16)
                act.wait_ge(weights_in, at(16 * 2 * FFN_EXPERTS))

            @block.vector
            def _(vec):
                with vec.Fori(0, ROUNDS) as r:
                    for i in range(2):
                        vec.wait_ge(gone[i], at(r))
                        for k in range(PICKS):
                            for j in range(NT):
                                vec.tensor_copy(to[i][k * NT + j][:, :], slots[:, k, bass.ds((r * 2 + i) * NT + j, 1)]).then_inc(to_ready, 1)

            @block.gpsimd
            def _(pool):
                with pool.Fori(0, ROUNDS) as r:
                    for i in range(2):
                        pool.wait_ge(h_in[i], at((r + 1) * 16))
                        pool.wait_ge(to_ready, at((r * 2 + i + 1) * (NT * PICKS)))
                        pool.sem_inc(passed, 1)
                        for k in range(PICKS):
                            for j in range(NT):
                                pool.indirect_dma_start(d["xs"], bass.IndirectOffsetOnAxis(ap=to[i][k * NT + j][:, :], axis=0), h[i][:, j, :], None,
                                                        bounds_check=SLOTS - 1, oob_is_err=False).then_inc(sent[i], 16)
                    for i in range(2):
                        pool.wait_ge(sent[i], (r + 1) * (NT * PICKS * 16))
                        pool.sem_inc(gone[i], 1)


def build_slot_experts(nc, d, route):
    tile_expert = route["tile_expert"]
    N = 2
    with ExitStack() as ctx:
        sb = lambda name, shape, dt=F32: ctx.enter_context(nc.sbuf_tensor("se_" + name, shape, dt))
        ps = lambda name, shape: ctx.enter_context(nc.psum_tensor("se_" + name, shape, F32))
        sem = Semaphores(nc, ctx, "se_")
        ident = sb("ident", [P, P])
        w1, w2 = route["w1"], route["w2"]
        xs = [[sb(f"xs{i}_{n}", [P, DIM]) for n in range(N)] for i in range(2)]
        xT = [sb(f"xT{n}", [P, HALVES, P]) for n in range(N)]
        act1 = [sb(f"act1_{n}", [P, DFF]) for n in range(N)]
        aT = [sb(f"aT{n}", [P, FC, P]) for n in range(N)]
        y = [[sb(f"y{i}_{n}", [P, DIM]) for n in range(N)] for i in range(2)]
        xt_ps = [ps(f"xt_ps{n}", [P, HALVES * P]) for n in range(N)]
        up_ps = [ps(f"up_ps{n}", [P, DFF]) for n in range(N)]
        at_ps = [ps(f"at_ps{n}", [P, FC * P]) for n in range(N)]
        y_ps = [ps(f"y_ps{n}", [P, DIM]) for n in range(N)]
        consts = sem("consts")
        xs_in = [sem(f"xs_in{i}") for i in range(2)]
        y_out = [sem.from_zero(f"y_out{i}") for i in range(2)]
        y_gone = [sem(f"y_gone{i}") for i in range(2)]
        x_turned, xT_ready, up_done, act_ready, a_turned, aT_ready, down_done, y_ready = map(sem, (
            "x_turned", "xT_ready", "up_done", "act_ready", "a_turned", "aT_ready", "down_done", "y_ready"))
        both = range(2)
        ROUNDS = SLOT_TILES // (2 * N)
        sem.start()
        with nc.Block() as block:
            @block.sync
            def _(sync):
                sync.dma_start(ident[:, :], d["ident"]).then_inc(consts, 16)
                with sync.Fori(0, ROUNDS) as r:
                    for i in range(2):
                        for n in range(N):
                            sync.wait_ge(x_turned, at((r * 2 + i) * N - N + n + 1 if i > 0 else r * (2 * N)))
                            sync.dma_start(xs[i][n][:, :], slot_rows(d["xs"], (r * 2 + i) * N + n)).then_inc(xs_in[i], 16)

            @block.tensor
            def _(pe):
                pe.wait_ge(consts, at(16))

                def experts_of(turn):
                    return [pe.value_load(tile_expert[0:1, bass.ds(turn + n, 1)], min_val=0, max_val=FFN_EXPERTS - 1) for n in range(N)]

                def turn_rows(turn, i, used):
                    pe.wait_ge(xs_in[i], at(used * (16 * N)))
                    for n in range(N):
                        pe.wait_ge(xT_ready, at(turn))
                        for k in range(HALVES):
                            mm = pe.transpose(xt_ps[n][:, k * P:(k + 1) * P], xs[i][n][:, k * P:(k + 1) * P], ident[:, :])
                        mm.then_inc(x_turned, 1)

                def up(turn):
                    experts = experts_of(turn)
                    for n in range(N):
                        pe.wait_ge(xT_ready, at(turn + n + 1))
                        pe.wait_ge(act_ready, at(turn))
                        for k in range(HALVES):
                            mm = pe.matmul(up_ps[n][:, :], xT[n][:, k, :], w1[:, bass.ds(experts[n], 1), k * DFF:(k + 1) * DFF].rearrange("p a f -> p (a f)"),
                                           start=(k == 0), stop=(k == HALVES - 1))
                        mm.then_inc(up_done, 1)

                def turn_hidden(turn):
                    for n in range(N):
                        pe.wait_ge(act_ready, at(turn + n + 1))
                        pe.wait_ge(aT_ready, at(turn))
                        for c in range(FC):
                            mm = pe.transpose(at_ps[n][:, c * P:(c + 1) * P], act1[n][:, c * P:(c + 1) * P], ident[:, :])
                        mm.then_inc(a_turned, 1)

                def down(turn):
                    experts = experts_of(turn)
                    for n in range(N):
                        pe.wait_ge(aT_ready, at(turn + n + 1))
                        pe.wait_ge(y_ready, at(turn))
                        for c in range(FC):
                            mm = pe.matmul(y_ps[n][:, :], aT[n][:, c, :], w2[:, bass.ds(experts[n], 1), c * DIM:(c + 1) * DIM].rearrange("p a f -> p (a f)"),
                                           start=(c == 0), stop=(c == FC - 1))
                        mm.then_inc(down_done, 1)

                def round_of(r, last):
                    for i in both:
                        turn, more = (r * 2 + i) * N, not (last and i == 1)
                        turn_hidden(turn)
                        if more:
                            turn_rows(turn + N, 1 - i, r + 1 + i)
                        down(turn)
                        if more:
                            up(turn + N)

                turn_rows(0, 0, 1)
                up(0)
                with pe.Fori(0, ROUNDS - 1) as r:
                    round_of(r, last=False)
                round_of(ROUNDS - 1, last=True)

            @block.scalar
            def _(act):
                with act.Fori(0, ROUNDS) as r:
                    for i in both:
                        turn = (r * 2 + i) * N
                        for n in range(N):
                            act.wait_ge(x_turned, at(turn + n + 1))
                            act.wait_ge(up_done, at(turn))
                            act.copy(xT[n][:, :, :].rearrange("p k t -> p (k t)"), xt_ps[n][:, :]).then_inc(xT_ready, 1)
                        for n in range(N):
                            act.wait_ge(up_done, at(turn + n + 1))
                            act.wait_ge(a_turned, at(turn))
                            act.activation(act1[n][:, :], up_ps[n][:, :], ACT.Silu).then_inc(act_ready, 1)

            @block.vector
            def _(vec):
                with vec.Fori(0, ROUNDS) as r:
                    for i in range(2):
                        turn = (r * 2 + i) * N
                        for n in range(N):
                            vec.wait_ge(a_turned, at(turn + n + 1))
                            vec.wait_ge(down_done, at(turn))
                            vec.tensor_copy(aT[n][:, :, :].rearrange("p c t -> p (c t)"), at_ps[n][:, :]).then_inc(aT_ready, 1)
                        for n in range(N):
                            vec.wait_ge(y_gone[i], at(r))
                            vec.wait_ge(down_done, at(turn + n + 1))
                            vec.tensor_copy(y[i][n][:, :], y_ps[n][:, :]).then_inc(y_ready, 1)

            @block.gpsimd
            def _(pool):
                with pool.Fori(0, ROUNDS) as r:
                    for i in range(2):
                        for n in range(N):
                            pool.wait_ge(y_ready, at((r * 2 + i) * N + n + 1))
                            pool.dma_start(slot_rows(d["ys"], (r * 2 + i) * N + n), y[i][n][:, :]).then_inc(y_out[i], 16)
                        pool.wait_ge(y_out[i], (r + 1) * (16 * N))
                        pool.sem_inc(y_gone[i], 1)


def build_combine(nc, d, route):
    slots, shares, pass_w = route["slots"], route["shares"], route["pass_w"]
    VEC_STEPS, PREPARE_STEPS = 30, 2
    with ExitStack() as ctx:
        sb = lambda name, shape, dt=F32: ctx.enter_context(nc.sbuf_tensor("cb_" + name, shape, dt))
        sem = Semaphores(nc, ctx, "cb_")
        both = range(2)
        gb = [sb(f"gb{i}", [P, DIM]) for i in both]
        x = [sb(f"x{i}", [P, NT, DIM]) for i in both]
        h = [sb(f"h{i}", [P, NT, DIM]) for i in both]
        y = [sb(f"y{i}", [P, PICKS * NT, DIM]) for i in both]
        share = [sb(f"share{i}", [P, PICKS + 1, NT]) for i in both]
        to = [[sb(f"to{i}_{n}", [P, 1], INT) for n in range(NT * PICKS)] for i in both]
        cleared, order, to_ready, passed = map(sem, ("cleared", "order", "to_ready", "passed"))
        rows_in = [sem(f"rows_in{i}") for i in both]
        fetched = [sem.from_zero(f"fetched{i}") for i in both]
        x_ready = [sem(f"x_ready{i}") for i in both]
        x_out = [sem(f"x_out{i}") for i in both]
        ROUNDS = ALL_STEPS // 2
        sem.start()
        with nc.Block() as block:
            @block.sync
            def _(sync):
                with sync.Fori(0, ROUNDS) as r:
                    for i in both:
                        sync.wait_ge(x_out[i], at(r * 16))
                        sync.dma_start(x[i][:, :, :], step_rows(d["x3"], r * 2 + i)).then_inc(rows_in[i], 16)
                        sync.dma_start(h[i][:, :, :], step_rows(d["h3"], r * 2 + i)).then_inc(rows_in[i], 16)
                        sync.dma_start(gb[i][:, :], step_mod(d, r * 2 + i, MOD_GB)).then_inc(rows_in[i], 16)
                    for i in both:
                        sync.wait_ge(x_ready[i], at(r + 1))
                        sync.dma_start(step_rows(d["out"], r * 2 + i), x[i][:, :, :]).then_inc(x_out[i], 16)
                for i in both:
                    sync.wait_ge(x_out[i], at(ROUNDS * 16))

            @block.gpsimd
            def _(pool):
                pool.wait_ge(cleared, at(2))
                with pool.Fori(0, ROUNDS) as r:
                    for i in both:
                        pool.wait_ge(to_ready, at((r * 2 + i + 1) * (NT * PICKS)))
                        pool.sem_inc(passed, 1)
                        for k in range(PICKS):
                            for j in range(NT):
                                pool.indirect_dma_start(y[i][:, k * NT + j, :], None, d["ys"], bass.IndirectOffsetOnAxis(ap=to[i][k * NT + j][:, :], axis=0),
                                                        bounds_check=SLOTS - 1, oob_is_err=False).then_inc(fetched[i], 16)

            @block.vector
            def _(vec):
                for i in both:
                    vec.memset(y[i][:, :, :], 0.0).then_inc(cleared, 1)

                def prepare(seq, step, i, done):
                    vec.wait_ge(x_ready[i], at(done))
                    tiles = bass.ds(step * NT, NT)
                    for k in range(PICKS):
                        for j in range(NT):
                            vec.tensor_copy(to[i][k * NT + j][:, :], slots[:, k, bass.ds(step * NT + j, 1)]).then_inc(to_ready, 1)
                    seq.done(vec.tensor_copy(share[i][:, 0:PICKS, :], shares[:, :, tiles]))
                    seq.done(vec.tensor_copy(share[i][:, PICKS, :], pass_w[:, tiles]))

                def combine(seq, r, i):
                    seq.wait()
                    vec.wait_ge(rows_in[i], at((r + 1) * 48))
                    for j in range(NT):
                        seq.done(vec.tensor_scalar(h[i][:, j, :], h[i][:, j, :], share[i][:, PICKS, j:j + 1], None, ALU.mult))
                    vec.wait_ge(fetched[i], (r + 1) * (NT * PICKS * 16))
                    for k in range(PICKS):
                        seq.wait()
                        for j in range(NT):
                            seq.done(vec.scalar_tensor_tensor(h[i][:, j, :], y[i][:, k * NT + j, :], share[i][:, k, j:j + 1], h[i][:, j, :], ALU.mult, ALU.add))
                    seq.wait()
                    seq.done(vec.tensor_tensor(h[i][:, :, :], h[i][:, :, :], gb[i][:, :].unsqueeze(1).broadcast_to([P, NT, DIM]), ALU.mult))
                    seq.wait()
                    seq.tell(vec.tensor_tensor(x[i][:, :, :], x[i][:, :, :], h[i][:, :, :], ALU.add), x_ready[i], r + 1)

                seq = Chain(vec, order)
                for i in both:
                    prepare(seq, i, i, 0)
                assert seq.steps == 2 * PREPARE_STEPS, seq.steps
                with vec.Fori(0, ROUNDS - 1) as r:
                    seq = Chain(vec, order, r * VEC_STEPS + 2 * PREPARE_STEPS)
                    for i in both:
                        combine(seq, r, i)
                        prepare(seq, r * 2 + 2 + i, i, r + 1)
                    assert seq.steps == VEC_STEPS, seq.steps
                seq = Chain(vec, order, (ROUNDS - 1) * VEC_STEPS + 2 * PREPARE_STEPS)
                for i in both:
                    combine(seq, ROUNDS - 1, i)


def build_mixture(nc, d, logits):
    with ExitStack() as ctx:
        sb = lambda name, shape, dt=F32: ctx.enter_context(nc.sbuf_tensor("mx_" + name, shape, dt))
        route = {
            "logits": logits, "shares": sb("shares", [P, PICKS, TILES]), "pass_w": sb("pass_w", [P, TILES]),
            "slots": sb("slots", [P, PICKS, TILES], INT), "tile_expert": sb("tile_expert", [1, SLOT_TILES], INT),
            "w1": sb("w1", [P, FFN_EXPERTS, HALVES * DFF]), "w2": sb("w2", [P, FFN_EXPERTS, FC * DIM]),
        }
        build_slots(nc, d, route)
        build_dispatch(nc, d, route)
        build_slot_experts(nc, d, route)
        build_combine(nc, d, route)


def build_program(nc, d):
    build_modulation(nc, d)
    with nc.sbuf_tensor("gamma_last", [P, HALVES, CHUNKS], F32) as gamma_last:
        build_delta_chunks(nc, d, gamma_last)
        build_state_scan(nc, d, gamma_last)
    build_delta_outputs(nc, d)
    with ExitStack() as ffn:
        chosen = ffn.enter_context(nc.sbuf_tensor("chosen", [EXPERTS, BATCH, SEQ], F32))
        merged = ffn.enter_context(nc.sbuf_tensor("merged", [P, HALVES, EXPERTS, BATCH], F32))
        expert_out = ffn.enter_context(nc.sbuf_tensor("expert_out", [EXPERTS, BATCH, DIM], F32))
        build_token_choice(nc, d, merged, chosen)
        build_experts(nc, d, merged, expert_out)
        build_scatter(nc, d, chosen, expert_out)
    with nc.sbuf_tensor("logits", [P, TILES, ALL_EXPERTS], F32) as logits:
        build_window_attention(nc, d, logits)
        build_mixture(nc, d, logits)


def constants():
    import numpy as np
    token, key = np.arange(P)[:, None], np.arange(SPAN)[None]
    other = np.arange(P)[None]
    in_window = (key >= token) & (key < token + WINDOW)
    band = np.where(in_window, 0.0, NEG)
    first = np.where(in_window & (key >= WINDOW), 0.0, NEG)
    keep = np.ones((P, ALL_STEPS))
    keep[0, ::STEPS] = 0.0
    same_phrase = (token // PHRASE == other // PHRASE) & (token <= other)
    tables = {
        "ident": np.eye(P),
        "block_mask": np.kron(np.eye(P // HEAD), np.ones((HEAD, HEAD))),
        "chunk_mask": np.arange(P)[:, None] // CHUNK == np.arange(TILE_CHUNKS)[None],
        "ones": np.ones((P, 1)),
        "means": np.where(same_phrase, 1.0 / (other % PHRASE + 1), 0.0),
        "nears": 1.0 + (key == token + WINDOW - 1),
        "band": np.stack(([first] + [band] * (STEPS - 1)) * BATCH, axis=1),
        "keep": keep,
        "before": token < other,
        "ones_square": np.ones((P, P)),
        "tile_starts": np.tile(P * np.arange(TILES), (P, 1)),
        "slot_tiles": np.tile(np.arange(SLOT_TILES), (P, 1)),
        "numbers": np.tile(np.arange(ALL_EXPERTS), (P, 1)),
    }
    return {name: np.ascontiguousarray(table, dtype=np.float32) for name, table in tables.items()}


def kernel(**inputs):
    import numpy as np
    import concourse.bacc as bacc
    from concourse.bass_utils import run_bass_kernel_spmd as run

    a = {name: np.asarray(value) for name, value in inputs.items()}
    L0, L1 = "L0_attn_", "L1_attn_"
    halves = lambda v: v.reshape(HALVES, P)
    layouts = {
        "cT": np.stack([a[f"L{l}_c"].T.reshape(HALVES, P, BATCH).transpose(1, 0, 2).reshape(P, HALVES * BATCH) for l in range(2)]),
        "wmod": np.stack([a["L0_wmod"], a["L1_wmod"]]),
        "x": a["L0_attn_x"].reshape(TOKENS, DIM),
        "w_proj": np.concatenate([a[L0 + n] for n in ("Wq", "Wk", "Wv", "Wgate", "Walpha", "Wbeta")], axis=1),
        "dt_bias": a[L0 + "dt_bias"], "A_log": a[L0 + "A_log"], "rms_w": a[L0 + "rms_w"], "w_out": a[L0 + "Wout"],
        "gate0_wT": a["L0_ffn_gate_w"].T, "gate0_b": a["L0_ffn_gate_b"].reshape(EXPERTS, 1),
        "w1_all": a["L0_ffn_w1"], "w2_all": a["L0_ffn_w2"],
        "w1_bias": a["L0_ffn_w1"][:, DIM, :].reshape(EXPERTS, P, HC).transpose(1, 0, 2),
        "w_cols": np.stack([a[L1 + n + "_w"].T for n in ("q", "k", "pk")]),
        "w_rows": np.stack([a[L1 + n + "_w"].T for n in ("v", "pv")]),
        "col_bias": np.stack([halves(a[L1 + n + "_b"]) for n in ("q", "k", "pk")]).transpose(2, 0, 1),
        "row_bias": np.concatenate([a[L1 + n + "_b"] for n in ("v", "pv")]),
        "gate1_wT": a["L1_ffn_gate_w"].T, "gate1_b": a["L1_ffn_expert_bias"],
        "ffn1_w1T": a["L1_ffn_w1"].transpose(0, 2, 1), "ffn1_w2T": a["L1_ffn_w2"].transpose(0, 2, 1),
    }
    layouts.update(constants())

    nc = bacc.Bacc("TRN2", target_bir_lowering=False, num_devices=1)
    arrays, d = {}, {}
    for name, value in layouts.items():
        value = np.ascontiguousarray(value)
        arrays[f"in_{name}"] = value
        d[name] = nc.dram_tensor(f"in_{name}", value.shape, F32, kind="ExternalInput").ap()
    scratch = {
        "mod": (2, GROUPS, MODS), "mod_steps": (ALL_STEPS, MODS), "qk": (TOKENS, 2 * DIM), "vw": (TOKENS, 2 * DIM), "gate": (TOKENS, DIM),
        "qkd": (TOKENS, DIM), "inverse": (TOKENS, DIM), "vk": (TOKENS, 2 * DIM), "u": (TOKENS, DIM), "qs": (TOKENS, DIM),
        "x1": (TOKENS, DIM), "x2": (TOKENS, DIM), "x3": (TOKENS, DIM), "h3": (TOKENS, DIM),
        "xs": (SLOTS, DIM), "ys": (SLOTS, DIM),
    }
    for name, shape in scratch.items():
        d[name] = nc.dram_tensor(f"scratch_{name}", shape, F32, kind="Internal").ap()
    d["out"] = nc.dram_tensor("out", (TOKENS, DIM), F32, kind="ExternalOutput").ap()
    build_program(nc, d)
    result = run(nc, [arrays], core_ids=[0])
    return result.results[0]["out"].reshape(BATCH, SEQ, DIM)
```
